# Optimizing a Trainium2 kernel written in Bass

```python
import numpy as np
import jax
import jax.numpy as jnp

def _softmax(x, axis=-1):
    return jax.nn.softmax(x, axis=axis)

def _gelu(x):
    return jax.nn.gelu(x, approximate=True)

def _silu(x):
    return jax.nn.silu(x)

def _sigmoid(x):
    return jax.nn.sigmoid(x)

def _layernorm(x, axis=-1, eps=1e-05):
    m = jnp.mean(x, axis=axis, keepdims=True)
    v = jnp.var(x, axis=axis, keepdims=True)
    return (x - m) / jnp.sqrt(v + eps)

def _scatter_add(tgt, idx, src, axis=0):
    return tgt.at[idx].add(src)

def _segment_sum(src, seg, n):
    return jax.ops.segment_sum(src, seg, n)
kernel_name = 'mk_gps_d2_gnn_r32_e4e9b8'

def setup_inputs(seed: int=0):
    np.random.seed(seed)
    _w = jnp.asarray

    def _rec_inputs():
        import jax
        import jax.numpy as jnp
        _gk = jax.random.key(seed)
        x = -0.0002117 + 1 * jax.random.normal(jax.random.fold_in(_gk, 1), (3125, 256), jnp.float32)
        _s = jax.random.randint(jax.random.fold_in(_gk, 2), (25000,), 0, 3125, jnp.int32)
        _d = jax.random.randint(jax.random.fold_in(_gk, 3), (25000,), 0, 3125, jnp.int32)
        _loop = jnp.arange(3125, dtype=jnp.int32)
        src = jnp.concatenate([_s, _d, _loop])
        dst = jnp.concatenate([_d, _s, _loop])
        _o = jnp.argsort(dst, stable=True)
        src = src[_o]
        dst = dst[_o]
        return (x, src, dst)
    x, src, dst = _rec_inputs()

    def _L0_gnn_setup():
        import jax, jax.numpy as jnp
        import numpy as np
        N_NODES = 3125
        N_EDGES = 100000
        D_IN = 256
        D_OUT = 256
        key = jax.random.key(seed)
        k1, k2, k3, k4 = jax.random.split(key, 4)
        x = jax.random.normal(k1, (N_NODES, D_IN), dtype=jnp.float32)
        edge_row = jax.random.randint(k2, (N_EDGES,), 0, N_NODES, dtype=jnp.int32)
        edge_col = jax.random.randint(k3, (N_EDGES,), 0, N_NODES, dtype=jnp.int32)
        bound = float(np.sqrt(6.0 / D_IN))
        weight = jax.random.uniform(k4, (D_IN, D_OUT), dtype=jnp.float32, minval=-bound, maxval=bound)
        bias = jnp.zeros((D_OUT,), dtype=jnp.float32)
        return {'x': x, 'edge_row': edge_row, 'edge_col': edge_col, 'weight': weight, 'bias': bias}
    _L0_gnn_all = _L0_gnn_setup()
    _L0_gnn_in = {k: v for k, v in _L0_gnn_all.items() if k in ('weight', 'bias')}
    del _L0_gnn_all

    def _L0_mix_setup():
        import jax, jax.numpy as jnp
        import numpy as np
        DIM = 256
        HEADS = 4
        HEAD_DIM = DIM // HEADS
        MLP_HIDDEN = DIM * 3
        B, N = (8, 128)
        EPS = 1e-05

        def _layernorm(x, g, b):
            mu = jnp.mean(x, axis=-1, keepdims=True)
            var = jnp.mean(jnp.square(x - mu), axis=-1, keepdims=True)
            return (x - mu) * jax.lax.rsqrt(var + EPS) * g + b
        key = jax.random.key(seed)
        ks = jax.random.split(key, 8)
        s = 0.02
        return {'x': jax.random.normal(ks[0], (B, N, DIM), dtype=jnp.float32), 'w_qkv': jax.random.normal(ks[1], (DIM, 3 * DIM), dtype=jnp.float32) * s, 'b_qkv': jnp.zeros((3 * DIM,), dtype=jnp.float32), 'norm_g': jnp.ones((DIM,), dtype=jnp.float32), 'norm_b': jnp.zeros((DIM,), dtype=jnp.float32), 'w_fc1': jax.random.normal(ks[2], (DIM, MLP_HIDDEN), dtype=jnp.float32) * s, 'b_fc1': jnp.zeros((MLP_HIDDEN,), dtype=jnp.float32), 'w_fc2': jax.random.normal(ks[3], (MLP_HIDDEN, DIM), dtype=jnp.float32) * s, 'b_fc2': jnp.zeros((DIM,), dtype=jnp.float32)}
    _L0_mix_all = _L0_mix_setup()
    _L0_mix_in = {k: v for k, v in _L0_mix_all.items() if k in ('w_qkv', 'b_qkv', 'norm_g', 'norm_b', 'w_fc1', 'b_fc1', 'w_fc2', 'b_fc2')}
    del _L0_mix_all

    def _L0_ffn_setup():
        import jax, jax.numpy as jnp
        import numpy as np
        B, S, H, F, E, K = (8, 128, 256, 512, 16, 2)
        EPS = 1e-05
        key = jax.random.key(seed)
        ks = jax.random.split(key, 9)
        sc = 0.02
        return {'x': jax.random.normal(ks[0], (B, S, H), dtype=jnp.float32), 'gate_w': jax.random.normal(ks[1], (H, E), dtype=jnp.float32) * sc, 'gate_b': jnp.zeros((E,), dtype=jnp.float32), 'w1': jax.random.normal(ks[2], (E, H, F), dtype=jnp.float32) * sc, 'b1': jnp.zeros((E, F), dtype=jnp.float32), 'w2': jax.random.normal(ks[3], (E, F, H), dtype=jnp.float32) * sc, 'b2': jnp.zeros((E, H), dtype=jnp.float32), 'gamma': jnp.ones((H,), dtype=jnp.float32), 'beta': jnp.zeros((H,), dtype=jnp.float32)}
    _L0_ffn_all = _L0_ffn_setup()
    _L0_ffn_in = {k: v for k, v in _L0_ffn_all.items() if k in ('gate_w', 'gate_b', 'w1', 'b1', 'w2', 'b2', 'gamma', 'beta')}
    del _L0_ffn_all

    def _L1_gnn_setup():
        import jax, jax.numpy as jnp
        import numpy as np
        N = 3125
        E = 25000
        EMB = 256
        HID = 256
        EPS = 1e-05

        def _pool_max(h, edge_src, edge_dst):
            pooled = jax.ops.segment_max(h[edge_src], edge_dst, num_segments=N)
            cnt = jax.ops.segment_sum(jnp.ones((edge_dst.shape[0],), h.dtype), edge_dst, num_segments=N)
            return jnp.where((cnt > 0)[:, None], pooled, jnp.zeros((), h.dtype))

        def _layernorm(x, g, b):
            mu = jnp.mean(x, axis=-1, keepdims=True)
            var = jnp.mean(jnp.square(x - mu), axis=-1, keepdims=True)
            return (x - mu) * jax.lax.rsqrt(var + EPS) * g + b
        key = jax.random.key(seed)
        ks = jax.random.split(key, 12)
        s = 0.05
        return {'embeddings': jax.random.normal(ks[0], (N, EMB), jnp.float32), 'edge_src': jax.random.randint(ks[1], (E,), 0, N, jnp.int32), 'edge_dst': jax.random.randint(ks[2], (E,), 0, N, jnp.int32), 'Wp1': jax.random.normal(ks[3], (HID, EMB), jnp.float32) * s, 'bp1': jnp.zeros((HID,), jnp.float32), 'Wm1': jax.random.normal(ks[4], (HID, EMB + HID), jnp.float32) * s, 'bm1': jnp.zeros((HID,), jnp.float32), 'Wm2': jax.random.normal(ks[5], (HID, 2 * HID), jnp.float32) * s, 'bm2': jnp.zeros((HID,), jnp.float32), 'Wm3': jax.random.normal(ks[6], (HID, 2 * HID), jnp.float32) * s, 'bm3': jnp.zeros((HID,), jnp.float32), 'ln2_g': jnp.ones((HID,), jnp.float32), 'ln2_b': jnp.zeros((HID,), jnp.float32), 'ln3_g': jnp.ones((HID,), jnp.float32), 'ln3_b': jnp.zeros((HID,), jnp.float32)}
    _L1_gnn_all = _L1_gnn_setup()
    _L1_gnn_in = {k: v for k, v in _L1_gnn_all.items() if k in ('Wp1', 'bp1', 'Wm1', 'bm1', 'Wm2', 'bm2', 'Wm3', 'bm3', 'ln2_g', 'ln2_b', 'ln3_g', 'ln3_b')}
    del _L1_gnn_all

    def _L1_mix_setup():
        import jax, jax.numpy as jnp
        import numpy as np
        D_MODEL = 256
        NUM_HEADS = 8
        DEPTH = D_MODEL // NUM_HEADS
        B, L = (32, 128)

        def _feature_map(x):
            return jax.nn.elu(x) + 1.0
        key = jax.random.key(seed)
        ks = jax.random.split(key, 9)
        sc = 1.0 / np.sqrt(D_MODEL)
        return {'x': jax.random.normal(ks[0], (B, L, D_MODEL), dtype=jnp.float32), 'wq': jax.random.normal(ks[1], (D_MODEL, D_MODEL), dtype=jnp.float32) * sc, 'bq': jnp.zeros((D_MODEL,), dtype=jnp.float32), 'wk': jax.random.normal(ks[2], (D_MODEL, D_MODEL), dtype=jnp.float32) * sc, 'bk': jnp.zeros((D_MODEL,), dtype=jnp.float32), 'wv': jax.random.normal(ks[3], (D_MODEL, D_MODEL), dtype=jnp.float32) * sc, 'bv': jnp.zeros((D_MODEL,), dtype=jnp.float32), 'wo': jax.random.normal(ks[4], (D_MODEL, D_MODEL), dtype=jnp.float32) * sc, 'bo': jnp.zeros((D_MODEL,), dtype=jnp.float32)}
    _L1_mix_all = _L1_mix_setup()
    _L1_mix_in = {k: v for k, v in _L1_mix_all.items() if k in ('wq', 'bq', 'wk', 'bk', 'wv', 'bv', 'wo', 'bo')}
    del _L1_mix_all

    def _L1_ffn_setup():
        import jax, jax.numpy as jnp
        import numpy as np
        NUM_EXPERTS = 8
        TOP_K = 2
        B, S, D = (8, 256, 256)

        def _moe(tokens, router_w, w1, b1, w2, b2):
            N = tokens.shape[0]
            E = router_w.shape[0]
            logits = tokens.astype(jnp.float32) @ router_w.astype(jnp.float32).T
            probs = jax.nn.softmax(logits, axis=-1)
            rw, re = jax.lax.top_k(probs, TOP_K)
            if TOP_K > 1:
                rw = rw / jnp.maximum(rw.sum(-1, keepdims=True), 1e-12)
            rw = rw.astype(tokens.dtype)
            combine = jnp.zeros((N, E), tokens.dtype).at[jnp.arange(N)[:, None], re].set(rw)
            out = tokens
            for e in range(E):
                h = jax.nn.gelu(tokens @ w1[e] + b1[e], approximate=False)
                y = h @ w2[e] + b2[e]
                out = out + combine[:, e:e + 1] * y
            return out
        key = jax.random.key(seed)
        ks = jax.random.split(key, 4)
        scale = 1.0 / np.sqrt(D).astype(np.float32)
        return {'input_embeddings': jax.random.normal(ks[0], (B, S, D), jnp.float32), 'router_w': jax.random.normal(ks[1], (NUM_EXPERTS, D), jnp.float32) * scale, 'w1': jax.random.normal(ks[2], (NUM_EXPERTS, D, D), jnp.float32) * scale, 'b1': jnp.zeros((NUM_EXPERTS, D), jnp.float32), 'w2': jax.random.normal(ks[3], (NUM_EXPERTS, D, D), jnp.float32) * scale, 'b2': jnp.zeros((NUM_EXPERTS, D), jnp.float32)}
    _L1_ffn_all = _L1_ffn_setup()
    _L1_ffn_in = {k: v for k, v in _L1_ffn_all.items() if k in ('router_w', 'w1', 'b1', 'w2', 'b2')}
    del _L1_ffn_all
    return {'x': x, 'src': src, 'dst': dst, 'L0_gnn_weight': _L0_gnn_in['weight'], 'L0_gnn_bias': _L0_gnn_in['bias'], 'L0_mix_w_qkv': _L0_mix_in['w_qkv'], 'L0_mix_b_qkv': _L0_mix_in['b_qkv'], 'L0_mix_norm_g': _L0_mix_in['norm_g'], 'L0_mix_norm_b': _L0_mix_in['norm_b'], 'L0_mix_w_fc1': _L0_mix_in['w_fc1'], 'L0_mix_b_fc1': _L0_mix_in['b_fc1'], 'L0_mix_w_fc2': _L0_mix_in['w_fc2'], 'L0_mix_b_fc2': _L0_mix_in['b_fc2'], 'L0_ffn_gate_w': _L0_ffn_in['gate_w'], 'L0_ffn_gate_b': _L0_ffn_in['gate_b'], 'L0_ffn_w1': _L0_ffn_in['w1'], 'L0_ffn_b1': _L0_ffn_in['b1'], 'L0_ffn_w2': _L0_ffn_in['w2'], 'L0_ffn_b2': _L0_ffn_in['b2'], 'L0_ffn_gamma': _L0_ffn_in['gamma'], 'L0_ffn_beta': _L0_ffn_in['beta'], 'L1_gnn_Wp1': _L1_gnn_in['Wp1'], 'L1_gnn_bp1': _L1_gnn_in['bp1'], 'L1_gnn_Wm1': _L1_gnn_in['Wm1'], 'L1_gnn_bm1': _L1_gnn_in['bm1'], 'L1_gnn_Wm2': _L1_gnn_in['Wm2'], 'L1_gnn_bm2': _L1_gnn_in['bm2'], 'L1_gnn_Wm3': _L1_gnn_in['Wm3'], 'L1_gnn_bm3': _L1_gnn_in['bm3'], 'L1_gnn_ln2_g': _L1_gnn_in['ln2_g'], 'L1_gnn_ln2_b': _L1_gnn_in['ln2_b'], 'L1_gnn_ln3_g': _L1_gnn_in['ln3_g'], 'L1_gnn_ln3_b': _L1_gnn_in['ln3_b'], 'L1_mix_wq': _L1_mix_in['wq'], 'L1_mix_bq': _L1_mix_in['bq'], 'L1_mix_wk': _L1_mix_in['wk'], 'L1_mix_bk': _L1_mix_in['bk'], 'L1_mix_wv': _L1_mix_in['wv'], 'L1_mix_bv': _L1_mix_in['bv'], 'L1_mix_wo': _L1_mix_in['wo'], 'L1_mix_bo': _L1_mix_in['bo'], 'L1_ffn_router_w': _L1_ffn_in['router_w'], 'L1_ffn_w1': _L1_ffn_in['w1'], 'L1_ffn_b1': _L1_ffn_in['b1'], 'L1_ffn_w2': _L1_ffn_in['w2'], 'L1_ffn_b2': _L1_ffn_in['b2']}

def reference(x, src, dst, L0_gnn_weight, L0_gnn_bias, L0_mix_w_qkv, L0_mix_b_qkv, L0_mix_norm_g, L0_mix_norm_b, L0_mix_w_fc1, L0_mix_b_fc1, L0_mix_w_fc2, L0_mix_b_fc2, L0_ffn_gate_w, L0_ffn_gate_b, L0_ffn_w1, L0_ffn_b1, L0_ffn_w2, L0_ffn_b2, L0_ffn_gamma, L0_ffn_beta, L1_gnn_Wp1, L1_gnn_bp1, L1_gnn_Wm1, L1_gnn_bm1, L1_gnn_Wm2, L1_gnn_bm2, L1_gnn_Wm3, L1_gnn_bm3, L1_gnn_ln2_g, L1_gnn_ln2_b, L1_gnn_ln3_g, L1_gnn_ln3_b, L1_mix_wq, L1_mix_bq, L1_mix_wk, L1_mix_bk, L1_mix_wv, L1_mix_bv, L1_mix_wo, L1_mix_bo, L1_ffn_router_w, L1_ffn_w1, L1_ffn_b1, L1_ffn_w2, L1_ffn_b2):
    import jax
    import jax.numpy as jnp

    def _L0_gnn_ref(x, edge_row, edge_col, weight, bias):
        import jax, jax.numpy as jnp
        import numpy as np
        N_NODES = 3125
        N_EDGES = 100000
        D_IN = 256
        D_OUT = 256
        support = x @ weight
        gathered = jnp.take(support, edge_col, axis=0)
        out = jax.ops.segment_sum(gathered, edge_row, num_segments=N_NODES)
        return out + bias

    def _L0_mix_ref(x, w_qkv, b_qkv, norm_g, norm_b, w_fc1, b_fc1, w_fc2, b_fc2):
        import jax, jax.numpy as jnp
        import numpy as np
        DIM = 256
        HEADS = 4
        HEAD_DIM = DIM // HEADS
        MLP_HIDDEN = DIM * 3
        B, N = (8, 128)
        EPS = 1e-05

        def _layernorm(x, g, b):
            mu = jnp.mean(x, axis=-1, keepdims=True)
            var = jnp.mean(jnp.square(x - mu), axis=-1, keepdims=True)
            return (x - mu) * jax.lax.rsqrt(var + EPS) * g + b
        Bx, Nx, C = x.shape
        scale = HEAD_DIM ** (-0.5)
        qkv = (x @ w_qkv + b_qkv).reshape(Bx, Nx, 3, HEADS, HEAD_DIM)
        qkv = jnp.transpose(qkv, (2, 0, 3, 1, 4))
        q, k, v = (qkv[0], qkv[1], qkv[2])
        k = k * scale
        attn = jnp.einsum('bhnd,bhne->bhde', k, v)
        attn = jax.nn.softmax(attn, axis=-1)
        xf = jnp.einsum('bhde,bhne->bhnd', attn, q)
        xf = jnp.transpose(xf, (0, 2, 1, 3)).reshape(Bx, Nx, C)
        x = x + xf
        h = _layernorm(x, norm_g, norm_b)
        h = jax.nn.gelu(h @ w_fc1 + b_fc1, approximate=False) @ w_fc2 + b_fc2
        return x + h

    def _L0_ffn_ref(x, gate_w, gate_b, w1, b1, w2, b2, gamma, beta):
        import jax, jax.numpy as jnp
        import numpy as np
        B, S, H, F, E, K = (8, 128, 256, 512, 16, 2)
        EPS = 1e-05
        gate_logits = x @ gate_w + gate_b
        topk_vals, topk_idx = jax.lax.top_k(gate_logits, K)
        topk_w = jax.nn.softmax(topk_vals, axis=-1)
        h = jax.nn.relu(jnp.einsum('bsh,ehf->bsef', x, w1) + b1)
        expert_out = jnp.einsum('bsef,efh->bseh', h, w2) + b2
        sel = jnp.take_along_axis(expert_out, topk_idx[:, :, :, None], axis=2)
        moe = jnp.sum(topk_w[..., None] * sel, axis=2)
        y = x + moe
        mu = jnp.mean(y, axis=-1, keepdims=True)
        var = jnp.var(y, axis=-1, keepdims=True)
        return (y - mu) / jnp.sqrt(var + EPS) * gamma + beta

    def _L1_gnn_ref(embeddings, edge_src, edge_dst, Wp1, bp1, Wm1, bm1, Wm2, bm2, Wm3, bm3, ln2_g, ln2_b, ln3_g, ln3_b):
        import jax, jax.numpy as jnp
        import numpy as np
        N = 3125
        E = 25000
        EMB = 256
        HID = 256
        EPS = 1e-05

        def _pool_max(h, edge_src, edge_dst):
            pooled = jax.ops.segment_max(h[edge_src], edge_dst, num_segments=N)
            cnt = jax.ops.segment_sum(jnp.ones((edge_dst.shape[0],), h.dtype), edge_dst, num_segments=N)
            return jnp.where((cnt > 0)[:, None], pooled, jnp.zeros((), h.dtype))

        def _layernorm(x, g, b):
            mu = jnp.mean(x, axis=-1, keepdims=True)
            var = jnp.mean(jnp.square(x - mu), axis=-1, keepdims=True)
            return (x - mu) * jax.lax.rsqrt(var + EPS) * g + b
        h1 = jax.nn.relu(embeddings @ Wp1.T + bp1)
        p1 = _pool_max(h1, edge_src, edge_dst)
        x = jax.nn.relu(jnp.concatenate([embeddings, p1], axis=1) @ Wm1.T + bm1)
        p2 = _pool_max(x, edge_src, edge_dst)
        y2 = jax.nn.relu(jnp.concatenate([x, p2], axis=1) @ Wm2.T + bm2)
        x = _layernorm(y2 + x, ln2_g, ln2_b)
        p3 = _pool_max(x, edge_src, edge_dst)
        y3 = jax.nn.relu(jnp.concatenate([x, p3], axis=1) @ Wm3.T + bm3)
        x = _layernorm(y3 + x, ln3_g, ln3_b)
        return x

    def _L1_mix_ref(x, wq, bq, wk, bk, wv, bv, wo, bo):
        import jax, jax.numpy as jnp
        import numpy as np
        D_MODEL = 256
        NUM_HEADS = 8
        DEPTH = D_MODEL // NUM_HEADS
        B, L = (32, 128)

        def _feature_map(x):
            return jax.nn.elu(x) + 1.0
        b, l, _ = x.shape
        q = (x @ wq + bq).reshape(b, l, NUM_HEADS, DEPTH)
        k = (x @ wk + bk).reshape(b, l, NUM_HEADS, DEPTH)
        v = (x @ wv + bv).reshape(b, l, NUM_HEADS, DEPTH)
        q = _feature_map(q)
        k = _feature_map(k)
        kv = jnp.einsum('blhd,blhe->bhde', k, v)
        k_sum = jnp.sum(k, axis=1)
        qkv = jnp.einsum('blhd,bhde->blhe', q, kv)
        normalizer = jnp.einsum('blhd,bhd->blh', q, k_sum) + 1e-06
        out = qkv / normalizer[..., None]
        out = out.reshape(b, l, D_MODEL)
        return out @ wo + bo

    def _L1_ffn_ref(input_embeddings, router_w, w1, b1, w2, b2):
        import jax, jax.numpy as jnp
        import numpy as np
        NUM_EXPERTS = 8
        TOP_K = 2
        B, S, D = (8, 256, 256)

        def _moe(tokens, router_w, w1, b1, w2, b2):
            N = tokens.shape[0]
            E = router_w.shape[0]
            logits = tokens.astype(jnp.float32) @ router_w.astype(jnp.float32).T
            probs = jax.nn.softmax(logits, axis=-1)
            rw, re = jax.lax.top_k(probs, TOP_K)
            if TOP_K > 1:
                rw = rw / jnp.maximum(rw.sum(-1, keepdims=True), 1e-12)
            rw = rw.astype(tokens.dtype)
            combine = jnp.zeros((N, E), tokens.dtype).at[jnp.arange(N)[:, None], re].set(rw)
            out = tokens
            for e in range(E):
                h = jax.nn.gelu(tokens @ w1[e] + b1[e], approximate=False)
                y = h @ w2[e] + b2[e]
                out = out + combine[:, e:e + 1] * y
            return out
        b, s, d = input_embeddings.shape
        tokens = input_embeddings.reshape(b * s, d)
        return _moe(tokens, router_w, w1, b1, w2, b2).reshape(b, s, d)
    xn = _layernorm(x, axis=-1)
    x = x + _L0_gnn_ref(xn, src, dst, L0_gnn_weight, L0_gnn_bias) + _L0_mix_ref(xn[None], L0_mix_w_qkv, L0_mix_b_qkv, L0_mix_norm_g, L0_mix_norm_b, L0_mix_w_fc1, L0_mix_b_fc1, L0_mix_w_fc2, L0_mix_b_fc2)[0]
    x = x + _L0_ffn_ref(_layernorm(x, axis=-1)[None], L0_ffn_gate_w, L0_ffn_gate_b, L0_ffn_w1, L0_ffn_b1, L0_ffn_w2, L0_ffn_b2, L0_ffn_gamma, L0_ffn_beta)[0]
    xn = _layernorm(x, axis=-1)
    x = x + _L1_gnn_ref(xn, src, dst, L1_gnn_Wp1, L1_gnn_bp1, L1_gnn_Wm1, L1_gnn_bm1, L1_gnn_Wm2, L1_gnn_bm2, L1_gnn_Wm3, L1_gnn_bm3, L1_gnn_ln2_g, L1_gnn_ln2_b, L1_gnn_ln3_g, L1_gnn_ln3_b) + _L1_mix_ref(xn[None], L1_mix_wq, L1_mix_bq, L1_mix_wk, L1_mix_bk, L1_mix_wv, L1_mix_bv, L1_mix_wo, L1_mix_bo)[0]
    x = x + _L1_ffn_ref(_layernorm(x, axis=-1)[None], L1_ffn_router_w, L1_ffn_w1, L1_ffn_b1, L1_ffn_w2, L1_ffn_b2)[0]
    return x

_drawn_inputs = setup_inputs


def setup_inputs(seed=0):
    import zlib

    import numpy as np

    out = dict(_drawn_inputs(seed))
    spreads = {'L0_gnn_bias': (0.0, 0.46),
     'L0_mix_b_qkv': (0.0, 0.1),
     'L0_mix_norm_g': (1.0, 0.6),
     'L0_mix_norm_b': (0.0, 0.8),
     'L0_mix_b_fc1': (0.0, 0.8),
     'L0_mix_b_fc2': (0.0, 0.46),
     'L0_ffn_gate_b': (0.0, 0.762),
     'L0_ffn_b1': (0.0, 0.8),
     'L0_ffn_b2': (0.0, 0.689),
     'L0_ffn_gamma': (1.0, 0.2),
     'L0_ffn_beta': (0.0, 0.509),
     'L1_gnn_bp1': (0.0, 0.8),
     'L1_gnn_bm1': (0.0, 0.8),
     'L1_gnn_bm2': (0.0, 0.8),
     'L1_gnn_bm3': (0.0, 0.8),
     'L1_gnn_ln2_g': (1.0, 0.2),
     'L1_gnn_ln2_b': (0.0, 0.553),
     'L1_gnn_ln3_g': (1.0, 0.559),
     'L1_gnn_ln3_b': (0.0, 0.537),
     'L1_mix_bq': (0.0, 0.8),
     'L1_mix_bk': (0.0, 0.8),
     'L1_mix_bv': (0.0, 0.513),
     'L1_mix_bo': (0.0, 0.515),
     'L1_ffn_b1': (0.0, 0.8),
     'L1_ffn_b2': (0.0, 0.8)}
    factors = {'L0_mix_w_fc1': 3.373,
     'L0_mix_w_fc2': 3.213,
     'L0_ffn_gate_w': 3.902,
     'L0_ffn_w1': 6.031,
     'L0_ffn_w2': 4.845,
     'L1_mix_wq': 8.0,
     'L1_mix_wk': 8.0,
     'L1_mix_wv': 5.094,
     'L1_mix_wo': 3.128}
    for name, (base, spread) in spreads.items():
        noise = np.random.default_rng([zlib.crc32(name.encode()), seed]).standard_normal(out[name].shape)
        drawn = base * np.exp(spread * noise) if base else spread * noise
        out[name] = jnp.asarray(drawn.astype(out[name].dtype))
    for name, factor in factors.items():
        out[name] = (out[name] * factor).astype(out[name].dtype)
    return out
```

```python
from contextlib import ExitStack

import concourse.bass as bass
from concourse import mybir

F32 = mybir.dt.float32
BF16 = mybir.dt.bfloat16
I32 = mybir.dt.int32
U32 = mybir.dt.uint32
ALU = mybir.AluOpType
ACT = mybir.ActivationFunctionType
AX = mybir.AxisListType

P = 128
N = 3125
NT = -(-N // P)
NP = NT * P
G = 5
J = NT // G
GW = J * P
HALF = GW // 2
D = 256
KD = D // P
E = 53125
SLOTS = 3
RING = 14
TURN = 2 * RING
STORE = RING // 2
TURNS = SLOTS * G
LANE = TURNS * TURN
EP = P * LANE
LO = 64
HI = NP // LO
HOT = LANE // G
EPS = 1e-5
FAR = 1.5e38
ROUND = 12582912.0
HIDDEN = 3 * D
KH = HIDDEN // P
HEAD0 = D // 4
HEAD1 = D // 8
PER1 = P // HEAD1
assert NT == G * J and NP % LO == 0 and EP >= E and LANE % G == 0


class Chain:

    def __init__(self, engine, sem, before=0):
        self.engine, self.sem, self.n = engine, sem, before

    def __call__(self, instruction):
        self.n += 1
        instruction.then_inc(self.sem, 1)
        self.engine.wait_ge(self.sem, self.n)


class Core:

    def __init__(self, nc, ctx, dram):
        self.nc, self.ctx, self.dram = nc, ctx, dram
        self.live = []
        self.x = self.sb("x_acc", [P, NT, D])
        self.ident = self.sb("ident", [P, P])
        self.ones = self.sb("ones", [P, P])
        self.upper = self.sb("upper", [P, P])
        self.eps = self.sb("eps", [P, 1])
        self.real = self.sb("real", [P, NT])
        self.count_up = self.sb("count_up", [P, P], I32)
        self.keep = self.sb("keep", [P, LANE + TURN])
        self.cut = self.sb("cut", [P, LANE + TURN])
        self.src = self.sb("src_idx", [P, LANE + TURN], U32)
        self.lane_keep = self.sb("lane_keep", [P, P])
        self.lane_cut = self.sb("lane_cut", [P, P])
        self.end_idx = self.sb("end_idx", [P, NT], U32)
        self.run_idx = self.sb("run_idx", [P, 1], U32)
        self.fix_idx = self.sb("fix_idx", [P, 1], U32)
        self.bank = [ctx.enter_context(nc.psum_tensor(f"bank{i}", [P, 512], F32)) for i in range(8)]

    def sb(self, name, shape, dt=F32):
        return self.ctx.enter_context(self.nc.sbuf_tensor(name, shape, dt))

    def sem(self, name):
        self.live.append(self.nc.alloc_semaphore(name))
        return self.live[-1]

    def retire(self):
        if self.live:
            self.nc.clear_and_free_semaphores(self.live)
            self.nc.all_engine_barrier()
            self.live = []

    def sems(self, prefix, *names):
        return [self.sem(f"{prefix}_{n}") for n in names]


class Local:

    def __init__(self, c, own, prefix):
        self.c, self.own, self.prefix = c, own, prefix
        own.callback(c.retire)

    def __call__(self, name, shape, dt=F32):
        return self.own.enter_context(self.c.nc.sbuf_tensor(f"{self.prefix}_{name}", shape, dt))


def all_rows(ap):
    n = ap.shape[0]
    return ap.rearrange("(a n) -> a n", a=1).to_broadcast([P, n])


def one_row(ap):
    return ap.rearrange("(a n) -> a n", a=1)


def chunked(ap):
    return ap.rearrange("(k p) n -> p k n", p=P)


def group_rows(table, g):
    return table.rearrange("(g j p) d -> g p j d", g=G, p=P)[g]


class Norm:

    STEPS = 7

    def __init__(self, c, sb, prefix, width=J):
        self.c = c
        self.stats = sb(f"{prefix}_stats", [P, width, 6])
        self.m = sb(f"{prefix}_moment", [P, 4, width])
        self.var = sb(f"{prefix}_var", [P, width])
        self.std = sb(f"{prefix}_std", [P, width])
        self.rstd = sb(f"{prefix}_rstd", [P, width])
        self.shift = sb(f"{prefix}_shift", [P, width])
        self.var_ready, self.std_ready, self.step, self.go = c.sems(
            prefix, "var_ready", "std_ready", "norm_step", "norm_go")

    def vector(self, vec, g, rows):
        vec.sem_inc(self.go, 1)
        step = Chain(vec, self.step, g * self.STEPS)
        width = self.var.shape[1]
        for j in range(width):
            last = vec.bn_stats(self.stats[:, j, :], rows(j))
        step(last)
        self.moments(vec, step, g)

    def moments(self, vec, step, g):
        st, m = self.stats, self.m
        step(vec.tensor_tensor(m[:, 0, :], st[:, :, 1], st[:, :, 4], ALU.add))
        step(vec.tensor_tensor(m[:, 1, :], st[:, :, 1], st[:, :, 4], ALU.subtract))
        step(vec.tensor_tensor(m[:, 2, :], st[:, :, 2], st[:, :, 5], ALU.add))
        step(vec.tensor_tensor(m[:, 3, :], m[:, 1, :], m[:, 1, :], ALU.mult))
        vec.scalar_tensor_tensor(out=self.var[:, :], in0=m[:, 3, :], scalar=D / 4.0, in1=m[:, 2, :],
                                 op0=ALU.mult, op1=ALU.add).then_inc(self.var_ready, 1)
        vec.wait_ge(self.std_ready, g + 1)
        step(vec.reciprocal(self.rstd[:, :], self.std[:, :]))
        step(vec.scalar_tensor_tensor(out=self.shift[:, :], in0=m[:, 0, :], scalar=-0.5, in1=self.rstd[:, :],
                                      op0=ALU.mult, op1=ALU.mult))

    def scalar(self, act, g):
        act.wait_ge(self.var_ready, g + 1)
        act.activation(self.std[:, :], self.var[:, :], ACT.Sqrt, bias=self.c.eps[:, 0:1],
                       scale=1.0 / D).then_inc(self.std_ready, 1)

    def apply(self, vec, out, row, j):
        return vec.tensor_scalar(out, row, self.rstd[:, j:j + 1], self.shift[:, j:j + 1], ALU.mult, ALU.add)


def setup(c):
    nc, dram = c.nc, c.dram
    with ExitStack() as own:
        sb = Local(c, own, "setup")
        dst = sb("dst", [P, LANE], I32)
        before = sb("dst_before", [P, LANE], I32)
        run = sb("run", [P, LANE])
        step_no = sb("step_no", [P, LANE], I32)
        run_end = sb("run_end", [P, 1])
        lane_no = sb("lane_no", [P, 1], I32)
        lane_f = sb("lane_f", [P, 4])
        lane_full = sb("lane_full", [P, 1])
        diag = sb("diag", [P, P])
        zero = sb("zero", [P, D])
        z = sb("z", [P, J, D])
        zt = sb("zt", [P, KD, GW])
        norm = Norm(c, sb, "setup")
        x_in, edges_in, pool_step, const_ready, step_sem, consts_out = c.sems(
            "setup", "x_in", "edges_in", "pool_step", "const_ready", "step", "consts_out")
        diag_ready, lanes_ready, z_ready, z_saved, flipped, taken, zt_saved = c.sems(
            "setup", "diag_ready", "lanes_ready", "z_ready", "z_saved", "flipped", "taken", "zt_saved")
        block = own.enter_context(nc.Block())
        lanes = c.bank[7][:, 0:P]

        @block.sync
        def _(sp):
            def lane_view(at):
                return dram["dst"][at:at + EP].rearrange("(p k) -> p k", p=P)

            sp.dma_start(c.x[:, :, :], dram["x"].rearrange("(t p) d -> p t d", p=P)).then_inc(x_in, 16)
            sp.dma_start(dst[:, :], lane_view(1)).then_inc(edges_in, 16)
            sp.dma_start(before[:, :], lane_view(0)).then_inc(edges_in, 16)
            sp.dma_start(c.src[:, 0:LANE], dram["src"].rearrange("(p k) -> p k", p=P).bitcast(U32)
                         ).then_inc(edges_in, 16)
            sp.wait_ge(const_ready, 1)
            sp.dma_start(dram["state"][EP:EP + P, :], zero[:, :]).then_inc(consts_out, 16)
            sp.dma_start(dram["state"][EP + P:EP + P + 1, :], zero[0:1, :]).then_inc(consts_out, 16)
            for k in range(2):
                sp.dma_start(dram["expert_out"][k * NP + N:k * NP + NP, :], zero[0:NP - N, :]
                             ).then_inc(consts_out, 16)
            with sp.Fori(0, G) as g:
                sp.wait_ge(z_ready, g * J + J)
                sp.dma_start(group_rows(dram["z0"], g), z[:, :, :]).then_inc(z_saved, 16)
                sp.wait_ge(taken, g * J + 2 * J)
                sp.dma_start(dram["z0_cols"][:, :, bass.ds(g * GW, GW)], zt[:, :, :]).then_inc(zt_saved, 16)
            sp.wait_ge(consts_out, 4 * 16)
            sp.wait_ge(z_saved, 16 * G + 16)
            sp.wait_ge(zt_saved, 16 * G + 16)

        @block.gpsimd
        def _(pool):
            step = Chain(pool, pool_step)
            pool.memset(zero[:, :], 0.0)
            pool.memset(c.ones[:, :], 1.0)
            pool.memset(c.eps[:, :], EPS)
            pool.memset(c.src[:, LANE:], 0)
            pool.iota(c.count_up[:, :], pattern=[[1, P]], base=0, channel_multiplier=0)
            pool.iota(step_no[:, :], pattern=[[1, LANE]], base=0, channel_multiplier=0)
            pool.iota(lane_no[:, :], pattern=[[0, 1]], base=0, channel_multiplier=1)
            pool.memset(c.ident[:, :], 0.0)
            pool.memset(c.real[:, :], 1.0)
            step(pool.memset(c.upper[:, :], 1.0))
            pool.affine_select(out=c.ident[:, :], in_=c.ident[:, :], compare_op=ALU.not_equal, fill=1.0,
                               base=0, pattern=[[-1, P]], channel_multiplier=1)
            pool.affine_select(out=c.real[:, :], in_=c.real[:, :], compare_op=ALU.is_ge, fill=0.0,
                               base=N - 1, pattern=[[-P, NT]], channel_multiplier=-1)
            pool.affine_select(out=c.upper[:, :], in_=c.upper[:, :], compare_op=ALU.is_gt, fill=0.0,
                               base=0, pattern=[[1, P]], channel_multiplier=-1).then_inc(const_ready, 1)

        @block.vector
        def _(vec):
            step = Chain(vec, step_sem)
            vec.wait_ge(edges_in, 3 * 16)
            vec.wait_ge(const_ready, 1)
            vec.memset(c.keep[:, LANE:], 0.0)
            vec.memset(c.cut[:, LANE:], 0.0)
            step(vec.tensor_tensor(c.keep[:, 0:LANE], dst[:, :], before[:, :], ALU.is_equal))
            step(vec.tensor_scalar(c.cut[:, 0:LANE], c.keep[:, 0:LANE], FAR, -FAR, ALU.mult, ALU.add))
            step(vec.memset(c.cut[:, 0:1], -FAR))
            step(vec.tensor_tensor(lane_full[:, :], dst[:, LANE - 1:LANE], before[:, 0:1], ALU.is_equal))
            vec.tensor_scalar(diag[:, :], c.ident[:, :], lane_full[:, 0:1], None, ALU.mult
                              ).then_inc(diag_ready, 1)
            step(vec.tensor_scalar(run[:, :], c.keep[:, 0:LANE], float(LANE), None, ALU.mult))
            step(vec.tensor_tensor(run[:, :], run[:, :], step_no[:, :], ALU.add))
            step(vec.tensor_reduce(run_end[:, :], run[:, :], AX.X, ALU.min))
            f = lane_f
            step(vec.tensor_scalar(f[:, 0:1], lane_no[:, :], float(LANE), None, ALU.mult))
            step(vec.tensor_scalar(f[:, 1:2], run_end[:, :], -1.0, 0.0, ALU.add, ALU.max))
            step(vec.tensor_tensor(f[:, 1:2], f[:, 1:2], f[:, 0:1], ALU.add))
            step(vec.tensor_copy(c.run_idx[:, :], f[:, 1:2]))
            step(vec.tensor_scalar(f[:, 2:3], run_end[:, :], 0.0, None, ALU.is_gt))
            step(vec.tensor_scalar(f[:, 3:4], lane_no[:, :], EP + 1.0, None, ALU.add))
            step(vec.tensor_tensor(f[:, 0:1], f[:, 1:2], f[:, 3:4], ALU.subtract))
            step(vec.tensor_tensor(f[:, 0:1], f[:, 0:1], f[:, 2:3], ALU.mult))
            step(vec.tensor_tensor(f[:, 0:1], f[:, 0:1], f[:, 3:4], ALU.add))
            step(vec.tensor_copy(c.fix_idx[:, :], f[:, 0:1]))
            vec.wait_ge(lanes_ready, 1)
            step(vec.tensor_copy(c.lane_keep[:, :], lanes))
            vec.tensor_scalar(c.lane_cut[:, :], c.lane_keep[:, :], FAR, -FAR, ALU.mult, ALU.add)
            vec.wait_ge(x_in, 16)
            vec.sem_inc(z_saved, 16)
            with vec.Fori(0, G) as g:
                norm.vector(vec, g, lambda j: c.x[:, g * J + j, :])
                vec.wait_ge(z_saved, 16 * g + 16)
                vec.wait_ge(flipped, g * J + 1)
                for j in range(J):
                    norm.apply(vec, z[:, j, :], c.x[:, g * J + j, :], j).then_inc(z_ready, 1)

        @block.tensor
        def _(pe):
            pe.wait_ge(diag_ready, 1)
            pe.matmul(lanes, c.ones[:, :], diag[:, :], start=True, stop=True).then_inc(lanes_ready, 1)
            pe.sem_inc(flipped, 1)
            with pe.Fori(0, G) as g:
                for j in range(J):
                    pe.wait_ge(z_ready, g * J + j + 1)
                    pe.wait_ge(taken, g * J + j + 1)
                    for k in range(KD):
                        last = pe.transpose(c.bank[j][:, k * P:k * P + P], z[:, j, k * P:k * P + P], c.ident[:, :])
                    last.then_inc(flipped, 1)

        @block.scalar
        def _(act):
            act.sem_inc(taken, J)
            act.sem_inc(zt_saved, 16)
            with act.Fori(0, G) as g:
                norm.scalar(act, g)
                act.wait_ge(zt_saved, 16 * g + 16)
                for j in range(J):
                    act.wait_ge(flipped, g * J + j + 2)
                    act.copy(zt[:, :, j * P:j * P + P], c.bank[j][:, 0:D].rearrange("p (k n) -> p k n", k=KD)
                             ).then_inc(taken, 1)


def reuse(j, n):
    return n if j >= n else J + j - max(i for i in range(J) if i % n == j % n)


class Work:

    def buffers(self, sb):
        pass

    def first(self, engine, which):
        pass

    def before(self, engine, which):
        pass

    def turn(self, engine, which, g):
        pass

    def after(self, engine, which):
        pass


def edge_walk(c, name, table, reduce, work=(Work(), Work(), Work())):
    nc, dram = c.nc, c.dram
    restart = c.cut if reduce == "max" else c.keep
    join = ALU.add if reduce == "max" else ALU.mult
    merge = ALU.add if reduce == "sum" else ALU.max
    lane_restart = c.lane_cut if reduce == "max" else c.lane_keep
    nothing = -FAR if reduce == "max" else 0.0
    CREDIT = RING + 1
    states = dram["state"][0:EP, :].rearrange("(p k) d -> p k d", p=P)

    with ExitStack() as own:
        sb = Local(c, own, name)
        ring = sb("ring", [P, RING, D])
        state = sb("state", [P, RING, D])
        idx = sb("idx", [P, 2, RING], U32)
        mark = sb("mark", [P, 2, RING])
        scanned = sb("scanned", [P, KD, P + 1])
        carry = sb("carry", [P, D])
        run = sb("run", [P, D])
        walked, idx_ready, turn_go = c.sems(name, "walked", "idx_ready", "turn_go")
        stored = c.sems(name, "stored0", "stored1")
        arrived = c.sems(name, *(f"arrived{j}" for j in range(RING)))
        flipped, summed, back, carry_rows, run_in, merged, fixed = c.sems(
            name, "flipped", "summed", "back", "carry_rows", "run_in", "merged", "fixed")
        for w in work:
            w.buffers(sb)
        block = own.enter_context(nc.Block())

        def slots(engine, which, walk_turn):
            for w in work:
                w.first(engine, which)
            for s, w in enumerate(work):
                w.before(engine, which)
                with engine.Fori(0, G) as g:
                    walk_turn(s * G + g, g, w)
                w.after(engine, which)

        @block.gpsimd
        def _(pool):
            with pool.Fori(0, TURNS) as i:
                for h in range(2):
                    pool.wait_ge(idx_ready, i * 2 + h + 1)
                    for j in range(RING):
                        if j % 2 == 0:
                            pool.wait_ge(walked, i * TURN + (h * RING + j + 2 + 1))
                            pool.sem_inc(turn_go, 1)
                        pool.indirect_dma_start(ring[:, j, :], None, table[:, :],
                                                bass.IndirectOffsetOnAxis(idx[:, h, j:j + 1], 0)
                                                ).then_inc(arrived[j], 16)
            for q in range(2):
                pool.wait_ge(stored[q], 16 + 16 * TURNS * 2)
            pool.indirect_dma_start(run[:, :], None, dram["state"][:, :],
                                    bass.IndirectOffsetOnAxis(c.run_idx[:, 0:1], 0)).then_inc(run_in, 16)
            pool.wait_ge(merged, 1)
            pool.indirect_dma_start(dram["state"][:, :], bass.IndirectOffsetOnAxis(c.fix_idx[:, 0:1], 0),
                                    run[:, :], None).then_inc(fixed, 16)
            pool.wait_ge(fixed, 16)

        @block.vector
        def _(vec):
            def stage(i, h):
                at = i * TURN + h * RING
                vec.tensor_copy(mark[:, h, :], restart[:, bass.ds(at, RING)])
                vec.tensor_copy(idx[:, h, :], c.src[:, bass.ds(at, RING)]).then_inc(idx_ready, 1)

            def walk_turn(i, g, w):
                for h in range(2):
                    for j in range(RING):
                        if j % STORE == 0:
                            vec.wait_ge(stored[j // STORE], i * 32 + (h + 1) * 16)
                        vec.wait_ge(arrived[j], i * 32 + (h + 1) * 16)
                        vec.wait_ge(walked, i * TURN + (h * RING + j + CREDIT))
                        vec.scalar_tensor_tensor(out=state[:, j, :], in0=state[:, (j - 1) % RING, :],
                                                 scalar=mark[:, h, j:j + 1], in1=ring[:, j, :],
                                                 op0=join, op1=merge).then_inc(walked, 1)
                    vec.wait_ge(walked, i * TURN + ((h + 1) * RING + CREDIT))
                    stage(i + 1, h)
                    w.turn(vec, f"vector{h}", g)
                    vec.wait_ge(idx_ready, i * 2 + (h + 3))

            stage(0, 0)
            stage(0, 1)
            vec.memset(state[:, RING - 1, :], 0.0).then_inc(walked, 1)
            vec.sem_inc(walked, RING)
            for q in range(2):
                vec.sem_inc(stored[q], 16)
            vec.wait_ge(idx_ready, 2)
            slots(vec, "vector", walk_turn)
            vec.memset(scanned[:, :, 0:1], nothing)
            vec.wait_ge(flipped, 1)
            for k in range(KD):
                vec.tensor_tensor_scan(scanned[:, k, 1:P + 1], lane_restart[:, :], c.bank[0][:, k * P:k * P + P],
                                       nothing, join, merge).then_inc(summed, 1)
            vec.wait_ge(run_in, 16)
            vec.wait_ge(carry_rows, 1)
            vec.tensor_tensor(run[:, :], run[:, :], carry[:, :], merge).then_inc(merged, 1)

        @block.sync
        def _(sp):
            def walk_turn(i, g, w):
                w.turn(sp, "sync", g)
                for q in range(4):
                    first = (q % 2) * STORE
                    sp.wait_ge(walked, i * TURN + ((q + 1) * STORE + CREDIT))
                    sp.dma_start(states[:, bass.ds(i * TURN + q * STORE, STORE), :],
                                 state[:, first:first + STORE, :]).then_inc(stored[q % 2], 16)

            slots(sp, "sync", walk_turn)
            for q in range(2):
                sp.wait_ge(stored[q], 16 + 16 * TURNS * 2)

        @block.tensor
        def _(pe):
            slots(pe, "tensor", lambda i, g, w: w.turn(pe, "tensor", g))
            pe.wait_ge(walked, LANE + CREDIT)
            for k in range(KD):
                last = pe.transpose(c.bank[0][:, k * P:k * P + P], state[:, RING - 1, k * P:k * P + P],
                                    c.ident[:, :])
            last.then_inc(flipped, 1)
            pe.wait_ge(summed, KD)
            for k in range(KD):
                last = pe.transpose(c.bank[1][:, k * P:k * P + P], scanned[:, k, 0:P], c.ident[:, :])
            last.then_inc(back, 1)

        @block.scalar
        def _(act):
            slots(act, "scalar", lambda i, g, w: w.turn(act, "scalar", g))
            act.wait_ge(back, 1)
            act.copy(carry[:, :], c.bank[1][:, 0:D]).then_inc(carry_rows, 1)


def columns(ap):
    return ap.rearrange("(k p) -> p k", p=P)


class EdgeCount:

    def __init__(self, c):
        self.c = c

    def buffers(self, sb):
        c = self.c
        self.dst = sb("dst", [P, LANE], I32)
        self.low = sb("dst_low", [P, LANE], I32)
        self.is_low = sb("is_low", [P, HOT, LO], BF16)
        self.is_high = sb("is_high", [P, HOT, HI], BF16)
        self.none = sb("none", [P, LO], BF16)
        self.along = sb("along", [HI, LO])
        self.total = sb("total", [HI, LO])
        self.zero = sb("zero", [1, 1])
        self.upto = sb("upto", [P, NT])
        self.start = sb("start", [P, NT])
        self.t = [sb(f"node_t{i}", [P, NT]) for i in range(2)]
        (self.dst_in, self.split, self.hot, self.counted, self.closed, self.step, self.along_ready,
         self.before_ready, self.total_ready, self.table_out, self.table_in, self.opened) = c.sems(
            "count", "dst_in", "split", "hot", "counted", "closed", "step", "along_ready", "before_ready",
            "total_ready", "table_out", "table_in", "opened")
        self.counts = c.bank[3][0:HI, 0:LO]
        self.before_rows = c.bank[6][0:HI, 0:1]
        self.chain = None

    def first(self, eng, which):
        c, nc = self.c, self.c.nc
        if which == "sync":
            eng.dma_start(self.dst[:, :], c.dram["dst"][1:1 + EP].rearrange("(p k) -> p k", p=P)
                          ).then_inc(self.dst_in, 16)
        if which == "vector":
            self.chain = Chain(eng, self.step)
            eng.memset(self.zero[:, :], 0.0)
            eng.memset(self.none[:, :], 0.0).then_inc(self.opened, 1)
            eng.wait_ge(self.dst_in, 16)
            self.chain(eng.tensor_scalar(self.low[:, :], self.dst[:, :], LO - 1, None, ALU.bitwise_and))
            self.chain(eng.tensor_scalar(self.dst[:, :], self.dst[:, :], LO.bit_length() - 1, None,
                                         ALU.arith_shift_right))
        if which == "tensor":
            eng.wait_ge(self.opened, 1)
            eng.matmul(self.counts, self.none[:, 0:HI], self.none[:, :], start=True, stop=False,
                       skip_group_check=True).then_inc(self.counted, 1)

    def turn(self, eng, which, g):
        c = self.c
        if which == "vector0":
            eng.wait_ge(self.counted, g + 1)
            part = bass.ds(g * HOT, HOT)
            eng.tensor_tensor(self.is_low[:, :, :],
                              self.low[:, part].unsqueeze(2).to_broadcast([P, HOT, LO]),
                              c.count_up[:, 0:LO].unsqueeze(1).to_broadcast([P, HOT, LO]), ALU.is_equal)
            eng.tensor_tensor(self.is_high[:, :, :],
                              self.dst[:, part].unsqueeze(2).to_broadcast([P, HOT, HI]),
                              c.count_up[:, 0:HI].unsqueeze(1).to_broadcast([P, HOT, HI]),
                              ALU.is_equal).then_inc(self.hot, 1)
        if which == "tensor":
            eng.wait_ge(self.hot, g + 1)
            for k in range(HOT):
                last = eng.matmul(self.counts, self.is_high[:, k, :], self.is_low[:, k, :], start=False,
                                  stop=False, skip_group_check=True)
            last.then_inc(self.counted, 1)

    def after(self, eng, which):
        c, flat, step = self.c, self.c.dram["node_ends"], self.chain
        if which == "tensor":
            eng.matmul(self.counts, self.none[:, 0:HI], self.none[:, :], start=False, stop=True,
                       skip_group_check=True).then_inc(self.closed, 1)
            eng.wait_ge(self.along_ready, 1)
            eng.matmul(self.before_rows, c.upper[0:HI, 0:HI], self.along[:, LO - 1:LO], start=True,
                       stop=True).then_inc(self.before_ready, 1)
        if which == "vector":
            eng.wait_ge(self.closed, 1)
            eng.tensor_tensor_scan(self.along[:, :], c.ones[0:HI, 0:LO], self.counts, 0.0, ALU.mult,
                                   ALU.add).then_inc(self.along_ready, 1)
            eng.wait_ge(self.along_ready, 1)
            eng.wait_ge(self.before_ready, 1)
            eng.tensor_scalar(self.total[:, :], self.along[:, :], self.before_rows, None, ALU.add
                              ).then_inc(self.total_ready, 1)
        if which == "sync":
            eng.wait_ge(self.total_ready, 1)
            eng.dma_start(one_row(flat[0:1]), self.zero[:, :]).then_inc(self.table_out, 16)
            eng.dma_start(flat[1:1 + NP].rearrange("(h l) -> h l", h=HI), self.total[:, :]
                          ).then_inc(self.table_out, 16)
            eng.wait_ge(self.table_out, 32)
            with c.nc.allow_non_contiguous_dma(reason="node numbers from rows to columns, once"):
                eng.dma_start(self.upto[:, :], flat[1:1 + NP].rearrange("(t p) -> p t", p=P)
                              ).then_inc(self.table_in, 16)
                eng.dma_start(self.start[:, :], flat[0:NP].rearrange("(t p) -> p t", p=P)
                              ).then_inc(self.table_in, 16)

    def finish(self, vec):
        step, (a, b) = self.chain, self.t
        vec.wait_ge(self.table_in, 32)
        step(vec.tensor_tensor(a[:, :], self.upto[:, :], self.start[:, :], ALU.is_gt))
        step(vec.tensor_scalar(b[:, :], self.upto[:, :], -1.0 - EP, None, ALU.add))
        step(vec.tensor_tensor(b[:, :], b[:, :], a[:, :], ALU.mult))
        step(vec.tensor_scalar(b[:, :], b[:, :], float(EP), None, ALU.add))
        step(vec.tensor_copy(self.c.end_idx[:, :], b[:, :]))


class Columns:

    def __init__(self, c, sb, name, table):
        self.table = table
        self.buf = sb(f"{name}_cols", [P, KD, GW])
        self.loaded, self.free = c.sems(name, "cols_in", "cols_free")

    def open(self, pe):
        pe.sem_inc(self.free, 1)

    def load(self, sp, g, n):
        sp.wait_ge(self.free, g + n + 1)
        sp.dma_start(self.buf[:, :, :], self.table[:, :, bass.ds(g * GW, GW)]).then_inc(self.loaded, 16)

    def wait(self, pe, g, n):
        pe.wait_ge(self.loaded, g * 16 + (n + 1) * 16)


class KeyValue0(Work):

    def __init__(self, c):
        self.c = c
        self.count = EdgeCount(c)

    def buffers(self, sb):
        c = self.c
        self.count.buffers(sb)
        self.cols = Columns(c, sb, "mix0", c.dram["z0_cols"])
        self.w = sb("w_kv", [P, KD, 2 * D])
        self.bias = sb("b_kv", [P, 2 * D])
        self.kv = sb("kv", [P, 2, 2 * D])
        self.wqt = sb("w_q_t", [P, KD, D])
        self.bq = sb("b_q", [P, KD])
        self.zero = sb("zeros", [P, D])
        self.top = sb("top", [P, KD])
        self.low = sb("minus_top", [P, KD])
        self.mass = sb("mass", [P, KD])
        self.inv = sb("inv_mass", [P, KD])
        self.attn = sb("attn", [P, KD, P])
        self.attn_t = sb("attn_t", [P, KD, P])
        self.map = sb("map", [P, KD, D])
        self.row = sb("map_row", [1, D])
        (self.w_in, self.made, self.product, self.rows, self.used, self.closed, self.top_ready, self.low_ready,
         self.exp_ready, self.attn_ready, self.attn_flipped, self.attn_t_ready, self.map_done, self.map_ready,
         self.step) = c.sems(
            "kv0", "w_in", "made", "product", "rows", "used", "closed", "top_ready", "low_ready", "exp_ready",
            "attn_ready", "attn_flipped", "attn_t_ready", "map_done", "map_ready", "step")
        self.sums = c.bank[2]

    def first(self, eng, which):
        c, d = self.c, self.c.dram
        self.count.first(eng, which)
        if which == "sync":
            eng.dma_start(self.w[:, :, :], chunked(d["L0_mix_w_qkv"])[:, :, D:]).then_inc(self.w_in, 16)
            eng.dma_start(self.bias[:, :], all_rows(d["L0_mix_b_qkv"][D:])).then_inc(self.w_in, 16)
            eng.dma_start(self.wqt[:, :, :], chunked(d["w_q_t"])).then_inc(self.w_in, 16)
            with c.nc.allow_non_contiguous_dma(reason="a bias as columns"):
                eng.dma_start(self.bq[:, :], columns(d["L0_mix_b_qkv"][0:D])).then_inc(self.w_in, 16)
        if which == "vector":
            eng.memset(self.attn[:, :, :], 0.0)
            eng.memset(self.zero[:, :], 0.0).then_inc(self.made, 1)
            eng.wait_ge(self.w_in, 4 * 16)
            eng.sem_inc(self.rows, J)
        if which == "tensor":
            self.cols.open(eng)
            eng.wait_ge(self.w_in, 4 * 16)
            eng.wait_ge(self.made, 1)
            eng.matmul(self.sums[:, 0:D], self.zero[:, 0:P], self.zero[:, :], start=True, stop=False,
                       skip_group_check=True)
            eng.sem_inc(self.used, J)

    def turn(self, eng, which, g):
        c = self.c
        self.count.turn(eng, which, g)
        if which == "sync":
            self.cols.load(eng, g, 0)
        if which == "tensor":
            self.cols.wait(eng, g, 0)

            def product(j):
                eng.wait_ge(self.rows, g * J + (j + 1 + J - reuse(j, 2)))
                for k in range(KD):
                    last = eng.matmul(c.bank[j % 2][:, :], self.cols.buf[:, k, j * P:j * P + P],
                                      self.w[:, k, :], start=(k == 0), stop=(k == KD - 1))
                last.then_inc(self.product, 1)

            product(0)
            for j in range(J):
                if j + 1 < J:
                    product(j + 1)
                eng.wait_ge(self.rows, g * J + (j + 1 + J))
                for k in range(KD):
                    last = eng.matmul(self.sums[:, k * P:k * P + P], self.kv[:, j % 2, k * P:k * P + P],
                                      self.kv[:, j % 2, D + k * P:D + k * P + P], start=False, stop=False,
                                      skip_group_check=True)
                last.then_inc(self.used, 1)
            eng.wait_ge(self.product, g * J + J)
            eng.sem_inc(self.cols.free, 1)
        if which == "vector1":
            for j in range(J):
                eng.wait_ge(self.product, g * J + (j + 1))
                eng.wait_ge(self.used, g * J + (j + 1 + J - reuse(j, 2)))
                eng.scalar_tensor_tensor(out=self.kv[:, j % 2, :], in0=self.bias[:, :],
                                         scalar=c.real[:, bass.ds(g * J + j, 1)], in1=c.bank[j % 2][:, :],
                                         op0=ALU.mult, op1=ALU.add).then_inc(self.rows, 1)

    def after(self, eng, which):
        c = self.c
        self.count.after(eng, which)
        heads = [(k, h) for k in range(KD) for h in range(P // HEAD0)]
        scale = HEAD0 ** -0.5

        def block(buf, k, h):
            return buf[h * HEAD0:(h + 1) * HEAD0, k, h * HEAD0:(h + 1) * HEAD0]

        sums = self.sums[:, 0:D].rearrange("p (k n) -> p k n", k=KD)
        if which == "tensor":
            eng.matmul(self.sums[:, 0:D], self.zero[:, 0:P], self.zero[:, :], start=False, stop=True,
                       skip_group_check=True).then_inc(self.closed, 1)
            eng.wait_ge(self.attn_ready, 1)
            for k in range(KD):
                last = eng.transpose(c.bank[4][:, k * P:k * P + P], self.attn[:, k, :], c.ident[:, :])
            last.then_inc(self.attn_flipped, 1)
            eng.wait_ge(self.attn_t_ready, 1)
            for m in range(KD):
                for k in range(KD):
                    eng.matmul(c.bank[5][:, m * D + k * P:m * D + k * P + P], self.wqt[:, k, m * P:m * P + P],
                               self.attn_t[:, k, :], start=True, stop=True)
            for k in range(KD):
                last = eng.matmul(c.bank[7][0:1, k * P:k * P + P], self.bq[:, k:k + 1], self.attn_t[:, k, :],
                                  start=True, stop=True)
            last.then_inc(self.map_done, 1)
        if which == "vector":
            step = Chain(eng, self.step)
            eng.wait_ge(self.closed, 1)
            for k, h in heads:
                part = slice(h * HEAD0, (h + 1) * HEAD0)
                last = eng.tensor_reduce(self.top[part, k:k + 1], block(sums, k, h), AX.X, ALU.max)
            step(last)
            eng.tensor_scalar(self.low[:, :], self.top[:, :], -scale, None, ALU.mult).then_inc(self.low_ready, 1)
            eng.wait_ge(self.exp_ready, 1)
            step(eng.reciprocal(self.inv[:, :], self.mass[:, :]))
            for k in range(KD):
                last = eng.tensor_scalar(self.attn[:, k, :], self.attn[:, k, :], self.inv[:, k:k + 1], None,
                                         ALU.mult)
            last.then_inc(self.attn_ready, 1)
            eng.wait_ge(self.map_done, 1)
            for k in range(KD):
                part = slice(k * P, k * P + P)
                step(eng.tensor_copy(self.map[:, k, :], c.bank[5][:, k * D:k * D + D]))
                step(eng.tensor_tensor(self.map[:, k, part], c.bank[5][:, k * D + k * P:k * D + k * P + P],
                                       c.ident[:, :], ALU.add))
            eng.tensor_copy(self.row[:, :], c.bank[7][0:1, 0:D]).then_inc(self.map_ready, 1)
            self.count.finish(eng)
        if which == "scalar":
            eng.wait_ge(self.low_ready, 1)
            for k, h in heads:
                part = slice(h * HEAD0, (h + 1) * HEAD0)
                last = eng.activation(block(self.attn, k, h), block(sums, k, h), ACT.Exp,
                                      bias=self.low[part, k:k + 1], scale=scale,
                                      accum_out=self.mass[part, k:k + 1])
            last.then_inc(self.exp_ready, 1)
            eng.wait_ge(self.attn_flipped, 1)
            eng.copy(self.attn_t[:, :, :], c.bank[4][:, 0:D].rearrange("p (k n) -> p k n", k=KD)
                     ).then_inc(self.attn_t_ready, 1)


class Mixed0(Work):

    def __init__(self, c, kv):
        self.c, self.kv = c, kv

    def buffers(self, sb):
        c = self.c
        self.x1 = sb("x1", [P, NT, D])
        self.norm = Norm(c, sb, "mixed0", NT)
        self.product, self.rows = c.sems("mixed0", "product", "rows")

    def turn(self, eng, which, g):
        c, kv = self.c, self.kv
        if which == "sync":
            kv.cols.load(eng, g, G)
        if which == "tensor":
            kv.cols.wait(eng, g, G)
            for j in range(J):
                eng.wait_ge(self.rows, g * J + (j + 1 + J - reuse(j, 2)))
                bank = c.bank[4 + j % 2][:, 0:D]
                for k in range(KD):
                    eng.matmul(bank, kv.cols.buf[:, k, j * P:j * P + P], kv.map[:, k, :], start=(k == 0), stop=False)
                eng.matmul(bank, c.ones[0:1, :], kv.row[:, :], start=False, stop=True).then_inc(self.product, 1)
            eng.wait_ge(self.product, g * J + J)
            eng.sem_inc(kv.cols.free, 1)
        if which == "scalar":
            for j in range(J):
                eng.wait_ge(self.product, g * J + (j + 1))
                eng.copy(self.x1[:, g * J + j, :], c.bank[4 + j % 2][:, 0:D]).then_inc(self.rows, 1)
        if which == "vector1":
            for j in range(J):
                eng.wait_ge(self.rows, g * J + (j + 1 + J))
                last = eng.bn_stats(self.norm.stats[:, g * J + j, :], self.x1[:, g * J + j, :])

    def before(self, eng, which):
        if which == "tensor":
            eng.wait_ge(self.kv.map_ready, 1)
        if which == "scalar":
            eng.sem_inc(self.rows, J)

    def after(self, eng, which):
        if which == "vector":
            step = Chain(eng, self.norm.step)
            step(eng.memset(self.norm.rstd[:, :], 0.0))
            self.norm.moments(eng, step, 0)
        if which == "scalar":
            self.norm.scalar(eng, 0)


class Mlp0(Work):

    def __init__(self, c, mixed):
        self.c, self.mixed = c, mixed

    def buffers(self, sb):
        c = self.c
        self.w1 = sb("w_fc1", [P, KD, HIDDEN])
        self.w1g = self.w1
        self.b1 = sb("b_fc1", [P, KH])
        self.b1g = sb("b_fc1_all", [P, KH])
        self.w2 = sb("w_fc2", [P, KH, D])
        self.gain = sb("ln_gain", [P, KD])
        self.offset = sb("ln_offset", [P, KD])
        self.bias = sb("b_rows", [1, 3, D])
        self.z = sb("z1", [P, J, D])
        self.zt = sb("z1_cols", [P, KD, GW])
        self.u = sb("hidden", [P, KH, GW])
        (self.w_in, self.bias_product, self.w_ready, self.bias_ready, self.step, self.z_ready, self.flipped,
         self.zt_ready, self.up, self.up_taken, self.down, self.added) = c.sems(
            "mlp0", "w_in", "bias_product", "w_ready", "bias_ready", "step", "z_ready", "flipped", "zt_ready",
            "up", "up_taken", "down", "added")

    def first(self, eng, which):
        c, d = self.c, self.c.dram
        if which == "sync":
            eng.dma_start(self.w1[:, :, :], chunked(d["L0_mix_w_fc1"])).then_inc(self.w_in, 16)
            eng.dma_start(self.w2[:, :, :], chunked(d["L0_mix_w_fc2"])).then_inc(self.w_in, 16)
            eng.dma_start(self.bias[:, 0, :], one_row(d["L0_mix_b_fc2"])).then_inc(self.w_in, 16)
            eng.dma_start(self.bias[:, 1, :], one_row(d["L0_gnn_bias"])).then_inc(self.w_in, 16)
            with c.nc.allow_non_contiguous_dma(reason="biases as columns"):
                eng.dma_start(self.b1[:, :], columns(d["L0_mix_b_fc1"])).then_inc(self.w_in, 16)
                eng.dma_start(self.gain[:, :], columns(d["L0_mix_norm_g"])).then_inc(self.w_in, 16)
                eng.dma_start(self.offset[:, :], columns(d["L0_mix_norm_b"])).then_inc(self.w_in, 16)
        if which == "tensor":
            eng.wait_ge(self.w_in, 7 * 16)
            for f in range(KH):
                for k in range(KD):
                    last = eng.matmul(c.bank[7][:, f:f + 1], self.w1[:, k, f * P:f * P + P],
                                      self.offset[:, k:k + 1], start=(k == 0), stop=(k == KD - 1))
            last.then_inc(self.bias_product, 1)
        if which == "vector":
            eng.wait_ge(self.w_in, 7 * 16)
            eng.wait_ge(self.bias_product, 1)
            for k in range(KD):
                eng.tensor_scalar(self.w1g[:, k, :], self.w1[:, k, :], self.gain[:, k:k + 1], None, ALU.mult)
            eng.tensor_tensor(self.bias[:, 2, :], self.bias[:, 0, :], self.bias[:, 1, :], ALU.add)
            eng.tensor_tensor(self.b1g[:, :], self.b1[:, :], c.bank[7][:, 0:KH], ALU.add
                              ).then_inc(self.w_ready, 1)
            eng.sem_inc(self.flipped, 1)
            eng.sem_inc(self.added, J)

    def before(self, eng, which):
        if which == "tensor":
            eng.wait_ge(self.w_ready, 1)
            eng.sem_inc(self.down, J)
        if which == "scalar":
            eng.sem_inc(self.zt_ready, J)
            eng.sem_inc(self.up_taken, 3)
            eng.wait_ge(self.w_ready, 1)

    def turn(self, eng, which, g):
        c, x1 = self.c, self.mixed.x1
        ups = 2 * KH
        if which == "vector0":
            eng.wait_ge(self.flipped, g * J + 1)
            for j in range(J):
                n = g * J + j
                eng.tensor_scalar(self.z[:, j, :], x1[:, n, :], self.mixed.norm.rstd[:, bass.ds(n, 1)],
                                  self.mixed.norm.shift[:, bass.ds(n, 1)], ALU.mult, ALU.add
                                  ).then_inc(self.z_ready, 1)
        if which == "vector1":
            for j in range(J):
                n = g * J + j
                eng.wait_ge(self.down, n + (1 + J))
                eng.tensor_tensor(c.x[:, n, :], c.x[:, n, :], c.bank[6 + j % 2][:, 0:D], ALU.add
                                  ).then_inc(self.added, 1)
            eng.wait_ge(self.added, g * J + 2 * J)
            eng.tensor_tensor(c.x[:, bass.ds(g * J, J), :], c.x[:, bass.ds(g * J, J), :],
                              x1[:, bass.ds(g * J, J), :], ALU.add).then_inc(self.step, 1)
            eng.wait_ge(self.step, g + 1)
        if which == "tensor":
            for j in range(J):
                eng.wait_ge(self.z_ready, g * J + (j + 1))
                eng.wait_ge(self.zt_ready, g * J + (j + 1 + J - reuse(j, 2)))
                for k in range(KD):
                    last = eng.transpose(c.bank[j % 2][:, k * P:k * P + P], self.z[:, j, k * P:k * P + P],
                                         c.ident[:, :])
                last.then_inc(self.flipped, 1)
            eng.wait_ge(self.zt_ready, g * J + 2 * J)
            for half in range(2):
                for f in range(KH):
                    n = half * KH + f
                    eng.wait_ge(self.up_taken, g * ups + (n + 1))
                    for k in range(KD):
                        last = eng.matmul(c.bank[2 + n % 3][:, 0:HALF], self.w1g[:, k, f * P:f * P + P],
                                          self.zt[:, k, half * HALF:half * HALF + HALF], start=(k == 0),
                                          stop=(k == KD - 1))
                    last.then_inc(self.up, 1)
            eng.wait_ge(self.up_taken, (g + 1) * ups + 3)
            for j in range(J):
                bank = c.bank[6 + j % 2][:, 0:D]
                eng.wait_ge(self.added, g * J + (j + 1 + J - reuse(j, 2)))
                for f in range(KH):
                    eng.matmul(bank, self.u[:, f, j * P:j * P + P], self.w2[:, f, :], start=(f == 0), stop=False)
                eng.matmul(bank, c.ones[0:1, :], self.bias[:, 2, :], start=False, stop=True).then_inc(self.down, 1)
        if which == "scalar":
            for j in range(J):
                eng.wait_ge(self.flipped, g * J + (j + 2))
                eng.copy(self.zt[:, :, j * P:j * P + P],
                         c.bank[j % 2][:, 0:D].rearrange("p (k n) -> p k n", k=KD)).then_inc(self.zt_ready, 1)
            for half in range(2):
                for f in range(KH):
                    n = half * KH + f
                    eng.wait_ge(self.up, g * ups + (n + 1))
                    if n == 0:
                        eng.wait_ge(self.down, g * J + J)
                    eng.activation(self.u[:, f, half * HALF:half * HALF + HALF], c.bank[2 + n % 3][:, 0:HALF],
                                   ACT.Gelu, bias=self.b1g[:, f:f + 1]).then_inc(self.up_taken, 1)


def stage(c, prefix):
    own = ExitStack()
    return own, Local(c, own, prefix)


def to_columns(pe, bank, rows, ident):
    for k in range(KD):
        last = pe.transpose(bank[:, k * P:k * P + P], rows[:, k * P:k * P + P], ident)
    return last


def split_columns(bank):
    return bank[:, 0:D].rearrange("p (k n) -> p k n", k=KD)


def fetch_nodes(c, pool, fetched, used, arrived):
    for t in range(NT):
        if t >= J:
            pool.wait_ge(used, t - J + 1)
        pool.indirect_dma_start(fetched[:, t % J, :], None, c.dram["state"][:, :],
                                bass.IndirectOffsetOnAxis(c.end_idx[:, t:t + 1], 0)
                                ).then_inc(arrived[t % J], 16)


def convolve0(c, logits):
    own, sb = stage(c, "conv0")
    with own:
        d = c.dram
        agg = sb("agg", [P, J, D])
        agg_t = sb("agg_cols", [P, J, KD, P])
        w = sb("w", [P, KD, D])
        gate = sb("gate", [P, KD, 16])
        gate_bias = sb("gate_bias", [1, 16])
        z = sb("z", [P, J, D])
        z_t = sb("z_cols", [P, J, KD, P])
        norm = Norm(c, sb, "conv0")
        agg_in = c.sems("conv0", *(f"agg_in{j}" for j in range(J)))
        w_in, flipped, agg_ready, product, added, z_ready, z_saved, z_flipped, z_cols, gated, logits_ready = c.sems(
            "conv0", "w_in", "flipped", "agg_ready", "product", "added", "z_ready", "z_saved", "z_flipped",
            "z_cols", "gated", "logits_ready")
        block = own.enter_context(c.nc.Block())

        @block.gpsimd
        def _(pool):
            fetch_nodes(c, pool, agg, flipped, agg_in)

        @block.sync
        def _(sp):
            sp.dma_start(w[:, :, :], chunked(d["L0_gnn_weight"])).then_inc(w_in, 16)
            sp.dma_start(gate[:, :, :], chunked(d["L0_ffn_gate_w"])).then_inc(w_in, 16)
            sp.dma_start(gate_bias[:, :], one_row(d["L0_ffn_gate_b"])).then_inc(w_in, 16)
            with sp.Fori(0, G) as g:
                sp.wait_ge(z_ready, g * J + J)
                sp.dma_start(group_rows(d["z2"], g), z[:, :, :]).then_inc(z_saved, 16)
            sp.wait_ge(z_saved, 16 * G + 16)

        @block.tensor
        def _(pe):
            pe.wait_ge(w_in, 3 * 16)
            with pe.Fori(0, G) as g:
                for j in range(J):
                    pe.wait_ge(agg_in[j], g * 16 + 16)
                    pe.wait_ge(agg_ready, g * J + (j + 1 + J - reuse(j, 2)))
                    to_columns(pe, c.bank[j % 2], agg[:, j, :], c.ident[:, :]).then_inc(flipped, 1)
                    pe.wait_ge(agg_ready, g * J + (j + 1 + J))
                    pe.wait_ge(added, g * J + (j + 1 + J - reuse(j, 2)))
                    for k in range(KD):
                        last = pe.matmul(c.bank[2 + j % 2][:, 0:D], agg_t[:, j, k, :], w[:, k, :],
                                         start=(k == 0), stop=(k == KD - 1))
                    last.then_inc(product, 1)
                pe.wait_ge(logits_ready, g + 1)
                for j in range(J):
                    pe.wait_ge(z_ready, g * J + (j + 1))
                    pe.wait_ge(z_cols, g * J + (j + 1 + J - reuse(j, 2)))
                    to_columns(pe, c.bank[4 + j % 2], z[:, j, :], c.ident[:, :]).then_inc(z_flipped, 1)
                    pe.wait_ge(z_cols, g * J + (j + 1 + J))
                    out = c.bank[6][:, j * 16:j * 16 + 16]
                    for k in range(KD):
                        pe.matmul(out, z_t[:, j, k, :], gate[:, k, :], start=(k == 0), stop=False)
                    pe.matmul(out, c.ones[0:1, :], gate_bias[:, :], start=False, stop=True).then_inc(gated, 1)

        @block.scalar
        def _(act):
            act.sem_inc(agg_ready, J)
            act.sem_inc(z_cols, J)
            act.sem_inc(logits_ready, 1)
            with act.Fori(0, G) as g:
                for j in range(J):
                    act.wait_ge(flipped, g * J + (j + 1))
                    act.copy(agg_t[:, j, :, :], split_columns(c.bank[j % 2])).then_inc(agg_ready, 1)
                norm.scalar(act, g)
                for j in range(J):
                    act.wait_ge(z_flipped, g * J + (j + 1))
                    act.copy(z_t[:, j, :, :], split_columns(c.bank[4 + j % 2])).then_inc(z_cols, 1)
                act.wait_ge(gated, g * J + J)
                act.copy(logits[:, bass.ds(g * J, J), :], c.bank[6][:, 0:J * 16].rearrange("p (j e) -> p j e", j=J)
                         ).then_inc(logits_ready, 1)

        @block.vector
        def _(vec):
            vec.sem_inc(added, J)
            vec.sem_inc(z_saved, 16)
            with vec.Fori(0, G) as g:
                for j in range(J):
                    vec.wait_ge(product, g * J + (j + 1))
                    vec.tensor_tensor(c.x[:, g * J + j, :], c.x[:, g * J + j, :], c.bank[2 + j % 2][:, 0:D],
                                      ALU.add).then_inc(added, 1)
                vec.wait_ge(added, g * J + 2 * J)
                norm.vector(vec, g, lambda j: c.x[:, g * J + j, :])
                vec.wait_ge(z_saved, g * 16 + 16)
                for j in range(J):
                    norm.apply(vec, z[:, j, :], c.x[:, g * J + j, :], j).then_inc(z_ready, 1)


B = 8


def places(experts):
    n = (2 * N + experts * (P - 1)) // P
    return n + -n % B


class Routes:

    def __init__(self, c, sb, experts, places):
        self.experts, self.tiles = experts, places
        self.logits = sb("logits", [P, NT, experts])
        self.weight = sb("weight", [P, 2, NT])
        self.combine = sb("combine", [P, NT, experts])
        self.read_idx = sb("read_idx", [P, places + B], U32)
        self.write_idx = sb("write_idx", [P, places + B], U32)
        self.tile_expert = sb("tile_expert", [P, places + B], I32)


def route(c, r, name, all_softmax):
    X, T = r.experts, r.tiles
    own, sb = stage(c, name)
    with own:
        top = sb("top", [P, NT, 8])
        top_i = sb("top_i", [P, NT, 8], U32)
        e_no = sb("e_no", [P, X])
        pick_f = sb("pick_f", [P, 2, NT])
        second = sb("second", [P, NT])
        total = sb("total", [P, NT])
        exps = sb("exps", [P, NT, X])
        pick = [sb(f"pick{k}", [P, X, NT]) for k in range(2)]
        both = sb("both", [P, X, NT])
        keep = sb("same_expert", [P, X, NT])
        running = sb("running", [P, X, NT])
        place = sb("place", [P, X, NT])
        tiles = sb("tiles", [P, 4, X])
        slot = sb("slot", [P, 2, NT])
        high = sb("high", [P, 2, NT])
        low = sb("low", [P, 2, NT])
        value_i = sb("value_i", [P, 2, NT], I32)
        value = sb("value", [P, 2, NT])
        up = sb("up", [P, P])
        is_low = sb("is_low", [P, 2 * NT, P])
        is_high = sb("is_high", [P, 2 * NT, T])
        spare_i = sb("spare_i", [P, T], I32)
        v = [sb(f"v{i}", [P, T]) for i in range(4)]
        at_least = sb("at_least", [P, T + B, X])
        tile_f = sb("tile_f", [P, T + B])
        step_sem, made, exp_go, exp_done, picked, ranked, hot, listed = c.sems(
            name, "step", "made", "exp_go", "exp_done", "picked", "ranked", "hot", "listed")
        block = own.enter_context(c.nc.Block())
        ranks = c.bank[0][:, 0:X * NT]
        totals = c.bank[1][:, 0:X * NT]
        inverse = c.bank[2][:, 0:T]

        def flat(ap):
            return ap[:, :, :].rearrange("p a b -> p (a b)")

        @block.gpsimd
        def _(pool):
            pool.memset(keep[:, :, :], 1.0)
            pool.iota(value_i[:, :, :], pattern=[[NP, 2], [P, NT]], base=1, channel_multiplier=1)
            pool.iota(spare_i[:, :], pattern=[[P, T]], base=2 * NP, channel_multiplier=1).then_inc(made, 1)
            pool.wait_ge(made, 1)
            pool.memset(keep[:, :, 0:1], 0.0).then_inc(made, 1)

        @block.scalar
        def _(act):
            act.wait_ge(exp_go, 1)
            act.activation(exps[:, :, :], exps[:, :, :], ACT.Exp).then_inc(exp_done, 1)

        @block.vector
        def _(vec):
            step = Chain(vec, step_sem)
            vec.tensor_copy(e_no[:, :], c.count_up[:, 0:X])
            vec.tensor_copy(up[:, :], c.count_up[:, :])
            vec.wait_ge(made, 2)
            vec.tensor_copy(value[:, :, :], value_i[:, :, :])
            for t in range(NT):
                last = vec.max(top[:, t, :], r.logits[:, t, :])
            step(last)
            for t in range(NT):
                last = vec.max_index(top_i[:, t, :], top[:, t, :], r.logits[:, t, :])
            step(last)
            vec.tensor_tensor(exps[:, :, :], r.logits[:, :, :], top[:, :, 0:1].to_broadcast([P, NT, X]),
                              ALU.subtract).then_inc(exp_go, 1)
            for k in range(2):
                last = vec.tensor_copy(pick_f[:, k, :], top_i[:, :, k])
            step(last)
            for k in range(2):
                step(vec.tensor_tensor(pick[k][:, :, :], e_no[:, :].unsqueeze(2).to_broadcast([P, X, NT]),
                                       pick_f[:, k, :].unsqueeze(1).to_broadcast([P, X, NT]), ALU.is_equal))
                step(vec.tensor_tensor(pick[k][:, :, :], pick[k][:, :, :],
                                       c.real[:, :].unsqueeze(1).to_broadcast([P, X, NT]), ALU.mult))
            vec.tensor_tensor(both[:, :, :], pick[0][:, :, :], pick[1][:, :, :], ALU.add).then_inc(picked, 1)
            vec.wait_ge(exp_done, 1)
            step(vec.tensor_tensor(place[:, :, :], pick[1][:, :, :], exps[:, :, :].rearrange("p t e -> p e t"),
                                   ALU.mult))
            step(vec.tensor_reduce(second[:, :], place[:, :, :].rearrange("p e t -> p t e"), AX.X, ALU.add))
            w = r.weight
            if all_softmax:
                step(vec.tensor_reduce(total[:, :], exps[:, :, :], AX.X, ALU.add))
                step(vec.reciprocal(total[:, :], total[:, :]))
                step(vec.tensor_tensor(second[:, :], second[:, :], total[:, :], ALU.mult))
                step(vec.tensor_tensor(w[:, 1, :], second[:, :], total[:, :], ALU.add))
                step(vec.tensor_scalar(w[:, 1, :], w[:, 1, :], 1e-12, None, ALU.max))
                step(vec.reciprocal(w[:, 1, :], w[:, 1, :]))
                step(vec.tensor_tensor(w[:, 0, :], total[:, :], w[:, 1, :], ALU.mult))
                step(vec.tensor_tensor(w[:, 1, :], second[:, :], w[:, 1, :], ALU.mult))
            else:
                step(vec.tensor_scalar(total[:, :], second[:, :], 1.0, None, ALU.add))
                step(vec.reciprocal(w[:, 0, :], total[:, :]))
                step(vec.tensor_tensor(w[:, 1, :], second[:, :], w[:, 0, :], ALU.mult))
            cp = r.combine[:, :, :].rearrange("p t e -> p e t")
            step(vec.tensor_tensor(cp, pick[0][:, :, :], w[:, 0, :].unsqueeze(1).to_broadcast([P, X, NT]), ALU.mult))
            step(vec.tensor_tensor(place[:, :, :], pick[1][:, :, :],
                                   w[:, 1, :].unsqueeze(1).to_broadcast([P, X, NT]), ALU.mult))
            step(vec.tensor_tensor(cp, cp, place[:, :, :], ALU.add))
            vec.wait_ge(ranked, 1)
            step(vec.tensor_tensor_scan(flat(running), flat(keep), totals, 0.0, ALU.mult, ALU.add))
            t = tiles
            step(vec.tensor_scalar(t[:, 0, :], running[:, :, NT - 1], (P - 1) / 2.0, 1.0 / P, ALU.add, ALU.mult))
            step(vec.tensor_scalar(t[:, 1, :], t[:, 0, :], ROUND, None, ALU.add))
            step(vec.tensor_scalar(t[:, 0, :], t[:, 1, :], -ROUND, None, ALU.add))
            step(vec.tensor_tensor_scan(t[:, 1, :], c.ones[:, 0:X], t[:, 0, :], 0.0, ALU.mult, ALU.add))
            step(vec.tensor_tensor(t[:, 2, :], t[:, 1, :], t[:, 0, :], ALU.subtract))
            step(vec.tensor_scalar(t[:, 3, :], t[:, 2, :], float(P), None, ALU.mult))
            step(vec.tensor_tensor(flat(running), flat(running), totals, ALU.subtract))
            step(vec.tensor_tensor(flat(running), flat(running), ranks, ALU.add))
            step(vec.tensor_tensor(running[:, :, :], running[:, :, :],
                                   t[:, 3, :].unsqueeze(2).to_broadcast([P, X, NT]), ALU.add))
            for k in range(2):
                step(vec.tensor_tensor(place[:, :, :], pick[k][:, :, :], running[:, :, :], ALU.mult))
                step(vec.tensor_reduce(slot[:, k, :], place[:, :, :].rearrange("p e t -> p t e"), AX.X, ALU.add))
            step(vec.tensor_scalar(high[:, :, :], slot[:, :, :], -(P - 1) / 2.0, 1.0 / P, ALU.add, ALU.mult))
            step(vec.tensor_scalar(low[:, :, :], high[:, :, :], ROUND, None, ALU.add))
            step(vec.tensor_scalar(high[:, :, :], low[:, :, :], -ROUND, None, ALU.add))
            step(vec.scalar_tensor_tensor(out=low[:, :, :], in0=high[:, :, :], scalar=-float(P), in1=slot[:, :, :],
                                          op0=ALU.mult, op1=ALU.add))
            step(vec.tensor_tensor(value[:, :, :], value[:, :, :], c.real[:, :].unsqueeze(1).to_broadcast([P, 2, NT]),
                                   ALU.mult))
            vec.tensor_tensor(is_low[:, :, :], flat(low).unsqueeze(2).to_broadcast([P, 2 * NT, P]),
                              up[:, :].unsqueeze(1).to_broadcast([P, 2 * NT, P]), ALU.is_equal)
            step(vec.tensor_tensor(is_high[:, :, :], flat(high).unsqueeze(2).to_broadcast([P, 2 * NT, T]),
                                   up[:, 0:T].unsqueeze(1).to_broadcast([P, 2 * NT, T]), ALU.is_equal))
            vec.tensor_tensor(is_high[:, :, :], is_high[:, :, :], flat(value).unsqueeze(2).to_broadcast([P, 2 * NT, T]),
                              ALU.mult).then_inc(hot, 1)
            step(vec.tensor_tensor(at_least[:, 0:T, :], up[:, 0:T].unsqueeze(2).to_broadcast([P, T, X]),
                                   t[:, 1, :].unsqueeze(1).to_broadcast([P, T, X]), ALU.is_ge))
            step(vec.memset(tile_f[:, :], 0.0))
            step(vec.tensor_reduce(tile_f[:, 0:T], at_least[:, 0:T, :], AX.X, ALU.add))
            step(vec.tensor_scalar(tile_f[:, :], tile_f[:, :], float(X - 1), None, ALU.min))
            step(vec.tensor_copy(r.tile_expert[:, :], tile_f[:, :]))
            vec.memset(r.read_idx[:, T:], 0)
            vec.memset(r.write_idx[:, T:], 2 * NP)
            vec.wait_ge(listed, 1)
            filled, place_no, is_second, spare = v
            step(vec.tensor_scalar(filled[:, :], inverse, 0.0, None, ALU.is_gt))
            step(vec.tensor_scalar(place_no[:, :], inverse, -1.0, None, ALU.add))
            step(vec.tensor_scalar(is_second[:, :], place_no[:, :], float(NP), -float(NP), ALU.is_ge, ALU.mult))
            step(vec.tensor_tensor(is_second[:, :], is_second[:, :], place_no[:, :], ALU.add))
            step(vec.tensor_tensor(is_second[:, :], is_second[:, :], filled[:, :], ALU.mult))
            step(vec.tensor_copy(r.read_idx[:, 0:T], is_second[:, :]))
            step(vec.tensor_copy(spare[:, :], spare_i[:, :]))
            step(vec.tensor_tensor(place_no[:, :], place_no[:, :], spare[:, :], ALU.subtract))
            step(vec.tensor_tensor(place_no[:, :], place_no[:, :], filled[:, :], ALU.mult))
            step(vec.tensor_tensor(place_no[:, :], place_no[:, :], spare[:, :], ALU.add))
            step(vec.tensor_copy(r.write_idx[:, 0:T], place_no[:, :]))

        @block.tensor
        def _(pe):
            pe.wait_ge(picked, 1)
            pe.matmul(ranks, c.upper[:, :], flat(both), start=True, stop=True)
            pe.matmul(totals, c.ones[:, :], flat(both), start=True, stop=True).then_inc(ranked, 1)
            pe.wait_ge(hot, 1)
            for n in range(2 * NT):
                last = pe.matmul(inverse, is_low[:, n, :], is_high[:, n, :], start=(n == 0), stop=(n == 2 * NT - 1))
            last.then_inc(listed, 1)


def experts(c, r, name, table, w1, b1, w2, act_func):
    X, T = r.experts, r.tiles
    F = w1.shape[2]
    KF = F // P
    assert T % B == 0
    own, sb = stage(c, name)
    with own:
        rows = sb("rows", [P, B, D])
        cols = sb("cols", [P, 2, KD, P])
        up_w = sb("up_w", [P, 2, KD, F])
        up_b = sb("up_b", [P, 2, KF])
        down_w = sb("down_w", [P, 2, KF, D])
        hidden = sb("hidden", [P, 2, KF, P])
        result = sb("result", [P, B, D])
        idx = sb("idx", [P, 2, B], U32)
        first_sent = sb("first_sent", [1, B])
        arrived = c.sems(name, *(f"arrived{q}" for q in range(B)))
        sent = c.sems(name, *(f"sent{q}" for q in range(B)))
        up_in = c.sems(name, "up_in0", "up_in1")
        up_b_in = c.sems(name, "up_b_in0", "up_b_in1")
        down_in = c.sems(name, "down_in0", "down_in1")
        staged, go, flipped, cols_ready, up, hidden_ready, down, result_ready = c.sems(
            name, "staged", "go", "flipped", "cols_ready", "up", "hidden_ready", "down", "result_ready")
        passed = c.sem(f"{name}_passed")
        block = own.enter_context(c.nc.Block())
        out = c.dram["expert_out"]
        turns = T // B
        table_w1 = w1.rearrange("e (k p) f -> e p k f", p=P)
        table_w2 = w2.rearrange("e (k p) d -> e p k d", p=P)

        @block.gpsimd
        def _(pool):
            def gather(q):
                pool.indirect_dma_start(rows[:, q, :], None, table[:, :],
                                        bass.IndirectOffsetOnAxis(idx[:, 0, q:q + 1], 0)).then_inc(arrived[q], 16)

            for q in range(B):
                pool.dma_start(first_sent[0:1, q:q + 1], c.eps[0:1, 0:1]).then_inc(sent[q], 16)
            pool.tensor_copy(idx[:, 0, :], r.read_idx[:, 0:B]).then_inc(staged, 1)
            pool.wait_ge(staged, 1)
            for q in range(B):
                gather(q)
            with pool.Fori(0, turns) as i:
                for q in range(B):
                    pool.wait_ge(arrived[q], i * 16 + 16)
                    pool.wait_ge(sent[q], i * 16 + 16)
                pool.sem_inc(go, 1)
                pool.tensor_copy(idx[:, 0, :], r.read_idx[:, bass.ds(i * B + B, B)])
                pool.tensor_copy(idx[:, 1, :], r.write_idx[:, bass.ds(i * B, B)]).then_inc(staged, 1)
                pool.wait_ge(staged, i + 2)
                for q in range(B):
                    pool.wait_ge(flipped, i * B + (q + 1))
                    pool.sem_inc(go, 1)
                    gather(q)
                    pool.wait_ge(result_ready, i * B + (q + 3))
                    pool.sem_inc(go, 1)
                    pool.indirect_dma_start(out[:, :], bass.IndirectOffsetOnAxis(idx[:, 1, q:q + 1], 0),
                                            result[:, q, :], None).then_inc(sent[q], 16)
            for q in range(B):
                pool.wait_ge(sent[q], turns * 16 + 16)
                pool.wait_ge(arrived[q], turns * 16 + 16)

        @block.sync
        def _(sp):
            def load(n, i, q):
                e = sp.value_load(r.tile_expert[0:1, bass.ds(n, 1)], min_val=0, max_val=X - 1)
                b = q % 2
                if i is not None:
                    sp.wait_ge(up, i * B + (q + 1))
                sp.dma_start(up_w[:, b, :, :], table_w1[e]).then_inc(up_in[b], 16)
                if i is not None:
                    sp.wait_ge(hidden_ready, i * B + (q + 2))
                sp.dma_start(up_b[:, b, :], b1[e]).then_inc(up_b_in[b], 16)
                if i is not None:
                    sp.wait_ge(down, i * B + (q + 2))
                sp.dma_start(down_w[:, b, :, :], table_w2[e]).then_inc(down_in[b], 16)

            load(0, None, 0)
            load(1, None, 1)
            with sp.Fori(0, turns) as i:
                for q in range(B):
                    load(i * B + (q + 2), i, q)
            for b in range(2):
                for weights in (up_in[b], up_b_in[b], down_in[b]):
                    sp.wait_ge(weights, 16 * (T // 2 + 1))

        @block.tensor
        def _(pe):
            def flip(q, arrivals, copies):
                pe.wait_ge(arrived[q % B], arrivals)
                if copies is not None:
                    pe.wait_ge(cols_ready, copies)
                to_columns(pe, c.bank[q % 2], rows[:, q % B, :], c.ident[:, :]).then_inc(flipped, 1)

            def first(q, n, weights):
                b = q % 2
                pe.wait_ge(up_in[b], weights)
                pe.wait_ge(cols_ready, n + 1)
                if not (isinstance(n, int) and n == 0):
                    pe.wait_ge(hidden_ready, n)
                for f in range(KF):
                    for k in range(KD):
                        last = pe.matmul(c.bank[2 + b][:, f * P:f * P + P], up_w[:, b, k, f * P:f * P + P],
                                         cols[:, b, k, :], start=(k == 0), stop=(k == KD - 1))
                last.then_inc(up, 1)

            flip(0, 16, None)
            flip(1, 16, None)
            first(0, 0, 16)
            with pe.Fori(0, turns) as i:
                for q in range(B):
                    b = q % 2
                    flip(q + 2, i * 16 + (32 if q + 2 >= B else 16), i * B + (q + 1))
                    first(q + 1, i * B + (q + 1), i * (8 * B) + 16 * ((q + 1) // 2 + 1))
                    pe.wait_ge(down_in[b], i * (8 * B) + 16 * (q // 2 + 1))
                    pe.wait_ge(hidden_ready, i * B + (q + 2))
                    pe.wait_ge(result_ready, i * B + (q + 1))
                    for f in range(KF):
                        last = pe.matmul(c.bank[4 + b][:, 0:D], hidden[:, b, f, :], down_w[:, b, f, :],
                                         start=(f == 0), stop=(f == KF - 1))
                    last.then_inc(down, 1)

        @block.scalar
        def _(act):
            def unit(q, n, biases):
                b = q % 2
                act.wait_ge(up_b_in[b], biases)
                act.wait_ge(up, n + 1)
                if not (isinstance(n, int) and n == 0):
                    act.wait_ge(down, n)
                    act.sem_inc(passed, 1)
                for f in range(KF):
                    last = act.activation(hidden[:, b, f, :], c.bank[2 + b][:, f * P:f * P + P], act_func,
                                          bias=up_b[:, b, f:f + 1])
                last.then_inc(hidden_ready, 1)

            act.sem_inc(hidden_ready, 1)
            unit(0, 0, 16)
            with act.Fori(0, turns) as i:
                for q in range(B):
                    unit(q + 1, i * B + (q + 1), i * (8 * B) + 16 * ((q + 1) // 2 + 1))

        @block.vector
        def _(vec):
            vec.sem_inc(down, 1)
            vec.sem_inc(result_ready, 2)
            for q in range(2):
                vec.wait_ge(flipped, q + 1)
                vec.tensor_copy(cols[:, q, :, :], split_columns(c.bank[q])).then_inc(cols_ready, 1)
            with vec.Fori(0, turns) as i:
                for q in range(B):
                    b = q % 2
                    vec.wait_ge(flipped, i * B + (q + 3))
                    vec.wait_ge(up, i * B + (q + 1))
                    vec.tensor_copy(cols[:, b, :, :], split_columns(c.bank[b])).then_inc(cols_ready, 1)
                    vec.wait_ge(sent[q], i * 16 + 16)
                    vec.wait_ge(down, i * B + (q + 2))
                    vec.tensor_copy(result[:, q, :], c.bank[4 + b][:, 0:D]).then_inc(result_ready, 1)


class ExpertSum:

    def __init__(self, c, r, sb, name, table, bias):
        self.c, self.r, self.table, self.bias_table = c, r, table, bias
        X = r.experts
        self.z = sb("z_in", [P, J, D])
        self.y = sb("y_in", [P, 2, J, D])
        self.shares = sb("shares", [P, J, X])
        self.shares_t = sb("shares_t", [X, J, P])
        self.bias = sb("expert_bias", [X, D])
        self.total = sb("total", [P, J, D])
        (self.bias_in, self.rows_in, self.used, self.shares_ready, self.flipped, self.shares_t_ready,
         self.product, self.step, self.summed) = c.sems(
            name, "bias_in", "rows_in", "rows_used", "shares_ready", "shares_flipped", "shares_t_ready",
            "bias_product", "sum_step", "summed")

    def sync(self, sp, g):
        sp.wait_ge(self.used, g * J + 1)
        sp.dma_start(self.z[:, :, :], group_rows(self.table, g)).then_inc(self.rows_in, 16)
        for k in range(2):
            half = self.c.dram["expert_out"][k * NP:k * NP + NP, :]
            sp.dma_start(self.y[:, k, :, :], group_rows(half, g)).then_inc(self.rows_in, 16)

    def sync_first(self, sp):
        sp.dma_start(self.bias[:, :], self.bias_table).then_inc(self.bias_in, 16)

    def pool(self, pool, g):
        pool.wait_ge(self.flipped, g * J + 1)
        pool.sem_inc(self.step, 1)
        pool.tensor_copy(self.shares[:, :, :], self.r.combine[:, bass.ds(g * J, J), :]).then_inc(self.shares_ready, 1)

    def tensor(self, pe, g, banks):
        c, X = self.c, self.r.experts
        pe.wait_ge(self.shares_ready, g + 1)
        pe.wait_ge(self.shares_t_ready, g + 1)
        for j in range(J):
            pe.transpose(c.bank[banks[0]][0:X, (j % 4) * P:(j % 4) * P + P] if j < 4 else
                         c.bank[banks[3]][0:X, 0:P], self.shares[:, j, :], c.ident[:, :]).then_inc(self.flipped, 1)
        pe.wait_ge(self.shares_t_ready, g + 2)
        for j in range(J):
            pe.wait_ge(self.summed, g * J + (j + 1 + J - reuse(j, 2)))
            pe.matmul(c.bank[banks[1 + j % 2]][:, D:2 * D], self.shares_t[:, j, :], self.bias[:, :], start=True,
                      stop=True).then_inc(self.product, 1)

    def scalar(self, act, g, banks):
        c, X = self.c, self.r.experts
        act.wait_ge(self.flipped, g * J + J + 1)
        act.wait_ge(self.product, g * J + 1)
        act.copy(self.shares_t[:, 0:4, :], c.bank[banks[0]][0:X, :].rearrange("p (j n) -> p j n", j=4))
        act.copy(self.shares_t[:, 4, :], c.bank[banks[3]][0:X, 0:P]).then_inc(self.shares_t_ready, 1)

    def open(self, eng):
        eng.sem_inc(self.used, 1)
        eng.sem_inc(self.flipped, 1)
        eng.sem_inc(self.shares_t_ready, 1)
        eng.sem_inc(self.summed, J)
        eng.sem_inc(self.product, 1)

    STEPS = 2 * J

    def vector(self, vec, g, chain_sem, banks):
        c, w = self.c, self.r.weight
        vec.wait_ge(self.rows_in, g * 48 + 48)
        for k in range(2):
            for j in range(J):
                vec.scalar_tensor_tensor(out=self.total[:, j, :], in0=self.y[:, k, j, :],
                                         scalar=w[:, k, bass.ds(g * J + j, 1)],
                                         in1=self.z[:, j, :] if k == 0 else self.total[:, j, :],
                                         op0=ALU.mult, op1=ALU.add).then_inc(chain_sem if k == 0 else self.used, 1)
            if k == 0:
                vec.wait_ge(chain_sem, g * J + J)
        vec.wait_ge(self.used, g * J + J + 1)
        for j in range(J):
            vec.wait_ge(self.product, g * J + (j + 2))
            vec.tensor_tensor(self.total[:, j, :], self.total[:, j, :], c.bank[banks[1 + j % 2]][:, D:2 * D],
                              ALU.add).then_inc(self.summed, 1)
        vec.wait_ge(self.summed, g * J + 2 * J)


def finish_layer0(c, r):
    own, sb = stage(c, "finish0")
    with own:
        d = c.dram
        es = ExpertSum(c, r, sb, "sum0", d["z2"], d["L0_ffn_b2"])
        norm_a, norm_b = Norm(c, sb, "finish0a"), Norm(c, sb, "finish0b")
        gamma = sb("gamma", [P, D])
        beta = sb("beta", [P, D])
        w = sb("w", [P, KD, D])
        b = sb("b", [1, D])
        y = sb("y", [P, J, D])
        xb = sb("x_beta", [P, J, D])
        z = sb("z", [P, J, D])
        zt = sb("z_cols", [P, KD, GW])
        h = sb("h", [P, J, D])
        (w_in, y_ready, xb_ready, y_used, x_ready, z_ready, flipped, zt_ready, zt_saved, product, h_ready,
         h_saved, step) = c.sems(
            "finish0", "w_in", "y_ready", "xb_ready", "y_used", "x_ready", "z_ready", "flipped", "zt_ready",
            "zt_saved", "product", "h_ready", "h_saved", "step")
        passed = [c.sem(f"finish0_passed{i}") for i in range(3)]
        banks = (0, 1, 2, 3)
        block = own.enter_context(c.nc.Block())

        @block.sync
        def _(sp):
            es.sync_first(sp)
            sp.dma_start(w[:, :, :], chunked(d["w_p1_t"])).then_inc(w_in, 16)
            sp.dma_start(b[:, :], one_row(d["L1_gnn_bp1"])).then_inc(w_in, 16)
            sp.dma_start(gamma[:, :], all_rows(d["L0_ffn_gamma"])).then_inc(w_in, 16)
            sp.dma_start(beta[:, :], all_rows(d["L0_ffn_beta"])).then_inc(w_in, 16)
            es.sync(sp, 0)
            with sp.Fori(0, G - 1) as g:
                es.sync(sp, g + 1)
                sp.wait_ge(zt_ready, g * J + 2 * J)
                sp.dma_start(d["z3_cols"][:, :, bass.ds(g * GW, GW)], zt[:, :, :]).then_inc(zt_saved, 16)
                sp.wait_ge(h_ready, g * J + 2 * J)
                sp.dma_start(group_rows(d["h"], g), h[:, :, :]).then_inc(h_saved, 16)
            sp.wait_ge(zt_ready, G * J + J)
            sp.dma_start(d["z3_cols"][:, :, NP - GW:], zt[:, :, :]).then_inc(zt_saved, 16)
            sp.wait_ge(h_ready, G * J + J)
            sp.dma_start(group_rows(d["h"], G - 1), h[:, :, :]).then_inc(h_saved, 16)
            sp.wait_ge(zt_saved, 16 * G + 16)
            sp.wait_ge(h_saved, 16 * G + 16)

        @block.gpsimd
        def _(pool):
            pool.wait_ge(w_in, 4 * 16)
            with pool.Fori(0, G) as g:
                es.pool(pool, g)
                pool.wait_ge(x_ready, g + 1)
                pool.sem_inc(passed[0], 1)
                pool.tensor_tensor(xb[:, :, :], c.x[:, bass.ds(g * J, J), :],
                                   beta[:, :].unsqueeze(1).to_broadcast([P, J, D]), ALU.add).then_inc(xb_ready, 1)

        @block.tensor
        def _(pe):
            pe.wait_ge(w_in, 4 * 16)
            pe.wait_ge(es.bias_in, 16)
            es.open(pe)
            with pe.Fori(0, G) as g:
                es.tensor(pe, g, banks)

                def flip(j):
                    pe.wait_ge(z_ready, g * J + (j + 1))
                    pe.wait_ge(zt_ready, g * J + (j + 1 + J - reuse(j, 2)))
                    to_columns(pe, c.bank[4 + j % 2], z[:, j, :], c.ident[:, :]).then_inc(flipped, 1)

                flip(0)
                for j in range(J):
                    if j + 1 < J:
                        flip(j + 1)
                    pe.wait_ge(zt_ready, g * J + (j + 1 + J))
                    pe.wait_ge(h_ready, g * J + (j + 1 + J - reuse(j, 2)))
                    out = c.bank[6 + j % 2][:, 0:D]
                    for k in range(KD):
                        pe.matmul(out, zt[:, k, j * P:j * P + P], w[:, k, :], start=(k == 0), stop=False)
                    pe.matmul(out, c.ones[0:1, :], b[:, :], start=False, stop=True).then_inc(product, 1)

        @block.scalar
        def _(act):
            act.sem_inc(zt_ready, J)
            act.sem_inc(h_ready, J)
            act.sem_inc(zt_saved, 16)
            act.sem_inc(h_saved, 16)
            with act.Fori(0, G) as g:
                es.scalar(act, g, banks)
                norm_a.scalar(act, g)
                act.wait_ge(norm_a.step, g * Norm.STEPS + Norm.STEPS)
                for j in range(J):
                    act.activation(y[:, j, :], es.total[:, j, :], ACT.Identity, bias=norm_a.shift[:, j:j + 1],
                                   scale=norm_a.rstd[:, j:j + 1]).then_inc(y_ready, 1)
                norm_b.scalar(act, g)
                act.wait_ge(norm_b.step, g * Norm.STEPS + Norm.STEPS)
                for j in range(J):
                    act.activation(z[:, j, :], c.x[:, g * J + j, :], ACT.Identity, bias=norm_b.shift[:, j:j + 1],
                                   scale=norm_b.rstd[:, j:j + 1]).then_inc(z_ready, 1)
                act.wait_ge(zt_saved, g * 16 + 16)
                act.wait_ge(h_saved, g * 16 + 16)

                def columns_of(j):
                    act.wait_ge(flipped, g * J + (j + 1))
                    act.copy(zt[:, :, j * P:j * P + P], split_columns(c.bank[4 + j % 2])).then_inc(zt_ready, 1)

                columns_of(0)
                for j in range(J):
                    if j + 1 < J:
                        columns_of(j + 1)
                    act.wait_ge(product, g * J + (j + 1))
                    act.activation(h[:, j, :], c.bank[6 + j % 2][:, 0:D], ACT.Relu).then_inc(h_ready, 1)

        @block.vector
        def _(vec):
            vec.wait_ge(w_in, 4 * 16)
            vec.sem_inc(x_ready, 1)
            with vec.Fori(0, G) as g:
                es.vector(vec, g, step, banks)
                norm_a.vector(vec, g, lambda j: es.total[:, j, :])
                vec.wait_ge(y_ready, g * J + J)
                vec.tensor_tensor(y[:, :, :], y[:, :, :], gamma[:, :].unsqueeze(1).to_broadcast([P, J, D]),
                                  ALU.mult).then_inc(y_used, 1)
                vec.wait_ge(y_used, g + 1)
                vec.wait_ge(xb_ready, g + 1)
                vec.tensor_tensor(c.x[:, bass.ds(g * J, J), :], y[:, :, :], xb[:, :, :], ALU.add
                                  ).then_inc(x_ready, 1)
                vec.wait_ge(x_ready, g + 2)
                norm_b.vector(vec, g, lambda j: c.x[:, g * J + j, :])


class KeyValue1(Work):

    W = P + PER1

    def __init__(self, c):
        self.c = c

    def buffers(self, sb):
        c = self.c
        self.cols = Columns(c, sb, "mix1", c.dram["z3_cols"])
        self.w = sb("w_kv", [P, KD, 2 * D])
        self.bias = sb("b_kv", [P, 2 * D])
        self.raw = sb("kv_raw", [P, 2, 2 * D])
        self.low = sb("k_low", [P, 2, D])
        self.key = sb("key", [P, 2, D])
        self.value = sb("value", [P, 2, KD, P + 1])
        self.zero = sb("zeros", [P, KD * (P + 1)])
        self.map = sb("map", [P, KD, self.W])
        self.sums = c.bank[2][:, 0:KD * (P + 1)]
        (self.w_in, self.made, self.product, self.rows, self.low_ready, self.exp_ready, self.key_ready,
         self.value_ready, self.used, self.closed, self.map_ready, self.step) = c.sems(
            "kv1", "w_in", "made", "product", "rows", "low_ready", "exp_ready", "key_ready", "value_ready", "used",
            "closed", "map_ready", "step")

    def first(self, eng, which):
        c, d = self.c, self.c.dram
        if which == "sync":
            eng.dma_start(self.w[:, :, 0:D], chunked(d["L1_mix_wk"])).then_inc(self.w_in, 16)
            eng.dma_start(self.w[:, :, D:], chunked(d["L1_mix_wv"])).then_inc(self.w_in, 16)
            eng.dma_start(self.bias[:, 0:D], all_rows(d["L1_mix_bk"])).then_inc(self.w_in, 16)
            eng.dma_start(self.bias[:, D:], all_rows(d["L1_mix_bv"])).then_inc(self.w_in, 16)
        if which == "vector":
            eng.memset(self.map[:, :, :], 0.0)
            eng.memset(self.zero[:, :], 0.0).then_inc(self.made, 1)
            eng.wait_ge(self.w_in, 4 * 16)
            eng.sem_inc(self.rows, J)
        if which == "scalar":
            eng.sem_inc(self.value_ready, J)
        if which == "tensor":
            self.cols.open(eng)
            eng.wait_ge(self.w_in, 4 * 16)
            eng.wait_ge(self.made, 1)
            eng.matmul(self.sums, self.zero[:, 0:P], self.zero[:, :], start=True, stop=False,
                       skip_group_check=True)
            eng.sem_inc(self.used, J)

    def turn(self, eng, which, g):
        c = self.c
        if which == "sync":
            self.cols.load(eng, g, 0)
        if which == "tensor":
            self.cols.wait(eng, g, 0)

            def product(j):
                eng.wait_ge(self.rows, g * J + (j + 1 + J - reuse(j, 2)))
                for k in range(KD):
                    last = eng.matmul(c.bank[j % 2][:, :], self.cols.buf[:, k, j * P:j * P + P],
                                      self.w[:, k, :], start=(k == 0), stop=(k == KD - 1))
                last.then_inc(self.product, 1)

            product(0)
            for j in range(J):
                if j + 1 < J:
                    product(j + 1)
                eng.wait_ge(self.key_ready, g * J + (j + 1))
                eng.wait_ge(self.value_ready, g * J + (j + 1 + J))
                for k in range(KD):
                    last = eng.matmul(self.sums[:, k * (P + 1):(k + 1) * (P + 1)], self.key[:, j % 2, k * P:k * P + P],
                                      self.value[:, j % 2, k, :], start=False, stop=False, skip_group_check=True)
                last.then_inc(self.used, 1)
            eng.wait_ge(self.product, g * J + J)
            eng.sem_inc(self.cols.free, 1)
        if which == "vector1":
            for j in range(J):
                s = j % 2
                eng.wait_ge(self.product, g * J + (j + 1))
                eng.wait_ge(self.used, g * J + (j + 1 + J - reuse(j, 2)))
                eng.tensor_tensor(self.raw[:, s, :], c.bank[s][:, :], self.bias[:, :], ALU.add).then_inc(self.rows, 1)
                eng.wait_ge(self.rows, g * J + (j + 1 + J))
                eng.tensor_scalar(self.low[:, s, :], self.raw[:, s, 0:D], 0.0, None, ALU.min
                                  ).then_inc(self.low_ready, 1)
                eng.wait_ge(self.exp_ready, g * J + (j + 1))
                eng.scalar_tensor_tensor(out=self.key[:, s, :], in0=self.raw[:, s, 0:D], scalar=0.0,
                                         in1=self.low[:, s, :], op0=ALU.max, op1=ALU.add).then_inc(self.key_ready, 1)
        if which == "scalar":
            for j in range(J):
                s = j % 2
                eng.wait_ge(self.low_ready, g * J + (j + 1))
                eng.activation(self.low[:, s, :], self.low[:, s, :], ACT.Exp).then_inc(self.exp_ready, 1)
                real = c.real[:, bass.ds(g * J + j, 1)]
                eng.activation(self.value[:, s, :, 0:P], self.raw[:, s, D:].rearrange("p (k n) -> p k n", k=KD),
                               ACT.Copy, scale=real)
                for k in range(KD):
                    last = eng.copy(self.value[:, s, k, P:P + 1], real)
                last.then_inc(self.value_ready, 1)

    def after(self, eng, which):
        if which == "tensor":
            eng.matmul(self.sums, self.zero[:, 0:P], self.zero[:, :], start=False, stop=True,
                       skip_group_check=True).then_inc(self.closed, 1)
        if which == "vector":
            eng.wait_ge(self.closed, 1)
            for k in range(KD):
                for h in range(PER1):
                    part = slice(h * HEAD1, (h + 1) * HEAD1)
                    at = k * (P + 1)
                    eng.tensor_copy(self.map[part, k, part], self.sums[part, at + h * HEAD1:at + (h + 1) * HEAD1])
                    last = eng.tensor_copy(self.map[part, k, P + h:P + h + 1], self.sums[part, at + P:at + P + 1])
            last.then_inc(self.map_ready, 1)


class Mixed1(Work):

    def __init__(self, c, kv):
        self.c, self.kv = c, kv

    def buffers(self, sb):
        c = self.c
        self.wq = sb("w_q", [P, KD, D])
        self.bq = sb("b_q", [P, KD])
        self.wo = sb("w_o", [P, KD, D])
        self.bo = sb("b_o", [1, D])
        self.q = sb("q", [P, KD, GW])
        self.low = sb("q_low", [P, 2, HALF])
        self.inv = sb("inv", [P, J, 2 * PER1])
        self.heads = sb("heads", [P, J, D])
        self.heads_t = sb("heads_t", [P, 2, KD, P])
        (self.w_in, self.query, self.low_ready, self.exp_ready, self.relu_ready, self.q_ready, self.spread,
         self.inverse, self.heads_ready, self.flipped, self.heads_t_ready, self.product, self.added,
         self.step) = c.sems(
            "mixed1", "w_in", "query", "low_ready", "exp_ready", "relu_ready", "q_ready", "spread", "inverse",
            "heads_ready", "flipped", "heads_t_ready", "product", "added", "step")

    def first(self, eng, which):
        c, d = self.c, self.c.dram
        if which == "sync":
            eng.dma_start(self.wq[:, :, :], chunked(d["L1_mix_wq"])).then_inc(self.w_in, 16)
            eng.dma_start(self.wo[:, :, :], chunked(d["L1_mix_wo"])).then_inc(self.w_in, 16)
            eng.dma_start(self.bo[:, :], one_row(d["L1_mix_bo"])).then_inc(self.w_in, 16)
            with c.nc.allow_non_contiguous_dma(reason="a bias as columns"):
                eng.dma_start(self.bq[:, :], columns(d["L1_mix_bq"])).then_inc(self.w_in, 16)

    def before(self, eng, which):
        eng.wait_ge(self.w_in, 4 * 16)
        if which == "tensor":
            eng.wait_ge(self.kv.map_ready, 1)
            eng.sem_inc(self.spread, 1)
        if which == "vector":
            eng.sem_inc(self.q_ready, 2)
            eng.sem_inc(self.heads_ready, J)
            eng.sem_inc(self.added, J)
        if which == "scalar":
            eng.sem_inc(self.heads_t_ready, J)

    def turn(self, eng, which, g):
        c, kv = self.c, self.kv
        parts = [(m, half) for half in range(2) for m in range(KD)]
        if which == "sync":
            kv.cols.load(eng, g, G)
        if which == "tensor":
            kv.cols.wait(eng, g, G)
            for n, (m, half) in enumerate(parts):
                eng.wait_ge(self.q_ready, g * 4 + (n + 1))
                for k in range(KD):
                    last = eng.matmul(c.bank[n % 2][:, 0:HALF], self.wq[:, k, m * P:m * P + P],
                                      kv.cols.buf[:, k, half * HALF:half * HALF + HALF], start=(k == 0),
                                      stop=(k == KD - 1))
                last.then_inc(self.query, 1)
            eng.wait_ge(self.q_ready, g * 4 + 6)
            eng.sem_inc(kv.cols.free, 1)
            for j in range(J):
                eng.wait_ge(self.heads_ready, g * J + (j + 1 + J - reuse(j, 2)))
                for k in range(KD):
                    last = eng.matmul(c.bank[3 + j % 2][:, k * kv.W:(k + 1) * kv.W], self.q[:, k, j * P:j * P + P],
                                      kv.map[:, k, :], start=True, stop=True)
                last.then_inc(self.spread, 1)
            for j in range(J):
                eng.wait_ge(self.heads_ready, g * J + (j + 1 + J))
                eng.wait_ge(self.heads_t_ready, g * J + (j + 1 + J - reuse(j, 2)))
                to_columns(eng, c.bank[5 + j % 2], self.heads[:, j, :], c.ident[:, :]).then_inc(self.flipped, 1)
                eng.wait_ge(self.heads_t_ready, g * J + (j + 1 + J))
                eng.wait_ge(self.added, g * J + (j + 1 + J - 1))
                out = c.bank[7][:, 0:D]
                for k in range(KD):
                    eng.matmul(out, self.heads_t[:, j % 2, k, :], self.wo[:, k, :], start=(k == 0), stop=False)
                eng.matmul(out, c.ones[0:1, :], self.bo[:, :], start=False, stop=True).then_inc(self.product, 1)
        if which == "scalar":
            for n, (m, half) in enumerate(parts):
                eng.wait_ge(self.low_ready, g * 4 + (n + 1))
                eng.activation(self.low[:, n % 2, :], self.low[:, n % 2, :], ACT.Exp).then_inc(self.exp_ready, 1)
                if n == 0:
                    eng.wait_ge(self.spread, g * J + 1)
                eng.activation(self.q[:, m, half * HALF:half * HALF + HALF], c.bank[n % 2][:, 0:HALF], ACT.Relu,
                               bias=self.bq[:, m:m + 1]).then_inc(self.relu_ready, 1)
            for j in range(J):
                eng.wait_ge(self.flipped, g * J + (j + 1))
                eng.copy(self.heads_t[:, j % 2, :, :], split_columns(c.bank[5 + j % 2])
                         ).then_inc(self.heads_t_ready, 1)
        if which == "vector0":
            for n, (m, half) in enumerate(parts):
                eng.wait_ge(self.query, g * 4 + (n + 1))
                eng.tensor_scalar(self.low[:, n % 2, :], c.bank[n % 2][:, 0:HALF], self.bq[:, m:m + 1], 0.0,
                                  ALU.add, ALU.min).then_inc(self.low_ready, 1)
                eng.wait_ge(self.exp_ready, g * 4 + (n + 1))
                eng.wait_ge(self.relu_ready, g * 4 + (n + 1))
                part = self.q[:, m, half * HALF:half * HALF + HALF]
                eng.tensor_tensor(part, part, self.low[:, n % 2, :], ALU.add).then_inc(self.q_ready, 1)
        if which == "vector1":
            for j in range(J):
                eng.wait_ge(self.spread, g * J + (j + 2))
                bank = c.bank[3 + j % 2][:, 0:KD * kv.W].rearrange("p (k w) -> p k w", k=KD)
                inv = self.inv[:, j, :].rearrange("p (k h) -> p k h", k=KD)
                eng.tensor_scalar(inv, bank[:, :, P:], 1e-6, None, ALU.add).then_inc(self.inverse, 1)
                eng.wait_ge(self.inverse, g * 2 * J + (2 * j + 1))
                eng.reciprocal(inv, inv).then_inc(self.inverse, 1)
                eng.wait_ge(self.inverse, g * 2 * J + (2 * j + 2))
                for k in range(KD):
                    last = eng.tensor_tensor(
                        self.heads[:, j, k * P:k * P + P].rearrange("p (h e) -> p h e", h=PER1),
                        bank[:, k, 0:P].rearrange("p (h e) -> p h e", h=PER1),
                        inv[:, k, :].unsqueeze(2).to_broadcast([P, PER1, HEAD1]), ALU.mult)
                last.then_inc(self.heads_ready, 1)
            for j in range(J):
                eng.wait_ge(self.product, g * J + (j + 1))
                eng.tensor_tensor(c.x[:, g * J + j, :], c.x[:, g * J + j, :], c.bank[7][:, 0:D], ALU.add
                                  ).then_inc(self.added, 1)


def update(c, name, rows_cols, w, b, ln=None, out_rows=None, out_cols=None, last=None):
    own, sb = stage(c, name)
    with own:
        d = c.dram
        pooled = sb("pooled", [P, J, D])
        ins = sb("ins", [P, 2, KD, GW])
        weight = sb("w", [P, 2 * KD, D])
        bias = sb("b", [P, KD])
        yt = sb("y_cols", [P, KD, GW])
        y = sb("y", [P, J, D])
        norm = Norm(c, sb, name) if ln else None
        gain = sb("gain", [P, D])
        offset = sb("offset", [P, D])
        pooled_in = c.sems(name, *(f"pooled_in{j}" for j in range(J)))
        (w_in, flipped, pooled_t, ins_in, ins_free, product, sum_ready, yt_saved, back, y_ready,
         y_saved, out_ready, relu_done) = c.sems(
            name, "w_in", "flipped", "pooled_t", "ins_in", "ins_free", "product", "sum_ready",
            "yt_saved", "back", "y_ready", "y_saved", "out_ready", "relu_done")
        if ln:
            out = sb("out", [P, J, D])
            out_t = sb("out_cols", [P, KD, GW])
            out_flipped, out_t_ready, out_t_saved, gain_steps = c.sems(
                name, "out_flipped", "out_t_ready", "out_t_saved", "gain_steps")
        if last:
            norm_x = Norm(c, sb, name + "x")
            gate = sb("gate", [P, KD, last.experts])
            x_ready, gated, logits_ready, z_ready = c.sems(name, "x_ready", "gated", "logits_ready", "z_ready")
        ways = 1 if last else 2
        n_in = 2 + (2 if ln else 0) + (1 if last else 0)
        block = own.enter_context(c.nc.Block())
        parts = [(m, half) for half in range(2) for m in range(KD)]

        @block.gpsimd
        def _(pool):
            fetch_nodes(c, pool, pooled, flipped, pooled_in)

        @block.sync
        def _(sp):
            sp.dma_start(weight[:, :, :], chunked(w)).then_inc(w_in, 16)
            with c.nc.allow_non_contiguous_dma(reason="a bias as columns"):
                sp.dma_start(bias[:, :], columns(b)).then_inc(w_in, 16)
            if ln:
                sp.dma_start(gain[:, :], all_rows(ln[0])).then_inc(w_in, 16)
                sp.dma_start(offset[:, :], all_rows(ln[1])).then_inc(w_in, 16)
            if last:
                sp.dma_start(gate[:, :, :], chunked(d["router_w_t"])).then_inc(w_in, 16)

            def load(g):
                sp.wait_ge(ins_free, g + 1)
                sp.dma_start(ins[:, 0, :, :], rows_cols[:, :, bass.ds(g * GW, GW)]).then_inc(ins_in, 16)

            def save(g):
                if not ln:
                    sp.wait_ge(relu_done, g * 4 + 6)
                    sp.dma_start(out_cols[:, :, bass.ds(g * GW, GW)], yt[:, :, :]).then_inc(yt_saved, 16)
                    sp.wait_ge(y_ready, g * J + 2 * J)
                    sp.dma_start(group_rows(out_rows, g), y[:, :, :]).then_inc(y_saved, 16)
                else:
                    sp.wait_ge(z_ready if last else out_ready, g * J + J if last else g + 1)
                    sp.dma_start(group_rows(out_rows, g), out[:, :, :]).then_inc(y_saved, 16)
                    if not last:
                        sp.wait_ge(out_t_ready, g * J + 2 * J)
                        sp.dma_start(out_cols[:, :, bass.ds(g * GW, GW)], out_t[:, :, :]).then_inc(out_t_saved, 16)

            load(0)
            with sp.Fori(0, G - 1) as g:
                load(g + 1)
                save(g)
            save(G - 1)
            sp.wait_ge(y_saved, 16 * G + 16)
            if not ln:
                sp.wait_ge(yt_saved, 16 * G + 16)
            elif not last:
                sp.wait_ge(out_t_saved, 16 * G + 16)

        @block.tensor
        def _(pe):
            pe.wait_ge(w_in, n_in * 16)
            with pe.Fori(0, G) as g:
                for j in range(J):
                    pe.wait_ge(pooled_in[j], g * 16 + 16)
                    pe.wait_ge(pooled_t, g * J + (j + 1 + J - reuse(j, ways)))
                    to_columns(pe, c.bank[j % ways], pooled[:, j, :], c.ident[:, :]).then_inc(flipped, 1)
                pe.wait_ge(pooled_t, g * J + 2 * J)
                pe.wait_ge(ins_in, g * 16 + 16)
                for n, (m, half) in enumerate(parts):
                    pe.wait_ge(relu_done, g * 4 + (n + 1))
                    for k in range(2 * KD):
                        prod = pe.matmul(c.bank[2 + n % 2][:, 0:HALF], weight[:, k, m * P:m * P + P],
                                         ins[:, k // KD, k % KD, half * HALF:half * HALF + HALF],
                                         start=(k == 0), stop=(k == 2 * KD - 1))
                    prod.then_inc(product, 1)
                if ln:
                    pe.wait_ge(sum_ready, g + 1)
                else:
                    pe.wait_ge(relu_done, g * 4 + 6)
                    pe.sem_inc(ins_free, 1)
                for j in range(J):
                    pe.wait_ge(y_ready, g * J + (j + 1 + J - reuse(j, 2)))
                    for m in range(KD):
                        flip = pe.transpose(c.bank[4 + j % 2][:, m * P:m * P + P], yt[:, m, j * P:j * P + P],
                                            c.ident[:, :])
                    flip.then_inc(back, 1)
                if ln:
                    if last:
                        pe.wait_ge(logits_ready, g + 1)
                    else:
                        pe.wait_ge(out_ready, g + 1)
                    for j in range(J):
                        if last:
                            pe.wait_ge(z_ready, g * J + (j + 1))
                        pe.wait_ge(out_t_ready, g * J + (j + 1 + J - reuse(j, 2)))
                        to_columns(pe, c.bank[6 + j % 2], out[:, j, :], c.ident[:, :]).then_inc(out_flipped, 1)
                        if last:
                            pe.wait_ge(out_t_ready, g * J + (j + 1 + J))
                            X = last.experts
                            for k in range(KD):
                                prod = pe.matmul(c.bank[1][:, D + j * X:D + j * X + X], out_t[:, k, j * P:j * P + P],
                                                 gate[:, k, :], start=(k == 0), stop=(k == KD - 1))
                            prod.then_inc(gated, 1)

        @block.scalar
        def _(act):
            act.wait_ge(w_in, n_in * 16)
            act.sem_inc(pooled_t, J)
            act.sem_inc(relu_done, 2)
            act.sem_inc(yt_saved, 16)
            if last:
                act.sem_inc(logits_ready, 1)
            if ln:
                act.sem_inc(out_t_ready, J)
                act.sem_inc(out_t_saved, 16)
            with act.Fori(0, G) as g:
                for j in range(J):
                    act.wait_ge(flipped, g * J + (j + 1))
                    act.copy(ins[:, 1, :, j * P:j * P + P], split_columns(c.bank[j % ways])).then_inc(pooled_t, 1)
                act.wait_ge(back, g * J + 1)
                if not ln:
                    act.wait_ge(yt_saved, g * 16 + 16)
                for n, (m, half) in enumerate(parts):
                    act.wait_ge(product, g * 4 + (n + 1))
                    act.activation(yt[:, m, half * HALF:half * HALF + HALF], c.bank[2 + n % 2][:, 0:HALF], ACT.Relu,
                                   bias=bias[:, m:m + 1]).then_inc(relu_done, 1)
                if ln:
                    norm.scalar(act, g)
                    if last:
                        norm_x.scalar(act, g)
                    else:
                        act.wait_ge(out_t_saved, g * 16 + 16)
                    for j in range(J):
                        act.wait_ge(out_flipped, g * J + (j + 1))
                        act.copy(out_t[:, :, j * P:j * P + P], split_columns(c.bank[6 + j % 2])
                                 ).then_inc(out_t_ready, 1)
                    if last:
                        act.wait_ge(gated, g * J + J)
                        act.copy(last.logits[:, bass.ds(g * J, J), :],
                                 c.bank[1][:, D:D + J * last.experts].rearrange("p (j e) -> p j e", j=J)
                                 ).then_inc(logits_ready, 1)

        @block.vector
        def _(vec):
            vec.wait_ge(w_in, n_in * 16)
            vec.sem_inc(ins_free, 1)
            vec.sem_inc(y_ready, J)
            vec.sem_inc(y_saved, 16)
            vec.sem_inc(back, 1)
            with vec.Fori(0, G) as g:
                if ln:
                    vec.wait_ge(relu_done, g * 4 + 6)
                    vec.tensor_tensor(yt[:, :, :], yt[:, :, :], ins[:, 0, :, :], ALU.add).then_inc(sum_ready, 1)
                    vec.wait_ge(sum_ready, g + 1)
                    vec.sem_inc(ins_free, 1)
                else:
                    vec.wait_ge(y_saved, g * 16 + 16)
                for j in range(J):
                    vec.wait_ge(back, g * J + (j + 2))
                    vec.tensor_copy(y[:, j, :], c.bank[4 + j % 2][:, 0:D]).then_inc(y_ready, 1)
                if ln:
                    vec.wait_ge(y_ready, g * J + 2 * J)
                    norm.vector(vec, g, lambda j: y[:, j, :])
                    step = Chain(vec, gain_steps, g * 3)
                    for j in range(J):
                        move = norm.apply(vec, y[:, j, :], y[:, j, :], j)
                    step(move)
                    step(vec.tensor_tensor(y[:, :, :], y[:, :, :], gain[:, :].unsqueeze(1).to_broadcast([P, J, D]),
                                           ALU.mult))
                    if not last:
                        vec.wait_ge(y_saved, g * 16 + 16)
                        vec.wait_ge(out_t_ready, g * J + J)
                        step(vec.tensor_tensor(out[:, :, :], y[:, :, :],
                                               offset[:, :].unsqueeze(1).to_broadcast([P, J, D]), ALU.add))
                        vec.sem_inc(out_ready, 1)
                    else:
                        step(vec.tensor_tensor(y[:, :, :], y[:, :, :],
                                               offset[:, :].unsqueeze(1).to_broadcast([P, J, D]), ALU.add))
                        vec.tensor_tensor(c.x[:, bass.ds(g * J, J), :], c.x[:, bass.ds(g * J, J), :], y[:, :, :],
                                          ALU.add).then_inc(x_ready, 1)
                        vec.wait_ge(x_ready, g + 1)
                        norm_x.vector(vec, g, lambda j: c.x[:, g * J + j, :])
                        vec.wait_ge(y_saved, g * 16 + 16)
                        vec.wait_ge(out_t_ready, g * J + J)
                        for j in range(J):
                            norm_x.apply(vec, out[:, j, :], c.x[:, g * J + j, :], j).then_inc(z_ready, 1)


def finish_layer1(c, r, out):
    own, sb = stage(c, "finish1")
    with own:
        d = c.dram
        es = ExpertSum(c, r, sb, "sum1", d["z4"], d["L1_ffn_b2"])
        saved, step = c.sems("finish1", "saved", "step")
        done = c.sem("finish1_done")
        banks = (0, 1, 2, 3)
        block = own.enter_context(c.nc.Block())

        @block.sync
        def _(sp):
            es.sync_first(sp)
            es.sync(sp, 0)
            with sp.Fori(0, G - 1) as g:
                es.sync(sp, g + 1)
                sp.wait_ge(done, g + 1)
                sp.dma_start(group_rows(out, g), es.total[:, :, :]).then_inc(saved, 16)
            sp.wait_ge(done, G)
            sp.dma_start(group_rows(out, G - 1), es.total[:, :, :]).then_inc(saved, 16)
            sp.wait_ge(saved, 16 * G + 16)

        @block.gpsimd
        def _(pool):
            with pool.Fori(0, G) as g:
                es.pool(pool, g)

        @block.tensor
        def _(pe):
            pe.wait_ge(es.bias_in, 16)
            es.open(pe)
            with pe.Fori(0, G) as g:
                es.tensor(pe, g, banks)

        @block.scalar
        def _(act):
            with act.Fori(0, G) as g:
                es.scalar(act, g, banks)

        @block.vector
        def _(vec):
            vec.sem_inc(saved, 16)
            with vec.Fori(0, G) as g:
                vec.wait_ge(saved, g * 16 + 16)
                es.vector(vec, g, step, banks)
                vec.tensor_tensor(es.total[:, :, :], es.total[:, :, :], c.x[:, bass.ds(g * J, J), :], ALU.add
                                  ).then_inc(done, 1)


def program(nc, ins, out):
    with ExitStack() as ctx:
        def scratch(name, *shape):
            return nc.dram_tensor(name, shape, F32, kind="Internal").ap()

        d = dict(ins)
        for name in ("z0", "z2", "h", "a1", "a2", "z4"):
            d[name] = scratch(name, NP, D)
        for name in ("z0_cols", "z3_cols", "a1_cols", "a2_cols"):
            d[name] = scratch(name, P, KD, NP)
        d["state"] = scratch("state", EP + 1 + P, D)
        d["node_ends"] = scratch("node_ends", NP + 1)
        d["expert_out"] = scratch("expert_out", 2 * NP + max(places(16), places(8)) * P, D)
        c = Core(nc, ctx, d)

        setup(c)
        kv = KeyValue0(c)
        mixed = Mixed0(c, kv)
        edge_walk(c, "walk0", d["z0"], "sum", (kv, mixed, Mlp0(c, mixed)))
        own, sb = stage(c, "routes0")
        with own:
            r = Routes(c, sb, 16, places(16))
            convolve0(c, r.logits)
            route(c, r, "route0", False)
            experts(c, r, "experts0", d["z2"], d["L0_ffn_w1"], d["expert_b1_0"], d["L0_ffn_w2"], ACT.Relu)
            finish_layer0(c, r)

        kv = KeyValue1(c)
        edge_walk(c, "walk1", d["h"], "max0", (kv, Mixed1(c, kv), Work()))
        update(c, "update1", d["z3_cols"], d["w_m1_t"], d["L1_gnn_bm1"], out_rows=d["a1"], out_cols=d["a1_cols"])
        edge_walk(c, "walk2", d["a1"], "max0")
        update(c, "update2", d["a1_cols"], d["w_m2_t"], d["L1_gnn_bm2"], ln=(d["L1_gnn_ln2_g"], d["L1_gnn_ln2_b"]),
               out_rows=d["a2"], out_cols=d["a2_cols"])
        edge_walk(c, "walk3", d["a2"], "max")
        own, sb = stage(c, "routes1")
        with own:
            r = Routes(c, sb, 8, places(8))
            update(c, "update3", d["a2_cols"], d["w_m3_t"], d["L1_gnn_bm3"], ln=(d["L1_gnn_ln3_g"], d["L1_gnn_ln3_b"]),
                   out_rows=d["z4"], last=r)
            route(c, r, "route1", True)
            experts(c, r, "experts1", d["z4"], d["L1_ffn_w1"], d["expert_b1_1"], d["L1_ffn_w2"], ACT.Gelu)
            finish_layer1(c, r, out)



def kernel(**inputs):
    import numpy as np
    import concourse.bacc as bacc
    from concourse.bass_utils import run_bass_kernel_spmd as run

    def padded(a, size, fill, lead=0):
        out = np.full((size,) + a.shape[1:], fill, a.dtype)
        out[lead:lead + len(a)] = a
        return out

    a = {k: np.asarray(v) for k, v in inputs.items()}
    arrays = {k: v for k, v in a.items() if k.startswith(("L0_", "L1_"))}
    arrays["x"] = padded(a["x"], NP, 0)
    arrays["src"] = padded(a["src"], EP, 0)
    arrays["dst"] = padded(a["dst"], EP + 1, NP - 1, 1)
    arrays["dst"][0] = -1
    arrays["w_q_t"] = a["L0_mix_w_qkv"][:, :D].T
    arrays["w_p1_t"] = arrays.pop("L1_gnn_Wp1").T
    for n in (1, 2, 3):
        arrays[f"w_m{n}_t"] = arrays.pop(f"L1_gnn_Wm{n}").T
    arrays["router_w_t"] = arrays.pop("L1_ffn_router_w").T
    for n in (0, 1):
        b = arrays.pop(f"L{n}_ffn_b1")
        arrays[f"expert_b1_{n}"] = b.reshape(len(b), -1, P).transpose(0, 2, 1)
    arrays = {f"in_{k}": np.ascontiguousarray(v) for k, v in arrays.items()}

    nc = bacc.Bacc("TRN2", target_bir_lowering=False, num_devices=1)
    ins = {k[3:]: nc.dram_tensor(k, v.shape, mybir.dt.from_np(v.dtype), kind="ExternalInput").ap()
           for k, v in arrays.items()}
    out = nc.dram_tensor("out", (NP, D), F32, kind="ExternalOutput").ap()
    program(nc, ins, out)
    r = run(nc, [arrays], core_ids=[0])
    return r.results[0]["out"][:N]
```

```python
from contextlib import ExitStack

import concourse.bass as bass
from concourse import mybir

F32 = mybir.dt.float32
BF16 = mybir.dt.bfloat16
I32 = mybir.dt.int32
U32 = mybir.dt.uint32
ALU = mybir.AluOpType
ACT = mybir.ActivationFunctionType
AX = mybir.AxisListType

P = 128
N = 3125
NT = -(-N // P)
NP = NT * P
G = 5
J = NT // G
GW = J * P
HALF = GW // 2
D = 256
KD = D // P
E = 53125
SLOTS = 3
RING = 14
TURN = 2 * RING
STORE = RING // 2
TURNS = SLOTS * G
LANE = TURNS * TURN
EP = P * LANE
LO = 64
HI = NP // LO
HOT = LANE // G
EPS = 1e-5
FAR = 1.5e38
ROUND = 12582912.0
HIDDEN = 3 * D
KH = HIDDEN // P
HEAD0 = D // 4
HEAD1 = D // 8
PER1 = P // HEAD1
assert NT == G * J and NP % LO == 0 and EP >= E and LANE % G == 0


class Chain:

    def __init__(self, engine, sem, before=0):
        self.engine, self.sem, self.n = engine, sem, before

    def __call__(self, instruction):
        self.n += 1
        instruction.then_inc(self.sem, 1)
        self.engine.wait_ge(self.sem, self.n)


class Core:

    def __init__(self, nc, ctx, dram):
        self.nc, self.ctx, self.dram = nc, ctx, dram
        self.live = []
        self.x = self.sb("x_acc", [P, NT, D])
        self.ident = self.sb("ident", [P, P])
        self.ones = self.sb("ones", [P, P])
        self.upper = self.sb("upper", [P, P])
        self.eps = self.sb("eps", [P, 1])
        self.real = self.sb("real", [P, NT])
        self.count_up = self.sb("count_up", [P, P], I32)
        self.keep = self.sb("keep", [P, LANE + TURN])
        self.cut = self.sb("cut", [P, LANE + TURN])
        self.src = self.sb("src_idx", [P, LANE + TURN], U32)
        self.lane_keep = self.sb("lane_keep", [P, P])
        self.lane_cut = self.sb("lane_cut", [P, P])
        self.end_idx = self.sb("end_idx", [P, NT], U32)
        self.run_idx = self.sb("run_idx", [P, 1], U32)
        self.fix_idx = self.sb("fix_idx", [P, 1], U32)
        self.bank = [ctx.enter_context(nc.psum_tensor(f"bank{i}", [P, 512], F32)) for i in range(8)]

    def sb(self, name, shape, dt=F32):
        return self.ctx.enter_context(self.nc.sbuf_tensor(name, shape, dt))

    def sem(self, name):
        self.live.append(self.nc.alloc_semaphore(name))
        return self.live[-1]

    def retire(self):
        if self.live:
            self.nc.clear_and_free_semaphores(self.live)
            self.nc.all_engine_barrier()
            self.live = []

    def sems(self, prefix, *names):
        return [self.sem(f"{prefix}_{n}") for n in names]


class Local:

    def __init__(self, c, own, prefix):
        self.c, self.own, self.prefix = c, own, prefix
        own.callback(c.retire)

    def __call__(self, name, shape, dt=F32):
        return self.own.enter_context(self.c.nc.sbuf_tensor(f"{self.prefix}_{name}", shape, dt))


def all_rows(ap):
    n = ap.shape[0]
    return ap.rearrange("(a n) -> a n", a=1).to_broadcast([P, n])


def one_row(ap):
    return ap.rearrange("(a n) -> a n", a=1)


def chunked(ap):
    return ap.rearrange("(k p) n -> p k n", p=P)


def group_rows(table, g):
    return table.rearrange("(g j p) d -> g p j d", g=G, p=P)[g]


class Norm:

    STEPS = 6

    def __init__(self, c, sb, prefix):
        self.c = c
        self.stats = sb(f"{prefix}_stats", [P, J, 6])
        self.m = sb(f"{prefix}_moment", [P, 4, J])
        self.var = sb(f"{prefix}_var", [P, J])
        self.std = sb(f"{prefix}_std", [P, J])
        self.rstd = sb(f"{prefix}_rstd", [P, NT])
        self.shift = sb(f"{prefix}_shift", [P, NT])
        self.var_ready, self.std_ready, self.step, self.go = c.sems(
            prefix, "var_ready", "std_ready", "norm_step", "norm_go")

    def vector(self, vec, g, rows):
        vec.sem_inc(self.go, 1)
        step = Chain(vec, self.step, g * self.STEPS)
        for j in range(J):
            last = vec.bn_stats(self.stats[:, j, :], rows(j))
        step(last)
        self.moments(vec, step, g)

    def moments(self, vec, step, g):
        st, m = self.stats, self.m
        step(vec.tensor_tensor(m[:, 0:3:2, :], st[:, :, 1:3].rearrange("p j s -> p s j"),
                               st[:, :, 4:6].rearrange("p j s -> p s j"), ALU.add))
        step(vec.tensor_tensor(m[:, 1, :], st[:, :, 1], st[:, :, 4], ALU.subtract))
        step(vec.tensor_tensor(m[:, 3, :], m[:, 1, :], m[:, 1, :], ALU.mult))
        vec.scalar_tensor_tensor(out=self.var[:, :], in0=m[:, 3, :], scalar=D / 4.0, in1=m[:, 2, :],
                                 op0=ALU.mult, op1=ALU.add).then_inc(self.var_ready, 1)
        part = bass.ds(g * J, J)
        vec.wait_ge(self.std_ready, g + 1)
        vec.sem_inc(self.go, 1)
        step(vec.reciprocal(self.rstd[:, part], self.std[:, :]))
        step(vec.scalar_tensor_tensor(out=self.shift[:, part], in0=m[:, 0, :], scalar=-0.5, in1=self.rstd[:, part],
                                      op0=ALU.mult, op1=ALU.mult))

    def scalar(self, act, g):
        act.wait_ge(self.var_ready, g + 1)
        act.activation(self.std[:, :], self.var[:, :], ACT.Sqrt, bias=self.c.eps[:, 0:1],
                       scale=1.0 / D).then_inc(self.std_ready, 1)

    def apply(self, vec, out, row, t):
        return vec.tensor_scalar(out, row, self.rstd[:, bass.ds(t, 1)], self.shift[:, bass.ds(t, 1)],
                                 ALU.mult, ALU.add)

    def apply_act(self, act, out, row, t):
        return act.activation(out, row, ACT.Identity, bias=self.shift[:, bass.ds(t, 1)],
                              scale=self.rstd[:, bass.ds(t, 1)])


def setup(c):
    nc, dram = c.nc, c.dram
    with ExitStack() as own:
        sb = Local(c, own, "setup")
        dst = sb("dst", [P, LANE], I32)
        before = sb("dst_before", [P, LANE], I32)
        run = sb("run", [P, LANE])
        step_no = sb("step_no", [P, LANE], I32)
        run_end = sb("run_end", [P, 1])
        lane_no = sb("lane_no", [P, 1], I32)
        lane_f = sb("lane_f", [P, 4])
        lane_full = sb("lane_full", [P, 1])
        diag = sb("diag", [P, P])
        zero = sb("zero", [P, D])
        z = sb("z", [P, J, D])
        zt = sb("zt", [P, KD, GW])
        norm = Norm(c, sb, "setup")
        x_in, edges_in, pool_step, const_ready, step_sem, consts_out = c.sems(
            "setup", "x_in", "edges_in", "pool_step", "const_ready", "step", "consts_out")
        diag_ready, lanes_ready, z_ready, z_saved, flipped, taken, zt_saved = c.sems(
            "setup", "diag_ready", "lanes_ready", "z_ready", "z_saved", "flipped", "taken", "zt_saved")
        block = own.enter_context(nc.Block())
        lanes = c.bank[7][:, 0:P]

        @block.sync
        def _(sp):
            def lane_view(at):
                return dram["dst"][at:at + EP].rearrange("(p k) -> p k", p=P)

            sp.dma_start(c.x[:, :, :], dram["x"].rearrange("(t p) d -> p t d", p=P)).then_inc(x_in, 16)
            sp.dma_start(dst[:, :], lane_view(1)).then_inc(edges_in, 16)
            sp.dma_start(before[:, :], lane_view(0)).then_inc(edges_in, 16)
            sp.dma_start(c.src[:, 0:LANE], dram["src"].rearrange("(p k) -> p k", p=P).bitcast(U32)
                         ).then_inc(edges_in, 16)
            sp.wait_ge(const_ready, 1)
            sp.dma_start(dram["state"][EP:EP + P, :], zero[:, :]).then_inc(consts_out, 16)
            sp.dma_start(dram["state"][EP + P:EP + P + 1, :], zero[0:1, :]).then_inc(consts_out, 16)
            for k in range(2):
                sp.dma_start(dram["expert_out"][k * NP + N:k * NP + NP, :], zero[0:NP - N, :]
                             ).then_inc(consts_out, 16)
            with sp.Fori(0, G) as g:
                sp.wait_ge(z_ready, g * J + J)
                sp.dma_start(group_rows(dram["z0"], g), z[:, :, :]).then_inc(z_saved, 16)
                sp.wait_ge(taken, g * J + 2 * J)
                sp.dma_start(dram["z0_cols"][:, :, bass.ds(g * GW, GW)], zt[:, :, :]).then_inc(zt_saved, 16)
            sp.wait_ge(consts_out, 4 * 16)
            sp.wait_ge(z_saved, 16 * G + 16)
            sp.wait_ge(zt_saved, 16 * G + 16)

        @block.gpsimd
        def _(pool):
            step = Chain(pool, pool_step)
            pool.memset(zero[:, :], 0.0)
            pool.memset(c.ones[:, :], 1.0)
            pool.memset(c.eps[:, :], EPS)
            pool.memset(c.src[:, LANE:], 0)
            pool.iota(c.count_up[:, :], pattern=[[1, P]], base=0, channel_multiplier=0)
            pool.iota(step_no[:, :], pattern=[[1, LANE]], base=0, channel_multiplier=0)
            pool.iota(lane_no[:, :], pattern=[[0, 1]], base=0, channel_multiplier=1)
            pool.memset(c.ident[:, :], 0.0)
            pool.memset(c.real[:, :], 1.0)
            step(pool.memset(c.upper[:, :], 1.0))
            pool.affine_select(out=c.ident[:, :], in_=c.ident[:, :], compare_op=ALU.not_equal, fill=1.0,
                               base=0, pattern=[[-1, P]], channel_multiplier=1)
            pool.affine_select(out=c.real[:, :], in_=c.real[:, :], compare_op=ALU.is_ge, fill=0.0,
                               base=N - 1, pattern=[[-P, NT]], channel_multiplier=-1)
            pool.affine_select(out=c.upper[:, :], in_=c.upper[:, :], compare_op=ALU.is_gt, fill=0.0,
                               base=0, pattern=[[1, P]], channel_multiplier=-1).then_inc(const_ready, 1)

        @block.vector
        def _(vec):
            step = Chain(vec, step_sem)
            vec.wait_ge(edges_in, 3 * 16)
            vec.wait_ge(const_ready, 1)
            vec.memset(c.keep[:, LANE:], 0.0)
            vec.memset(c.cut[:, LANE:], 0.0)
            step(vec.tensor_tensor(c.keep[:, 0:LANE], dst[:, :], before[:, :], ALU.is_equal))
            step(vec.tensor_scalar(c.cut[:, 0:LANE], c.keep[:, 0:LANE], FAR, -FAR, ALU.mult, ALU.add))
            step(vec.memset(c.cut[:, 0:1], -FAR))
            step(vec.tensor_tensor(lane_full[:, :], dst[:, LANE - 1:LANE], before[:, 0:1], ALU.is_equal))
            vec.tensor_scalar(diag[:, :], c.ident[:, :], lane_full[:, 0:1], None, ALU.mult
                              ).then_inc(diag_ready, 1)
            step(vec.tensor_scalar(run[:, :], c.keep[:, 0:LANE], float(LANE), None, ALU.mult))
            step(vec.tensor_tensor(run[:, :], run[:, :], step_no[:, :], ALU.add))
            step(vec.tensor_reduce(run_end[:, :], run[:, :], AX.X, ALU.min))
            f = lane_f
            step(vec.tensor_scalar(f[:, 0:1], lane_no[:, :], float(LANE), None, ALU.mult))
            step(vec.tensor_scalar(f[:, 1:2], run_end[:, :], -1.0, 0.0, ALU.add, ALU.max))
            step(vec.tensor_tensor(f[:, 1:2], f[:, 1:2], f[:, 0:1], ALU.add))
            step(vec.tensor_copy(c.run_idx[:, :], f[:, 1:2]))
            step(vec.tensor_scalar(f[:, 2:3], run_end[:, :], 0.0, None, ALU.is_gt))
            step(vec.tensor_scalar(f[:, 3:4], lane_no[:, :], EP + 1.0, None, ALU.add))
            step(vec.tensor_tensor(f[:, 0:1], f[:, 1:2], f[:, 3:4], ALU.subtract))
            step(vec.tensor_tensor(f[:, 0:1], f[:, 0:1], f[:, 2:3], ALU.mult))
            step(vec.tensor_tensor(f[:, 0:1], f[:, 0:1], f[:, 3:4], ALU.add))
            step(vec.tensor_copy(c.fix_idx[:, :], f[:, 0:1]))
            vec.wait_ge(lanes_ready, 1)
            step(vec.tensor_copy(c.lane_keep[:, :], lanes))
            vec.tensor_scalar(c.lane_cut[:, :], c.lane_keep[:, :], FAR, -FAR, ALU.mult, ALU.add)
            vec.wait_ge(x_in, 16)
            vec.sem_inc(z_saved, 16)
            with vec.Fori(0, G) as g:
                norm.vector(vec, g, lambda j: c.x[:, g * J + j, :])
                vec.wait_ge(z_saved, 16 * g + 16)
                vec.wait_ge(flipped, g * J + 1)
                for j in range(J):
                    norm.apply(vec, z[:, j, :], c.x[:, g * J + j, :], g * J + j).then_inc(z_ready, 1)

        @block.tensor
        def _(pe):
            pe.wait_ge(diag_ready, 1)
            pe.matmul(lanes, c.ones[:, :], diag[:, :], start=True, stop=True).then_inc(lanes_ready, 1)
            pe.sem_inc(flipped, 1)
            with pe.Fori(0, G) as g:
                for j in range(J):
                    pe.wait_ge(z_ready, g * J + j + 1)
                    pe.wait_ge(taken, g * J + j + 1)
                    for k in range(KD):
                        last = pe.transpose(c.bank[j][:, k * P:k * P + P], z[:, j, k * P:k * P + P], c.ident[:, :])
                    last.then_inc(flipped, 1)

        @block.scalar
        def _(act):
            act.sem_inc(taken, J)
            act.sem_inc(zt_saved, 16)
            with act.Fori(0, G) as g:
                norm.scalar(act, g)
                act.wait_ge(zt_saved, 16 * g + 16)
                for j in range(J):
                    act.wait_ge(flipped, g * J + j + 2)
                    act.copy(zt[:, :, j * P:j * P + P], c.bank[j][:, 0:D].rearrange("p (k n) -> p k n", k=KD)
                             ).then_inc(taken, 1)


def reuse(j, n):
    return n if j >= n else J + j - max(i for i in range(J) if i % n == j % n)


class Work:

    TURNS = 1
    LAST_DIFFERS = False

    def buffers(self, sb):
        pass

    def first(self, engine, which):
        pass

    def before(self, engine, which):
        pass

    def turn(self, engine, which, g):
        pass

    def piece(self, vec, g, n):
        pass

    def after(self, engine, which):
        pass


def edge_walk(c, name, table, reduce, work=None):
    nc, dram = c.nc, c.dram
    work = work or (Work(), Work(), Work())
    assert sum(w.TURNS for w in work) == SLOTS
    restart = c.cut if reduce == "max" else c.keep
    join = ALU.add if reduce == "max" else ALU.mult
    merge = ALU.add if reduce == "sum" else ALU.max
    lane_restart = c.lane_cut if reduce == "max" else c.lane_keep
    nothing = -FAR if reduce == "max" else 0.0
    CREDIT = RING + 1
    states = dram["state"][0:EP, :].rearrange("(p k) d -> p k d", p=P)

    with ExitStack() as own:
        sb = Local(c, own, name)
        ring = sb("ring", [P, RING, D])
        state = sb("state", [P, RING, D])
        idx = sb("idx", [P, 2, RING], U32)
        mark = sb("mark", [P, 2, RING])
        scanned = sb("scanned", [P, KD, P + 1])
        carry = sb("carry", [P, D])
        run = sb("run", [P, D])
        walked, idx_ready, turn_go = c.sems(name, "walked", "idx_ready", "turn_go")
        stored = c.sems(name, "stored0", "stored1")
        arrived = c.sems(name, *(f"arrived{j}" for j in range(RING)))
        flipped, summed, back, carry_rows, run_in, merged, fixed = c.sems(
            name, "flipped", "summed", "back", "carry_rows", "run_in", "merged", "fixed")
        for w in work:
            w.buffers(sb)
        block = own.enter_context(nc.Block())

        def slots(engine, which, group):
            for w in work:
                w.first(engine, which)
            turn = 0
            for w in work:
                w.before(engine, which)
                with engine.Fori(0, G - 1 if w.LAST_DIFFERS else G) as g:
                    group(turn + g * w.TURNS, g, w)
                turn += G * w.TURNS
                if w.LAST_DIFFERS:
                    group(turn - w.TURNS, G - 1, w)
                w.after(engine, which)

        @block.gpsimd
        def _(pool):
            with pool.Fori(0, TURNS) as i:
                for h in range(2):
                    pool.wait_ge(idx_ready, i * 2 + h + 1)
                    for j in range(RING):
                        if j % 2 == 0:
                            pool.wait_ge(walked, i * TURN + (h * RING + j + 2 + 1))
                            pool.sem_inc(turn_go, 1)
                        pool.indirect_dma_start(ring[:, j, :], None, table[:, :],
                                                bass.IndirectOffsetOnAxis(idx[:, h, j:j + 1], 0)
                                                ).then_inc(arrived[j], 16)
            for q in range(2):
                pool.wait_ge(stored[q], 16 + 16 * TURNS * 2)
            pool.indirect_dma_start(run[:, :], None, dram["state"][:, :],
                                    bass.IndirectOffsetOnAxis(c.run_idx[:, 0:1], 0)).then_inc(run_in, 16)
            pool.wait_ge(merged, 1)
            pool.indirect_dma_start(dram["state"][:, :], bass.IndirectOffsetOnAxis(c.fix_idx[:, 0:1], 0),
                                    run[:, :], None).then_inc(fixed, 16)
            pool.wait_ge(fixed, 16)

        @block.vector
        def _(vec):
            def stage(i, h):
                at = i * TURN + h * RING
                vec.tensor_copy(mark[:, h, :], restart[:, bass.ds(at, RING)])
                vec.tensor_copy(idx[:, h, :], c.src[:, bass.ds(at, RING)]).then_inc(idx_ready, 1)

            def walk_turn(i, g, w, before):
                for h in range(2):
                    for j in range(RING):
                        if j % STORE == 0:
                            vec.wait_ge(stored[j // STORE], i * 32 + (h + 1) * 16)
                        vec.wait_ge(arrived[j], i * 32 + (h + 1) * 16)
                        vec.wait_ge(walked, i * TURN + (h * RING + j + CREDIT))
                        vec.scalar_tensor_tensor(out=state[:, j, :], in0=state[:, (j - 1) % RING, :],
                                                 scalar=mark[:, h, j:j + 1], in1=ring[:, j, :],
                                                 op0=join, op1=merge).then_inc(walked, 1)
                        w.piece(vec, g, before + h * RING + j)
                    vec.wait_ge(walked, i * TURN + ((h + 1) * RING + CREDIT))
                    stage(i + 1, h)
                    vec.wait_ge(idx_ready, i * 2 + (h + 3))

            stage(0, 0)
            stage(0, 1)
            vec.memset(state[:, RING - 1, :], 0.0).then_inc(walked, 1)
            vec.sem_inc(walked, RING)
            for q in range(2):
                vec.sem_inc(stored[q], 16)
            vec.wait_ge(idx_ready, 2)
            def group(i, g, w):
                for r in range(w.TURNS):
                    walk_turn(i + r, g, w, r * TURN)

            slots(vec, "vector", group)
            vec.memset(scanned[:, :, 0:1], nothing)
            vec.wait_ge(flipped, 1)
            for k in range(KD):
                vec.tensor_tensor_scan(scanned[:, k, 1:P + 1], lane_restart[:, :], c.bank[0][:, k * P:k * P + P],
                                       nothing, join, merge).then_inc(summed, 1)
            vec.wait_ge(run_in, 16)
            vec.wait_ge(carry_rows, 1)
            vec.tensor_tensor(run[:, :], run[:, :], carry[:, :], merge).then_inc(merged, 1)

        @block.sync
        def _(sp):
            def group(i, g, w):
                w.turn(sp, "sync", g)
                for q in range(4 * w.TURNS):
                    first = (q % 2) * STORE
                    sp.wait_ge(walked, i * TURN + ((q + 1) * STORE + CREDIT))
                    sp.dma_start(states[:, bass.ds(i * TURN + q * STORE, STORE), :],
                                 state[:, first:first + STORE, :]).then_inc(stored[q % 2], 16)

            slots(sp, "sync", group)
            for q in range(2):
                sp.wait_ge(stored[q], 16 + 16 * TURNS * 2)

        @block.tensor
        def _(pe):
            slots(pe, "tensor", lambda i, g, w: w.turn(pe, "tensor", g))
            pe.wait_ge(walked, LANE + CREDIT)
            for k in range(KD):
                last = pe.transpose(c.bank[0][:, k * P:k * P + P], state[:, RING - 1, k * P:k * P + P],
                                    c.ident[:, :])
            last.then_inc(flipped, 1)
            pe.wait_ge(summed, KD)
            for k in range(KD):
                last = pe.transpose(c.bank[1][:, k * P:k * P + P], scanned[:, k, 0:P], c.ident[:, :])
            last.then_inc(back, 1)

        @block.scalar
        def _(act):
            slots(act, "scalar", lambda i, g, w: w.turn(act, "scalar", g))
            act.wait_ge(back, 1)
            act.copy(carry[:, :], c.bank[1][:, 0:D]).then_inc(carry_rows, 1)


def columns(ap):
    return ap.rearrange("(k p) -> p k", p=P)


class EdgeCount:

    def __init__(self, c):
        self.c = c

    def buffers(self, sb):
        c = self.c
        self.dst = sb("dst", [P, LANE], I32)
        self.low = sb("dst_low", [P, LANE], I32)
        self.is_low = sb("is_low", [P, HOT, LO], BF16)
        self.is_high = sb("is_high", [P, HOT, HI], BF16)
        self.none = sb("none", [P, LO], BF16)
        self.along = sb("along", [HI, LO])
        self.total = sb("total", [HI, LO])
        self.zero = sb("zero", [1, 1])
        self.upto = sb("upto", [P, NT])
        self.start = sb("start", [P, NT])
        self.t = [sb(f"node_t{i}", [P, NT]) for i in range(2)]
        (self.dst_in, self.split, self.hot, self.counted, self.closed, self.step, self.along_ready,
         self.before_ready, self.total_ready, self.table_out, self.table_in, self.opened) = c.sems(
            "count", "dst_in", "split", "hot", "counted", "closed", "step", "along_ready", "before_ready",
            "total_ready", "table_out", "table_in", "opened")
        self.counts = c.bank[3][0:HI, 0:LO]
        self.before_rows = c.bank[6][0:HI, 0:1]
        self.chain = None

    def first(self, eng, which):
        c, nc = self.c, self.c.nc
        if which == "sync":
            eng.dma_start(self.dst[:, :], c.dram["dst"][1:1 + EP].rearrange("(p k) -> p k", p=P)
                          ).then_inc(self.dst_in, 16)
        if which == "vector":
            self.chain = Chain(eng, self.step)
            eng.memset(self.zero[:, :], 0.0)
            eng.memset(self.none[:, :], 0.0).then_inc(self.opened, 1)
            eng.wait_ge(self.dst_in, 16)
            self.chain(eng.tensor_scalar(self.low[:, :], self.dst[:, :], LO - 1, None, ALU.bitwise_and))
            self.chain(eng.tensor_scalar(self.dst[:, :], self.dst[:, :], LO.bit_length() - 1, None,
                                         ALU.arith_shift_right))
        if which == "tensor":
            eng.wait_ge(self.opened, 1)
            eng.matmul(self.counts, self.none[:, 0:HI], self.none[:, :], start=True, stop=False,
                       skip_group_check=True).then_inc(self.counted, 1)

    def turn(self, eng, which, g):
        c = self.c
        if which == "tensor":
            eng.wait_ge(self.hot, g + 1)
            for k in range(HOT):
                last = eng.matmul(self.counts, self.is_high[:, k, :], self.is_low[:, k, :], start=False,
                                  stop=False, skip_group_check=True)
            last.then_inc(self.counted, 1)

    def piece(self, eng, g, n):
        c = self.c
        part = bass.ds(g * HOT, HOT)
        if n == 4:
            eng.wait_ge(self.counted, g + 1)
            eng.tensor_tensor(self.is_low[:, :, :],
                              self.low[:, part].unsqueeze(2).to_broadcast([P, HOT, LO]),
                              c.count_up[:, 0:LO].unsqueeze(1).to_broadcast([P, HOT, LO]), ALU.is_equal)
        if n == 14:
            eng.tensor_tensor(self.is_high[:, :, :],
                              self.dst[:, part].unsqueeze(2).to_broadcast([P, HOT, HI]),
                              c.count_up[:, 0:HI].unsqueeze(1).to_broadcast([P, HOT, HI]),
                              ALU.is_equal).then_inc(self.hot, 1)

    def after(self, eng, which):
        c, flat, step = self.c, self.c.dram["node_ends"], self.chain
        if which == "tensor":
            eng.matmul(self.counts, self.none[:, 0:HI], self.none[:, :], start=False, stop=True,
                       skip_group_check=True).then_inc(self.closed, 1)
            eng.wait_ge(self.along_ready, 1)
            eng.matmul(self.before_rows, c.upper[0:HI, 0:HI], self.along[:, LO - 1:LO], start=True,
                       stop=True).then_inc(self.before_ready, 1)
        if which == "vector":
            eng.wait_ge(self.closed, 1)
            eng.tensor_tensor_scan(self.along[:, :], c.ones[0:HI, 0:LO], self.counts, 0.0, ALU.mult,
                                   ALU.add).then_inc(self.along_ready, 1)
            eng.wait_ge(self.along_ready, 1)
            eng.wait_ge(self.before_ready, 1)
            eng.tensor_scalar(self.total[:, :], self.along[:, :], self.before_rows, None, ALU.add
                              ).then_inc(self.total_ready, 1)
        if which == "sync":
            eng.wait_ge(self.total_ready, 1)
            eng.dma_start(one_row(flat[0:1]), self.zero[:, :]).then_inc(self.table_out, 16)
            eng.dma_start(flat[1:1 + NP].rearrange("(h l) -> h l", h=HI), self.total[:, :]
                          ).then_inc(self.table_out, 16)
            eng.wait_ge(self.table_out, 32)
            with c.nc.allow_non_contiguous_dma(reason="node numbers from rows to columns, once"):
                eng.dma_start(self.upto[:, :], flat[1:1 + NP].rearrange("(t p) -> p t", p=P)
                              ).then_inc(self.table_in, 16)
                eng.dma_start(self.start[:, :], flat[0:NP].rearrange("(t p) -> p t", p=P)
                              ).then_inc(self.table_in, 16)

    def finish(self, vec):
        step, (a, b) = self.chain, self.t
        vec.wait_ge(self.table_in, 32)
        step(vec.tensor_tensor(a[:, :], self.upto[:, :], self.start[:, :], ALU.is_gt))
        step(vec.tensor_scalar(b[:, :], self.upto[:, :], -1.0 - EP, None, ALU.add))
        step(vec.tensor_tensor(b[:, :], b[:, :], a[:, :], ALU.mult))
        step(vec.tensor_scalar(b[:, :], b[:, :], float(EP), None, ALU.add))
        step(vec.tensor_copy(self.c.end_idx[:, :], b[:, :]))


class Columns:

    def __init__(self, c, sb, name, table):
        self.table = table
        self.buf = sb(f"{name}_cols", [P, KD, GW])
        self.loaded, self.free = c.sems(name, "cols_in", "cols_free")

    def open(self, pe):
        pe.sem_inc(self.free, 1)

    def load(self, sp, g, n):
        sp.wait_ge(self.free, g + n + 1)
        sp.dma_start(self.buf[:, :, :], self.table[:, :, bass.ds(g * GW, GW)]).then_inc(self.loaded, 16)

    def wait(self, pe, g, n):
        pe.wait_ge(self.loaded, g * 16 + (n + 1) * 16)


class KeyValue0(Work):

    def __init__(self, c):
        self.c = c
        self.count = EdgeCount(c)

    def buffers(self, sb):
        c = self.c
        self.count.buffers(sb)
        self.cols = Columns(c, sb, "mix0", c.dram["z0_cols"])
        self.w = sb("w_kv", [P, KD, 2 * D])
        self.bias = sb("b_kv", [P, 2 * D])
        self.kv = sb("kv", [P, 2, 2 * D])
        self.wqt = sb("w_q_t", [P, KD, D])
        self.bq = sb("b_q", [P, KD])
        self.zero = sb("zeros", [P, D])
        self.top = sb("top", [P, KD])
        self.low = sb("minus_top", [P, KD])
        self.mass = sb("mass", [P, KD])
        self.inv = sb("inv_mass", [P, KD])
        self.attn = sb("attn", [P, KD, P])
        self.attn_t = sb("attn_t", [P, KD, P])
        self.map = sb("map", [P, KD, D])
        self.row = sb("map_row", [1, D])
        (self.w_in, self.made, self.product, self.rows, self.used, self.closed, self.top_ready, self.low_ready,
         self.exp_ready, self.attn_ready, self.attn_flipped, self.attn_t_ready, self.map_done, self.map_ready,
         self.step) = c.sems(
            "kv0", "w_in", "made", "product", "rows", "used", "closed", "top_ready", "low_ready", "exp_ready",
            "attn_ready", "attn_flipped", "attn_t_ready", "map_done", "map_ready", "step")
        self.sums = c.bank[2]

    def first(self, eng, which):
        c, d = self.c, self.c.dram
        self.count.first(eng, which)
        if which == "sync":
            eng.dma_start(self.w[:, :, :], chunked(d["L0_mix_w_qkv"])[:, :, D:]).then_inc(self.w_in, 16)
            eng.dma_start(self.bias[:, :], all_rows(d["L0_mix_b_qkv"][D:])).then_inc(self.w_in, 16)
            eng.dma_start(self.wqt[:, :, :], chunked(d["w_q_t"])).then_inc(self.w_in, 16)
            with c.nc.allow_non_contiguous_dma(reason="a bias as columns"):
                eng.dma_start(self.bq[:, :], columns(d["L0_mix_b_qkv"][0:D])).then_inc(self.w_in, 16)
        if which == "vector":
            eng.memset(self.attn[:, :, :], 0.0)
            eng.memset(self.zero[:, :], 0.0).then_inc(self.made, 1)
            eng.wait_ge(self.w_in, 4 * 16)
            eng.sem_inc(self.rows, J)
        if which == "tensor":
            self.cols.open(eng)
            eng.wait_ge(self.w_in, 4 * 16)
            eng.wait_ge(self.made, 1)
            eng.matmul(self.sums[:, 0:D], self.zero[:, 0:P], self.zero[:, :], start=True, stop=False,
                       skip_group_check=True)
            eng.sem_inc(self.used, J)

    def turn(self, eng, which, g):
        c = self.c
        if which == "sync":
            self.cols.load(eng, g, 0)
        if which == "tensor":
            self.cols.wait(eng, g, 0)

            def product(j):
                eng.wait_ge(self.rows, g * J + (j + 1 + J - reuse(j, 2)))
                for k in range(KD):
                    last = eng.matmul(c.bank[j % 2][:, :], self.cols.buf[:, k, j * P:j * P + P],
                                      self.w[:, k, :], start=(k == 0), stop=(k == KD - 1))
                last.then_inc(self.product, 1)

            product(0)
            for j in range(J):
                if j + 1 < J:
                    product(j + 1)
                eng.wait_ge(self.rows, g * J + (j + 1 + J))
                for k in range(KD):
                    last = eng.matmul(self.sums[:, k * P:k * P + P], self.kv[:, j % 2, k * P:k * P + P],
                                      self.kv[:, j % 2, D + k * P:D + k * P + P], start=False, stop=False,
                                      skip_group_check=True)
                last.then_inc(self.used, 1)
            eng.wait_ge(self.product, g * J + J)
            eng.sem_inc(self.cols.free, 1)
            self.count.turn(eng, which, g)

    def piece(self, eng, g, n):
        c = self.c
        self.count.piece(eng, g, n)
        if n % 5 == 2 and n // 5 < J:
            j = n // 5
            eng.wait_ge(self.product, g * J + (j + 1))
            eng.wait_ge(self.used, g * J + (j + 1 + J - reuse(j, 2)))
            eng.scalar_tensor_tensor(out=self.kv[:, j % 2, :], in0=self.bias[:, :],
                                     scalar=c.real[:, bass.ds(g * J + j, 1)], in1=c.bank[j % 2][:, :],
                                     op0=ALU.mult, op1=ALU.add).then_inc(self.rows, 1)

    def after(self, eng, which):
        c = self.c
        self.count.after(eng, which)
        heads = [(k, h) for k in range(KD) for h in range(P // HEAD0)]
        scale = HEAD0 ** -0.5

        def block(buf, k, h):
            return buf[h * HEAD0:(h + 1) * HEAD0, k, h * HEAD0:(h + 1) * HEAD0]

        sums = self.sums[:, 0:D].rearrange("p (k n) -> p k n", k=KD)
        if which == "tensor":
            eng.matmul(self.sums[:, 0:D], self.zero[:, 0:P], self.zero[:, :], start=False, stop=True,
                       skip_group_check=True).then_inc(self.closed, 1)
            eng.wait_ge(self.attn_ready, 1)
            for k in range(KD):
                last = eng.transpose(c.bank[4][:, k * P:k * P + P], self.attn[:, k, :], c.ident[:, :])
            last.then_inc(self.attn_flipped, 1)
            eng.wait_ge(self.attn_t_ready, 1)
            for m in range(KD):
                for k in range(KD):
                    eng.matmul(c.bank[5][:, m * D + k * P:m * D + k * P + P], self.wqt[:, k, m * P:m * P + P],
                               self.attn_t[:, k, :], start=True, stop=True)
            for k in range(KD):
                last = eng.matmul(c.bank[7][0:1, k * P:k * P + P], self.bq[:, k:k + 1], self.attn_t[:, k, :],
                                  start=True, stop=True)
            last.then_inc(self.map_done, 1)
        if which == "vector":
            step = Chain(eng, self.step)
            eng.wait_ge(self.closed, 1)
            for k, h in heads:
                part = slice(h * HEAD0, (h + 1) * HEAD0)
                last = eng.tensor_reduce(self.top[part, k:k + 1], block(sums, k, h), AX.X, ALU.max)
            step(last)
            eng.tensor_scalar(self.low[:, :], self.top[:, :], -scale, None, ALU.mult).then_inc(self.low_ready, 1)
            eng.wait_ge(self.exp_ready, 1)
            step(eng.reciprocal(self.inv[:, :], self.mass[:, :]))
            for k in range(KD):
                last = eng.tensor_scalar(self.attn[:, k, :], self.attn[:, k, :], self.inv[:, k:k + 1], None,
                                         ALU.mult)
            last.then_inc(self.attn_ready, 1)
            eng.wait_ge(self.map_done, 1)
            for k in range(KD):
                part = slice(k * P, k * P + P)
                step(eng.tensor_copy(self.map[:, k, :], c.bank[5][:, k * D:k * D + D]))
                step(eng.tensor_tensor(self.map[:, k, part], c.bank[5][:, k * D + k * P:k * D + k * P + P],
                                       c.ident[:, :], ALU.add))
            eng.tensor_copy(self.row[:, :], c.bank[7][0:1, 0:D]).then_inc(self.map_ready, 1)
            self.count.finish(eng)
        if which == "scalar":
            eng.wait_ge(self.low_ready, 1)
            for k, h in heads:
                part = slice(h * HEAD0, (h + 1) * HEAD0)
                last = eng.activation(block(self.attn, k, h), block(sums, k, h), ACT.Exp,
                                      bias=self.low[part, k:k + 1], scale=scale,
                                      accum_out=self.mass[part, k:k + 1])
            last.then_inc(self.exp_ready, 1)
            eng.wait_ge(self.attn_flipped, 1)
            eng.copy(self.attn_t[:, :, :], c.bank[4][:, 0:D].rearrange("p (k n) -> p k n", k=KD)
                     ).then_inc(self.attn_t_ready, 1)


class Mlp0(Work):

    TURNS = 2
    LAST_DIFFERS = True

    def __init__(self, c, kv):
        self.c, self.kv = c, kv

    def buffers(self, sb):
        c = self.c
        self.w1 = sb("w_fc1", [P, KD, HIDDEN])
        self.w1g = self.w1
        self.x1 = sb("x1", [P, NT, D])
        self.norm = Norm(c, sb, "mixed0")
        self.b1 = sb("b_fc1", [P, KH])
        self.b1g = sb("b_fc1_all", [P, KH])
        self.w2 = sb("w_fc2", [P, KH, D])
        self.gain = sb("ln_gain", [P, KD])
        self.offset = sb("ln_offset", [P, KD])
        self.bias = sb("b_rows", [1, 3, D])
        self.z = sb("z1", [P, J, D])
        self.zt = sb("z1_cols", [P, KD, GW])
        self.u = sb("hidden", [P, KH, GW])
        (self.w_in, self.bias_product, self.w_ready, self.bias_ready, self.step, self.z_ready, self.flipped,
         self.zt_ready, self.up, self.up_taken, self.down, self.added) = c.sems(
            "mlp0", "w_in", "bias_product", "w_ready", "bias_ready", "step", "z_ready", "flipped", "zt_ready",
            "up", "up_taken", "down", "added")
        self.mixed_product, self.x1_ready = c.sems("mixed0", "product", "x1_ready")

    def first(self, eng, which):
        c, d = self.c, self.c.dram
        if which == "sync":
            eng.dma_start(self.w1[:, :, :], chunked(d["L0_mix_w_fc1"])).then_inc(self.w_in, 16)
            eng.dma_start(self.w2[:, :, :], chunked(d["L0_mix_w_fc2"])).then_inc(self.w_in, 16)
            eng.dma_start(self.bias[:, 0, :], one_row(d["L0_mix_b_fc2"])).then_inc(self.w_in, 16)
            eng.dma_start(self.bias[:, 1, :], one_row(d["L0_gnn_bias"])).then_inc(self.w_in, 16)
            with c.nc.allow_non_contiguous_dma(reason="biases as columns"):
                eng.dma_start(self.b1[:, :], columns(d["L0_mix_b_fc1"])).then_inc(self.w_in, 16)
                eng.dma_start(self.gain[:, :], columns(d["L0_mix_norm_g"])).then_inc(self.w_in, 16)
                eng.dma_start(self.offset[:, :], columns(d["L0_mix_norm_b"])).then_inc(self.w_in, 16)
        if which == "tensor":
            eng.wait_ge(self.w_in, 7 * 16)
            for f in range(KH):
                for k in range(KD):
                    last = eng.matmul(c.bank[7][:, f:f + 1], self.w1[:, k, f * P:f * P + P],
                                      self.offset[:, k:k + 1], start=(k == 0), stop=(k == KD - 1))
            last.then_inc(self.bias_product, 1)
        if which == "vector":
            eng.wait_ge(self.w_in, 7 * 16)
            eng.wait_ge(self.bias_product, 1)
            for k in range(KD):
                eng.tensor_scalar(self.w1g[:, k, :], self.w1[:, k, :], self.gain[:, k:k + 1], None, ALU.mult)
            eng.tensor_tensor(self.bias[:, 2, :], self.bias[:, 0, :], self.bias[:, 1, :], ALU.add)
            eng.tensor_tensor(self.b1g[:, :], self.b1[:, :], c.bank[7][:, 0:KH], ALU.add
                              ).then_inc(self.w_ready, 1)
            eng.sem_inc(self.flipped, 1)
            eng.sem_inc(self.added, J)

    def mixed(self, eng, which, g):
        c, kv = self.c, self.kv
        if which == "tensor":
            kv.cols.wait(eng, g, G)
            for j in range(J):
                eng.wait_ge(self.x1_ready, g * J + (j + 1 + J - reuse(j, 2)))
                bank = c.bank[j % 2][:, 0:D]
                for k in range(KD):
                    eng.matmul(bank, kv.cols.buf[:, k, j * P:j * P + P], kv.map[:, k, :], start=(k == 0), stop=False)
                eng.matmul(bank, c.ones[0:1, :], kv.row[:, :], start=False, stop=True
                           ).then_inc(self.mixed_product, 1)
            eng.wait_ge(self.mixed_product, g * J + J)
            eng.sem_inc(kv.cols.free, 1)
        if which == "scalar":
            for j in range(J):
                eng.wait_ge(self.mixed_product, g * J + (j + 1))
                eng.copy(self.x1[:, g * J + j, :], c.bank[j % 2][:, 0:D]).then_inc(self.x1_ready, 1)
            self.norm.scalar(eng, g)

    def stats(self, vec, g, j):
        vec.wait_ge(self.x1_ready, g * J + (j + 1 + J))
        vec.sem_inc(self.norm.go, 1)
        return vec.bn_stats(self.norm.stats[:, j, :], self.x1[:, g * J + j, :])

    def normalised(self, vec, g, j):
        self.norm.apply(vec, self.z[:, j, :], self.x1[:, g * J + j, :], g * J + j).then_inc(self.z_ready, 1)

    def before(self, eng, which):
        if which == "sync":
            self.kv.cols.load(eng, 0, G)
        if which == "tensor":
            eng.wait_ge(self.w_ready, 1)
            eng.wait_ge(self.kv.map_ready, 1)
            eng.sem_inc(self.down, J)
        if which == "scalar":
            eng.sem_inc(self.zt_ready, J)
            eng.sem_inc(self.x1_ready, J)
            eng.sem_inc(self.up_taken, 3)
            eng.wait_ge(self.w_ready, 1)
        self.mixed(eng, which, 0)
        if which == "vector":
            for j in range(J):
                last = self.stats(eng, 0, j)
            step = Chain(eng, self.norm.step)
            step(last)
            self.norm.moments(eng, step, 0)
            for j in range(J):
                self.normalised(eng, 0, j)

    def piece(self, eng, g, n):
        c = self.c
        if 4 <= n < 4 + J:
            t = g * J + (n - 4)
            eng.tensor_tensor(c.x[:, bass.ds(t, 1), :], c.x[:, bass.ds(t, 1), :], self.x1[:, bass.ds(t, 1), :],
                              ALU.add).then_inc(self.step, 1)
        if not isinstance(g, int):
            if n in (32, 34, 36, 38, 40):
                last = self.stats(eng, g + 1, (n - 32) // 2)
                if n == 40:
                    step = Chain(eng, self.norm.step, (g + 1) * Norm.STEPS)
                    step(last)
                    self.norm.moments(eng, step, g + 1)
            if n in (41, 42, 43, 44, 45):
                self.normalised(eng, g + 1, n - 41)
        if n in (42, 46, 50, 54, 55):
            j = (42, 46, 50, 54, 55).index(n)
            eng.wait_ge(self.step, g * J + J)
            eng.wait_ge(self.down, g * J + (j + 1 + J))
            eng.tensor_tensor(c.x[:, g * J + j, :], c.x[:, g * J + j, :], c.bank[6 + j % 2][:, 0:D], ALU.add
                              ).then_inc(self.added, 1)

    def turn(self, eng, which, g):
        c = self.c
        ups = 2 * KH
        ahead = not isinstance(g, int)
        if which == "sync" and ahead:
            self.kv.cols.load(eng, g + 1, G)
        if which == "tensor":
            for j in range(J):
                eng.wait_ge(self.z_ready, g * J + (j + 1))
                eng.wait_ge(self.zt_ready, g * J + (j + 1 + J - reuse(j, 2)))
                for k in range(KD):
                    last = eng.transpose(c.bank[j % 2][:, k * P:k * P + P], self.z[:, j, k * P:k * P + P],
                                         c.ident[:, :])
                last.then_inc(self.flipped, 1)
            eng.wait_ge(self.zt_ready, g * J + 2 * J)
            for half in range(2):
                for f in range(KH):
                    n = half * KH + f
                    eng.wait_ge(self.up_taken, g * ups + (n + 1))
                    for k in range(KD):
                        last = eng.matmul(c.bank[2 + n % 3][:, 0:HALF], self.w1g[:, k, f * P:f * P + P],
                                          self.zt[:, k, half * HALF:half * HALF + HALF], start=(k == 0),
                                          stop=(k == KD - 1))
                    last.then_inc(self.up, 1)
            if ahead:
                self.mixed(eng, which, g + 1)
            eng.wait_ge(self.up_taken, g * ups + (ups + 3))
            for j in range(J):
                bank = c.bank[6 + j % 2][:, 0:D]
                eng.wait_ge(self.added, g * J + (j + 1 + J - reuse(j, 2)))
                for f in range(KH):
                    eng.matmul(bank, self.u[:, f, j * P:j * P + P], self.w2[:, f, :], start=(f == 0), stop=False)
                eng.matmul(bank, c.ones[0:1, :], self.bias[:, 2, :], start=False, stop=True).then_inc(self.down, 1)
        if which == "scalar":
            for j in range(J):
                eng.wait_ge(self.flipped, g * J + (j + 2))
                eng.copy(self.zt[:, :, j * P:j * P + P],
                         c.bank[j % 2][:, 0:D].rearrange("p (k n) -> p k n", k=KD)).then_inc(self.zt_ready, 1)
            for half in range(2):
                for f in range(KH):
                    n = half * KH + f
                    eng.wait_ge(self.up, g * ups + (n + 1))
                    if n == 0:
                        eng.wait_ge(self.down, g * J + J)
                    eng.activation(self.u[:, f, half * HALF:half * HALF + HALF], c.bank[2 + n % 3][:, 0:HALF],
                                   ACT.Gelu, bias=self.b1g[:, f:f + 1]).then_inc(self.up_taken, 1)
            if ahead:
                self.mixed(eng, which, g + 1)


def stage(c, prefix):
    own = ExitStack()
    return own, Local(c, own, prefix)


def to_columns(pe, bank, rows, ident):
    for k in range(KD):
        last = pe.transpose(bank[:, k * P:k * P + P], rows[:, k * P:k * P + P], ident)
    return last


def split_columns(bank):
    return bank[:, 0:D].rearrange("p (k n) -> p k n", k=KD)


def fetch_nodes(c, pool, fetched, used, arrived):
    for t in range(NT):
        if t >= J:
            pool.wait_ge(used, t - J + 1)
        pool.indirect_dma_start(fetched[:, t % J, :], None, c.dram["state"][:, :],
                                bass.IndirectOffsetOnAxis(c.end_idx[:, t:t + 1], 0)
                                ).then_inc(arrived[t % J], 16)


def convolve0(c, logits):
    own, sb = stage(c, "conv0")
    with own:
        d = c.dram
        agg = sb("agg", [P, J, D])
        agg_t = sb("agg_cols", [P, J, KD, P])
        w = sb("w", [P, KD, D])
        gate = sb("gate", [P, KD, 16])
        gate_bias = sb("gate_bias", [1, 16])
        z = sb("z", [P, J, D])
        z_t = sb("z_cols", [P, J, KD, P])
        norm = Norm(c, sb, "conv0")
        agg_in = c.sems("conv0", *(f"agg_in{j}" for j in range(J)))
        w_in, flipped, agg_ready, product, added, z_ready, z_saved, z_flipped, z_cols, gated, logits_ready = c.sems(
            "conv0", "w_in", "flipped", "agg_ready", "product", "added", "z_ready", "z_saved", "z_flipped",
            "z_cols", "gated", "logits_ready")
        block = own.enter_context(c.nc.Block())

        @block.gpsimd
        def _(pool):
            fetch_nodes(c, pool, agg, flipped, agg_in)

        @block.sync
        def _(sp):
            sp.dma_start(w[:, :, :], chunked(d["L0_gnn_weight"])).then_inc(w_in, 16)
            sp.dma_start(gate[:, :, :], chunked(d["L0_ffn_gate_w"])).then_inc(w_in, 16)
            sp.dma_start(gate_bias[:, :], one_row(d["L0_ffn_gate_b"])).then_inc(w_in, 16)
            with sp.Fori(0, G) as g:
                sp.wait_ge(z_ready, g * J + J)
                sp.dma_start(group_rows(d["z2"], g), z[:, :, :]).then_inc(z_saved, 16)
            sp.wait_ge(z_saved, 16 * G + 16)

        @block.tensor
        def _(pe):
            pe.wait_ge(w_in, 3 * 16)
            with pe.Fori(0, G) as g:
                for j in range(J):
                    pe.wait_ge(agg_in[j], g * 16 + 16)
                    pe.wait_ge(agg_ready, g * J + (j + 1 + J - reuse(j, 2)))
                    to_columns(pe, c.bank[j % 2], agg[:, j, :], c.ident[:, :]).then_inc(flipped, 1)
                    pe.wait_ge(agg_ready, g * J + (j + 1 + J))
                    pe.wait_ge(added, g * J + (j + 1 + J - reuse(j, 2)))
                    for k in range(KD):
                        last = pe.matmul(c.bank[2 + j % 2][:, 0:D], agg_t[:, j, k, :], w[:, k, :],
                                         start=(k == 0), stop=(k == KD - 1))
                    last.then_inc(product, 1)
                pe.wait_ge(logits_ready, g + 1)
                for j in range(J):
                    pe.wait_ge(z_ready, g * J + (j + 1))
                    pe.wait_ge(z_cols, g * J + (j + 1 + J - reuse(j, 2)))
                    to_columns(pe, c.bank[4 + j % 2], z[:, j, :], c.ident[:, :]).then_inc(z_flipped, 1)
                    pe.wait_ge(z_cols, g * J + (j + 1 + J))
                    out = c.bank[6][:, j * 16:j * 16 + 16]
                    for k in range(KD):
                        pe.matmul(out, z_t[:, j, k, :], gate[:, k, :], start=(k == 0), stop=False)
                    pe.matmul(out, c.ones[0:1, :], gate_bias[:, :], start=False, stop=True).then_inc(gated, 1)

        @block.scalar
        def _(act):
            act.sem_inc(agg_ready, J)
            act.sem_inc(z_cols, J)
            act.sem_inc(logits_ready, 1)
            with act.Fori(0, G) as g:
                for j in range(J):
                    act.wait_ge(flipped, g * J + (j + 1))
                    act.copy(agg_t[:, j, :, :], split_columns(c.bank[j % 2])).then_inc(agg_ready, 1)
                norm.scalar(act, g)
                for j in range(J):
                    act.wait_ge(z_flipped, g * J + (j + 1))
                    act.copy(z_t[:, j, :, :], split_columns(c.bank[4 + j % 2])).then_inc(z_cols, 1)
                act.wait_ge(gated, g * J + J)
                act.copy(logits[:, bass.ds(g * J, J), :], c.bank[6][:, 0:J * 16].rearrange("p (j e) -> p j e", j=J)
                         ).then_inc(logits_ready, 1)

        @block.vector
        def _(vec):
            vec.sem_inc(added, J)
            vec.sem_inc(z_saved, 16)
            with vec.Fori(0, G) as g:
                for j in range(J):
                    vec.wait_ge(product, g * J + (j + 1))
                    vec.tensor_tensor(c.x[:, g * J + j, :], c.x[:, g * J + j, :], c.bank[2 + j % 2][:, 0:D],
                                      ALU.add).then_inc(added, 1)
                vec.wait_ge(added, g * J + 2 * J)
                norm.vector(vec, g, lambda j: c.x[:, g * J + j, :])
                vec.wait_ge(z_saved, g * 16 + 16)
                for j in range(J):
                    norm.apply(vec, z[:, j, :], c.x[:, g * J + j, :], g * J + j).then_inc(z_ready, 1)


B = 8


def places(experts):
    n = (2 * N + experts * (P - 1)) // P
    return n + -n % B


class Routes:

    def __init__(self, c, sb, experts, places):
        self.experts, self.tiles = experts, places
        self.logits = sb("logits", [P, NT, experts])
        self.weight = sb("weight", [P, 2, NT])
        self.combine = sb("combine", [P, NT, experts])
        self.read_idx = sb("read_idx", [P, places + B], U32)
        self.write_idx = sb("write_idx", [P, places + B], U32)
        self.tile_expert = sb("tile_expert", [P, places + B], I32)


def route(c, r, name, all_softmax):
    X, T = r.experts, r.tiles
    own, sb = stage(c, name)
    with own:
        top = sb("top", [P, NT, 8])
        top_i = sb("top_i", [P, NT, 8], U32)
        e_no = sb("e_no", [P, X])
        pick_f = sb("pick_f", [P, 2, NT])
        second = sb("second", [P, NT])
        total = sb("total", [P, NT])
        exps = sb("exps", [P, NT, X])
        pick = [sb(f"pick{k}", [P, X, NT]) for k in range(2)]
        both = sb("both", [P, X, NT])
        keep = sb("same_expert", [P, X, NT])
        running = sb("running", [P, X, NT])
        place = sb("place", [P, X, NT])
        tiles = sb("tiles", [P, 4, X])
        slot = sb("slot", [P, 2, NT])
        high = sb("high", [P, 2, NT])
        low = sb("low", [P, 2, NT])
        value_i = sb("value_i", [P, 2, NT], I32)
        value = sb("value", [P, 2, NT])
        up = sb("up", [P, P])
        is_low = sb("is_low", [P, 2 * NT, P])
        is_high = sb("is_high", [P, 2 * NT, T])
        spare_i = sb("spare_i", [P, T], I32)
        v = [sb(f"v{i}", [P, T]) for i in range(4)]
        at_least = sb("at_least", [P, T + B, X])
        tile_f = sb("tile_f", [P, T + B])
        step_sem, made, exp_go, exp_done, picked, ranked, hot, listed = c.sems(
            name, "step", "made", "exp_go", "exp_done", "picked", "ranked", "hot", "listed")
        block = own.enter_context(c.nc.Block())
        ranks = c.bank[0][:, 0:X * NT]
        totals = c.bank[1][:, 0:X * NT]
        inverse = c.bank[2][:, 0:T]

        def flat(ap):
            return ap[:, :, :].rearrange("p a b -> p (a b)")

        @block.gpsimd
        def _(pool):
            pool.memset(keep[:, :, :], 1.0)
            pool.iota(value_i[:, :, :], pattern=[[NP, 2], [P, NT]], base=1, channel_multiplier=1)
            pool.iota(spare_i[:, :], pattern=[[P, T]], base=2 * NP, channel_multiplier=1).then_inc(made, 1)
            pool.wait_ge(made, 1)
            pool.memset(keep[:, :, 0:1], 0.0).then_inc(made, 1)

        @block.scalar
        def _(act):
            act.wait_ge(exp_go, 1)
            act.activation(exps[:, :, :], exps[:, :, :], ACT.Exp).then_inc(exp_done, 1)

        @block.vector
        def _(vec):
            step = Chain(vec, step_sem)
            vec.tensor_copy(e_no[:, :], c.count_up[:, 0:X])
            vec.tensor_copy(up[:, :], c.count_up[:, :])
            vec.wait_ge(made, 2)
            vec.tensor_copy(value[:, :, :], value_i[:, :, :])
            for t in range(NT):
                last = vec.max(top[:, t, :], r.logits[:, t, :])
            step(last)
            for t in range(NT):
                last = vec.max_index(top_i[:, t, :], top[:, t, :], r.logits[:, t, :])
            step(last)
            vec.tensor_tensor(exps[:, :, :], r.logits[:, :, :], top[:, :, 0:1].to_broadcast([P, NT, X]),
                              ALU.subtract).then_inc(exp_go, 1)
            for k in range(2):
                last = vec.tensor_copy(pick_f[:, k, :], top_i[:, :, k])
            step(last)
            for k in range(2):
                step(vec.tensor_tensor(pick[k][:, :, :], e_no[:, :].unsqueeze(2).to_broadcast([P, X, NT]),
                                       pick_f[:, k, :].unsqueeze(1).to_broadcast([P, X, NT]), ALU.is_equal))
                step(vec.tensor_tensor(pick[k][:, :, :], pick[k][:, :, :],
                                       c.real[:, :].unsqueeze(1).to_broadcast([P, X, NT]), ALU.mult))
            vec.tensor_tensor(both[:, :, :], pick[0][:, :, :], pick[1][:, :, :], ALU.add).then_inc(picked, 1)
            vec.wait_ge(exp_done, 1)
            step(vec.tensor_tensor(place[:, :, :], pick[1][:, :, :], exps[:, :, :].rearrange("p t e -> p e t"),
                                   ALU.mult))
            step(vec.tensor_reduce(second[:, :], place[:, :, :].rearrange("p e t -> p t e"), AX.X, ALU.add))
            w = r.weight
            if all_softmax:
                step(vec.tensor_reduce(total[:, :], exps[:, :, :], AX.X, ALU.add))
                step(vec.reciprocal(total[:, :], total[:, :]))
                step(vec.tensor_tensor(second[:, :], second[:, :], total[:, :], ALU.mult))
                step(vec.tensor_tensor(w[:, 1, :], second[:, :], total[:, :], ALU.add))
                step(vec.tensor_scalar(w[:, 1, :], w[:, 1, :], 1e-12, None, ALU.max))
                step(vec.reciprocal(w[:, 1, :], w[:, 1, :]))
                step(vec.tensor_tensor(w[:, 0, :], total[:, :], w[:, 1, :], ALU.mult))
                step(vec.tensor_tensor(w[:, 1, :], second[:, :], w[:, 1, :], ALU.mult))
            else:
                step(vec.tensor_scalar(total[:, :], second[:, :], 1.0, None, ALU.add))
                step(vec.reciprocal(w[:, 0, :], total[:, :]))
                step(vec.tensor_tensor(w[:, 1, :], second[:, :], w[:, 0, :], ALU.mult))
            cp = r.combine[:, :, :].rearrange("p t e -> p e t")
            step(vec.tensor_tensor(cp, pick[0][:, :, :], w[:, 0, :].unsqueeze(1).to_broadcast([P, X, NT]), ALU.mult))
            step(vec.tensor_tensor(place[:, :, :], pick[1][:, :, :],
                                   w[:, 1, :].unsqueeze(1).to_broadcast([P, X, NT]), ALU.mult))
            step(vec.tensor_tensor(cp, cp, place[:, :, :], ALU.add))
            vec.wait_ge(ranked, 1)
            step(vec.tensor_tensor_scan(flat(running), flat(keep), totals, 0.0, ALU.mult, ALU.add))
            t = tiles
            step(vec.tensor_scalar(t[:, 0, :], running[:, :, NT - 1], (P - 1) / 2.0, 1.0 / P, ALU.add, ALU.mult))
            step(vec.tensor_scalar(t[:, 1, :], t[:, 0, :], ROUND, None, ALU.add))
            step(vec.tensor_scalar(t[:, 0, :], t[:, 1, :], -ROUND, None, ALU.add))
            step(vec.tensor_tensor_scan(t[:, 1, :], c.ones[:, 0:X], t[:, 0, :], 0.0, ALU.mult, ALU.add))
            step(vec.tensor_tensor(t[:, 2, :], t[:, 1, :], t[:, 0, :], ALU.subtract))
            step(vec.tensor_scalar(t[:, 3, :], t[:, 2, :], float(P), None, ALU.mult))
            step(vec.tensor_tensor(flat(running), flat(running), totals, ALU.subtract))
            step(vec.tensor_tensor(flat(running), flat(running), ranks, ALU.add))
            step(vec.tensor_tensor(running[:, :, :], running[:, :, :],
                                   t[:, 3, :].unsqueeze(2).to_broadcast([P, X, NT]), ALU.add))
            for k in range(2):
                step(vec.tensor_tensor(place[:, :, :], pick[k][:, :, :], running[:, :, :], ALU.mult))
                step(vec.tensor_reduce(slot[:, k, :], place[:, :, :].rearrange("p e t -> p t e"), AX.X, ALU.add))
            step(vec.tensor_scalar(high[:, :, :], slot[:, :, :], -(P - 1) / 2.0, 1.0 / P, ALU.add, ALU.mult))
            step(vec.tensor_scalar(low[:, :, :], high[:, :, :], ROUND, None, ALU.add))
            step(vec.tensor_scalar(high[:, :, :], low[:, :, :], -ROUND, None, ALU.add))
            step(vec.scalar_tensor_tensor(out=low[:, :, :], in0=high[:, :, :], scalar=-float(P), in1=slot[:, :, :],
                                          op0=ALU.mult, op1=ALU.add))
            step(vec.tensor_tensor(value[:, :, :], value[:, :, :], c.real[:, :].unsqueeze(1).to_broadcast([P, 2, NT]),
                                   ALU.mult))
            vec.tensor_tensor(is_low[:, :, :], flat(low).unsqueeze(2).to_broadcast([P, 2 * NT, P]),
                              up[:, :].unsqueeze(1).to_broadcast([P, 2 * NT, P]), ALU.is_equal)
            step(vec.tensor_tensor(is_high[:, :, :], flat(high).unsqueeze(2).to_broadcast([P, 2 * NT, T]),
                                   up[:, 0:T].unsqueeze(1).to_broadcast([P, 2 * NT, T]), ALU.is_equal))
            vec.tensor_tensor(is_high[:, :, :], is_high[:, :, :], flat(value).unsqueeze(2).to_broadcast([P, 2 * NT, T]),
                              ALU.mult).then_inc(hot, 1)
            step(vec.tensor_tensor(at_least[:, 0:T, :], up[:, 0:T].unsqueeze(2).to_broadcast([P, T, X]),
                                   t[:, 1, :].unsqueeze(1).to_broadcast([P, T, X]), ALU.is_ge))
            step(vec.memset(tile_f[:, :], 0.0))
            step(vec.tensor_reduce(tile_f[:, 0:T], at_least[:, 0:T, :], AX.X, ALU.add))
            step(vec.tensor_scalar(tile_f[:, :], tile_f[:, :], float(X - 1), None, ALU.min))
            step(vec.tensor_copy(r.tile_expert[:, :], tile_f[:, :]))
            vec.memset(r.read_idx[:, T:], 0)
            vec.memset(r.write_idx[:, T:], 2 * NP)
            vec.wait_ge(listed, 1)
            filled, place_no, is_second, spare = v
            step(vec.tensor_scalar(filled[:, :], inverse, 0.0, None, ALU.is_gt))
            step(vec.tensor_scalar(place_no[:, :], inverse, -1.0, None, ALU.add))
            step(vec.tensor_scalar(is_second[:, :], place_no[:, :], float(NP), -float(NP), ALU.is_ge, ALU.mult))
            step(vec.tensor_tensor(is_second[:, :], is_second[:, :], place_no[:, :], ALU.add))
            step(vec.tensor_tensor(is_second[:, :], is_second[:, :], filled[:, :], ALU.mult))
            step(vec.tensor_copy(r.read_idx[:, 0:T], is_second[:, :]))
            step(vec.tensor_copy(spare[:, :], spare_i[:, :]))
            step(vec.tensor_tensor(place_no[:, :], place_no[:, :], spare[:, :], ALU.subtract))
            step(vec.tensor_tensor(place_no[:, :], place_no[:, :], filled[:, :], ALU.mult))
            step(vec.tensor_tensor(place_no[:, :], place_no[:, :], spare[:, :], ALU.add))
            step(vec.tensor_copy(r.write_idx[:, 0:T], place_no[:, :]))

        @block.tensor
        def _(pe):
            pe.wait_ge(picked, 1)
            pe.matmul(ranks, c.upper[:, :], flat(both), start=True, stop=True)
            pe.matmul(totals, c.ones[:, :], flat(both), start=True, stop=True).then_inc(ranked, 1)
            pe.wait_ge(hot, 1)
            for n in range(2 * NT):
                last = pe.matmul(inverse, is_low[:, n, :], is_high[:, n, :], start=(n == 0), stop=(n == 2 * NT - 1))
            last.then_inc(listed, 1)


def experts(c, r, name, table, w1, b1, w2, act_func):
    X, T = r.experts, r.tiles
    F = w1.shape[2]
    KF = F // P
    assert T % B == 0
    own, sb = stage(c, name)
    with own:
        rows = sb("rows", [P, B, D])
        cols = sb("cols", [P, 2, KD, P])
        up_w = sb("up_w", [P, 2, KD, F])
        up_b = sb("up_b", [P, 2, KF])
        down_w = sb("down_w", [P, 2, KF, D])
        hidden = sb("hidden", [P, 2, KF, P])
        result = sb("result", [P, B, D])
        idx = sb("idx", [P, 2, B], U32)
        first_sent = sb("first_sent", [1, B])
        arrived = c.sems(name, *(f"arrived{q}" for q in range(B)))
        sent = c.sems(name, *(f"sent{q}" for q in range(B)))
        up_in = c.sems(name, "up_in0", "up_in1")
        up_b_in = c.sems(name, "up_b_in0", "up_b_in1")
        down_in = c.sems(name, "down_in0", "down_in1")
        staged, go, flipped, cols_ready, up, hidden_ready, down, result_ready = c.sems(
            name, "staged", "go", "flipped", "cols_ready", "up", "hidden_ready", "down", "result_ready")
        passed = c.sem(f"{name}_passed")
        block = own.enter_context(c.nc.Block())
        out = c.dram["expert_out"]
        turns = T // B
        table_w1 = w1.rearrange("e (k p) f -> e p k f", p=P)
        table_w2 = w2.rearrange("e (k p) d -> e p k d", p=P)

        @block.gpsimd
        def _(pool):
            def gather(q):
                pool.indirect_dma_start(rows[:, q, :], None, table[:, :],
                                        bass.IndirectOffsetOnAxis(idx[:, 0, q:q + 1], 0)).then_inc(arrived[q], 16)

            for q in range(B):
                pool.dma_start(first_sent[0:1, q:q + 1], c.eps[0:1, 0:1]).then_inc(sent[q], 16)
            pool.tensor_copy(idx[:, 0, :], r.read_idx[:, 0:B]).then_inc(staged, 1)
            pool.wait_ge(staged, 1)
            for q in range(B):
                gather(q)
            with pool.Fori(0, turns) as i:
                for q in range(B):
                    pool.wait_ge(arrived[q], i * 16 + 16)
                    pool.wait_ge(sent[q], i * 16 + 16)
                pool.sem_inc(go, 1)
                pool.tensor_copy(idx[:, 0, :], r.read_idx[:, bass.ds(i * B + B, B)])
                pool.tensor_copy(idx[:, 1, :], r.write_idx[:, bass.ds(i * B, B)]).then_inc(staged, 1)
                pool.wait_ge(staged, i + 2)
                for q in range(B):
                    pool.wait_ge(flipped, i * B + (q + 1))
                    pool.sem_inc(go, 1)
                    gather(q)
                    pool.wait_ge(result_ready, i * B + (q + 3))
                    pool.sem_inc(go, 1)
                    pool.indirect_dma_start(out[:, :], bass.IndirectOffsetOnAxis(idx[:, 1, q:q + 1], 0),
                                            result[:, q, :], None).then_inc(sent[q], 16)
            for q in range(B):
                pool.wait_ge(sent[q], turns * 16 + 16)
                pool.wait_ge(arrived[q], turns * 16 + 16)

        @block.sync
        def _(sp):
            def load(n, i, q):
                e = sp.value_load(r.tile_expert[0:1, bass.ds(n, 1)], min_val=0, max_val=X - 1)
                b = q % 2
                if i is not None:
                    sp.wait_ge(up, i * B + (q + 1))
                sp.dma_start(up_w[:, b, :, :], table_w1[e]).then_inc(up_in[b], 16)
                if i is not None:
                    sp.wait_ge(hidden_ready, i * B + (q + 2))
                sp.dma_start(up_b[:, b, :], b1[e]).then_inc(up_b_in[b], 16)
                if i is not None:
                    sp.wait_ge(down, i * B + (q + 2))
                sp.dma_start(down_w[:, b, :, :], table_w2[e]).then_inc(down_in[b], 16)

            load(0, None, 0)
            load(1, None, 1)
            with sp.Fori(0, turns) as i:
                for q in range(B):
                    load(i * B + (q + 2), i, q)
            for b in range(2):
                for weights in (up_in[b], up_b_in[b], down_in[b]):
                    sp.wait_ge(weights, 16 * (T // 2 + 1))

        @block.tensor
        def _(pe):
            def flip(q, arrivals, copies):
                pe.wait_ge(arrived[q % B], arrivals)
                if copies is not None:
                    pe.wait_ge(cols_ready, copies)
                to_columns(pe, c.bank[q % 2], rows[:, q % B, :], c.ident[:, :]).then_inc(flipped, 1)

            def first(q, n, weights):
                b = q % 2
                pe.wait_ge(up_in[b], weights)
                pe.wait_ge(cols_ready, n + 1)
                if not (isinstance(n, int) and n == 0):
                    pe.wait_ge(hidden_ready, n)
                for f in range(KF):
                    for k in range(KD):
                        last = pe.matmul(c.bank[2 + b][:, f * P:f * P + P], up_w[:, b, k, f * P:f * P + P],
                                         cols[:, b, k, :], start=(k == 0), stop=(k == KD - 1))
                last.then_inc(up, 1)

            flip(0, 16, None)
            flip(1, 16, None)
            first(0, 0, 16)
            with pe.Fori(0, turns) as i:
                for q in range(B):
                    b = q % 2
                    flip(q + 2, i * 16 + (32 if q + 2 >= B else 16), i * B + (q + 1))
                    first(q + 1, i * B + (q + 1), i * (8 * B) + 16 * ((q + 1) // 2 + 1))
                    pe.wait_ge(down_in[b], i * (8 * B) + 16 * (q // 2 + 1))
                    pe.wait_ge(hidden_ready, i * B + (q + 2))
                    pe.wait_ge(result_ready, i * B + (q + 1))
                    for f in range(KF):
                        last = pe.matmul(c.bank[4 + b][:, 0:D], hidden[:, b, f, :], down_w[:, b, f, :],
                                         start=(f == 0), stop=(f == KF - 1))
                    last.then_inc(down, 1)

        @block.scalar
        def _(act):
            def unit(q, n, biases):
                b = q % 2
                act.wait_ge(up_b_in[b], biases)
                act.wait_ge(up, n + 1)
                if not (isinstance(n, int) and n == 0):
                    act.wait_ge(down, n)
                    act.sem_inc(passed, 1)
                for f in range(KF):
                    last = act.activation(hidden[:, b, f, :], c.bank[2 + b][:, f * P:f * P + P], act_func,
                                          bias=up_b[:, b, f:f + 1])
                last.then_inc(hidden_ready, 1)

            act.sem_inc(hidden_ready, 1)
            unit(0, 0, 16)
            with act.Fori(0, turns) as i:
                for q in range(B):
                    unit(q + 1, i * B + (q + 1), i * (8 * B) + 16 * ((q + 1) // 2 + 1))

        @block.vector
        def _(vec):
            vec.sem_inc(down, 1)
            vec.sem_inc(result_ready, 2)
            for q in range(2):
                vec.wait_ge(flipped, q + 1)
                vec.tensor_copy(cols[:, q, :, :], split_columns(c.bank[q])).then_inc(cols_ready, 1)
            with vec.Fori(0, turns) as i:
                for q in range(B):
                    b = q % 2
                    vec.wait_ge(flipped, i * B + (q + 3))
                    vec.wait_ge(up, i * B + (q + 1))
                    vec.tensor_copy(cols[:, b, :, :], split_columns(c.bank[b])).then_inc(cols_ready, 1)
                    vec.wait_ge(sent[q], i * 16 + 16)
                    vec.wait_ge(down, i * B + (q + 2))
                    vec.tensor_copy(result[:, q, :], c.bank[4 + b][:, 0:D]).then_inc(result_ready, 1)


class ExpertSum:

    def __init__(self, c, r, sb, name, table, bias):
        self.c, self.r, self.table, self.bias_table = c, r, table, bias
        X = r.experts
        self.z = sb("z_in", [P, J, D])
        self.y = sb("y_in", [P, 2, J, D])
        self.shares = sb("shares", [P, J, X])
        self.shares_t = sb("shares_t", [X, J, P])
        self.bias = sb("expert_bias", [X, D])
        self.total = sb("total", [P, J, D])
        (self.bias_in, self.rows_in, self.used, self.shares_ready, self.flipped, self.shares_t_ready,
         self.product, self.step, self.summed) = c.sems(
            name, "bias_in", "rows_in", "rows_used", "shares_ready", "shares_flipped", "shares_t_ready",
            "bias_product", "sum_step", "summed")

    def sync(self, sp, g):
        sp.wait_ge(self.used, g * J + 1)
        sp.dma_start(self.z[:, :, :], group_rows(self.table, g)).then_inc(self.rows_in, 16)
        for k in range(2):
            half = self.c.dram["expert_out"][k * NP:k * NP + NP, :]
            sp.dma_start(self.y[:, k, :, :], group_rows(half, g)).then_inc(self.rows_in, 16)

    def sync_first(self, sp):
        sp.dma_start(self.bias[:, :], self.bias_table).then_inc(self.bias_in, 16)

    def pool(self, pool, g):
        pool.wait_ge(self.flipped, g * J + 1)
        pool.sem_inc(self.step, 1)
        pool.tensor_copy(self.shares[:, :, :], self.r.combine[:, bass.ds(g * J, J), :]).then_inc(self.shares_ready, 1)

    def tensor(self, pe, g, banks):
        c, X = self.c, self.r.experts
        pe.wait_ge(self.shares_ready, g + 1)
        pe.wait_ge(self.shares_t_ready, g + 1)
        for j in range(J):
            pe.transpose(c.bank[banks[0]][0:X, (j % 4) * P:(j % 4) * P + P] if j < 4 else
                         c.bank[banks[3]][0:X, 0:P], self.shares[:, j, :], c.ident[:, :]).then_inc(self.flipped, 1)
        pe.wait_ge(self.shares_t_ready, g + 2)
        for j in range(J):
            pe.wait_ge(self.summed, g * J + (j + 1 + J - reuse(j, 2)))
            pe.matmul(c.bank[banks[1 + j % 2]][:, D:2 * D], self.shares_t[:, j, :], self.bias[:, :], start=True,
                      stop=True).then_inc(self.product, 1)

    def scalar(self, act, g, banks):
        c, X = self.c, self.r.experts
        act.wait_ge(self.flipped, g * J + J + 1)
        act.wait_ge(self.product, g * J + 1)
        act.copy(self.shares_t[:, 0:4, :], c.bank[banks[0]][0:X, :].rearrange("p (j n) -> p j n", j=4))
        act.copy(self.shares_t[:, 4, :], c.bank[banks[3]][0:X, 0:P]).then_inc(self.shares_t_ready, 1)

    def open(self, eng):
        eng.sem_inc(self.used, 1)
        eng.sem_inc(self.flipped, 1)
        eng.sem_inc(self.shares_t_ready, 1)
        eng.sem_inc(self.summed, J)
        eng.sem_inc(self.product, 1)

    STEPS = 2 * J

    def vector(self, vec, g, chain_sem, banks):
        c, w = self.c, self.r.weight
        vec.wait_ge(self.rows_in, g * 48 + 48)
        for k in range(2):
            for j in range(J):
                vec.scalar_tensor_tensor(out=self.total[:, j, :], in0=self.y[:, k, j, :],
                                         scalar=w[:, k, bass.ds(g * J + j, 1)],
                                         in1=self.z[:, j, :] if k == 0 else self.total[:, j, :],
                                         op0=ALU.mult, op1=ALU.add).then_inc(chain_sem if k == 0 else self.used, 1)
            if k == 0:
                vec.wait_ge(chain_sem, g * J + J)
        vec.wait_ge(self.used, g * J + J + 1)
        for j in range(J):
            vec.wait_ge(self.product, g * J + (j + 2))
            vec.tensor_tensor(self.total[:, j, :], self.total[:, j, :], c.bank[banks[1 + j % 2]][:, D:2 * D],
                              ALU.add).then_inc(self.summed, 1)
        vec.wait_ge(self.summed, g * J + 2 * J)


def finish_layer0(c, r):
    own, sb = stage(c, "finish0")
    with own:
        d = c.dram
        es = ExpertSum(c, r, sb, "sum0", d["z2"], d["L0_ffn_b2"])
        norm_a, norm_b = Norm(c, sb, "finish0a"), Norm(c, sb, "finish0b")
        gamma = sb("gamma", [P, D])
        beta = sb("beta", [P, D])
        w = sb("w", [P, KD, D])
        b = sb("b", [1, D])
        y = sb("y", [P, J, D])
        xb = sb("x_beta", [P, J, D])
        z = sb("z", [P, J, D])
        zt = sb("z_cols", [P, KD, GW])
        h = sb("h", [P, J, D])
        (w_in, y_ready, xb_ready, y_used, x_ready, z_ready, flipped, zt_ready, zt_saved, product, h_ready,
         h_saved, step) = c.sems(
            "finish0", "w_in", "y_ready", "xb_ready", "y_used", "x_ready", "z_ready", "flipped", "zt_ready",
            "zt_saved", "product", "h_ready", "h_saved", "step")
        passed = [c.sem(f"finish0_passed{i}") for i in range(3)]
        banks = (0, 1, 2, 3)
        block = own.enter_context(c.nc.Block())

        @block.sync
        def _(sp):
            es.sync_first(sp)
            sp.dma_start(w[:, :, :], chunked(d["w_p1_t"])).then_inc(w_in, 16)
            sp.dma_start(b[:, :], one_row(d["L1_gnn_bp1"])).then_inc(w_in, 16)
            sp.dma_start(gamma[:, :], all_rows(d["L0_ffn_gamma"])).then_inc(w_in, 16)
            sp.dma_start(beta[:, :], all_rows(d["L0_ffn_beta"])).then_inc(w_in, 16)
            es.sync(sp, 0)
            with sp.Fori(0, G - 1) as g:
                es.sync(sp, g + 1)
                sp.wait_ge(zt_ready, g * J + 2 * J)
                sp.dma_start(d["z3_cols"][:, :, bass.ds(g * GW, GW)], zt[:, :, :]).then_inc(zt_saved, 16)
                sp.wait_ge(h_ready, g * J + 2 * J)
                sp.dma_start(group_rows(d["h"], g), h[:, :, :]).then_inc(h_saved, 16)
            sp.wait_ge(zt_ready, G * J + J)
            sp.dma_start(d["z3_cols"][:, :, NP - GW:], zt[:, :, :]).then_inc(zt_saved, 16)
            sp.wait_ge(h_ready, G * J + J)
            sp.dma_start(group_rows(d["h"], G - 1), h[:, :, :]).then_inc(h_saved, 16)
            sp.wait_ge(zt_saved, 16 * G + 16)
            sp.wait_ge(h_saved, 16 * G + 16)

        @block.gpsimd
        def _(pool):
            pool.wait_ge(w_in, 4 * 16)
            with pool.Fori(0, G) as g:
                es.pool(pool, g)
                pool.wait_ge(x_ready, g + 1)
                pool.sem_inc(passed[0], 1)
                pool.tensor_tensor(xb[:, :, :], c.x[:, bass.ds(g * J, J), :],
                                   beta[:, :].unsqueeze(1).to_broadcast([P, J, D]), ALU.add).then_inc(xb_ready, 1)

        @block.tensor
        def _(pe):
            pe.wait_ge(w_in, 4 * 16)
            pe.wait_ge(es.bias_in, 16)
            es.open(pe)
            with pe.Fori(0, G) as g:
                es.tensor(pe, g, banks)

                def flip(j):
                    pe.wait_ge(z_ready, g * J + (j + 1))
                    pe.wait_ge(zt_ready, g * J + (j + 1 + J - reuse(j, 2)))
                    to_columns(pe, c.bank[4 + j % 2], z[:, j, :], c.ident[:, :]).then_inc(flipped, 1)

                flip(0)
                for j in range(J):
                    if j + 1 < J:
                        flip(j + 1)
                    pe.wait_ge(zt_ready, g * J + (j + 1 + J))
                    pe.wait_ge(h_ready, g * J + (j + 1 + J - reuse(j, 2)))
                    out = c.bank[6 + j % 2][:, 0:D]
                    for k in range(KD):
                        pe.matmul(out, zt[:, k, j * P:j * P + P], w[:, k, :], start=(k == 0), stop=False)
                    pe.matmul(out, c.ones[0:1, :], b[:, :], start=False, stop=True).then_inc(product, 1)

        @block.scalar
        def _(act):
            act.sem_inc(zt_ready, J)
            act.sem_inc(h_ready, J)
            act.sem_inc(zt_saved, 16)
            act.sem_inc(h_saved, 16)
            with act.Fori(0, G) as g:
                es.scalar(act, g, banks)
                norm_a.scalar(act, g)
                act.wait_ge(norm_a.step, g * Norm.STEPS + Norm.STEPS)
                for j in range(J):
                    norm_a.apply_act(act, y[:, j, :], es.total[:, j, :], g * J + j).then_inc(y_ready, 1)
                norm_b.scalar(act, g)
                act.wait_ge(norm_b.step, g * Norm.STEPS + Norm.STEPS)
                for j in range(J):
                    norm_b.apply_act(act, z[:, j, :], c.x[:, g * J + j, :], g * J + j).then_inc(z_ready, 1)
                act.wait_ge(zt_saved, g * 16 + 16)
                act.wait_ge(h_saved, g * 16 + 16)

                def columns_of(j):
                    act.wait_ge(flipped, g * J + (j + 1))
                    act.copy(zt[:, :, j * P:j * P + P], split_columns(c.bank[4 + j % 2])).then_inc(zt_ready, 1)

                columns_of(0)
                for j in range(J):
                    if j + 1 < J:
                        columns_of(j + 1)
                    act.wait_ge(product, g * J + (j + 1))
                    act.activation(h[:, j, :], c.bank[6 + j % 2][:, 0:D], ACT.Relu).then_inc(h_ready, 1)

        @block.vector
        def _(vec):
            vec.wait_ge(w_in, 4 * 16)
            vec.sem_inc(x_ready, 1)
            with vec.Fori(0, G) as g:
                es.vector(vec, g, step, banks)
                norm_a.vector(vec, g, lambda j: es.total[:, j, :])
                vec.wait_ge(y_ready, g * J + J)
                vec.tensor_tensor(y[:, :, :], y[:, :, :], gamma[:, :].unsqueeze(1).to_broadcast([P, J, D]),
                                  ALU.mult).then_inc(y_used, 1)
                vec.wait_ge(y_used, g + 1)
                vec.wait_ge(xb_ready, g + 1)
                vec.tensor_tensor(c.x[:, bass.ds(g * J, J), :], y[:, :, :], xb[:, :, :], ALU.add
                                  ).then_inc(x_ready, 1)
                vec.wait_ge(x_ready, g + 2)
                norm_b.vector(vec, g, lambda j: c.x[:, g * J + j, :])


class KeyValue1(Work):

    W = P + PER1

    def __init__(self, c):
        self.c = c

    def buffers(self, sb):
        c = self.c
        self.cols = Columns(c, sb, "mix1", c.dram["z3_cols"])
        self.w = sb("w_kv", [P, KD, 2 * D])
        self.bias = sb("b_kv", [P, 2 * D])
        self.raw = sb("kv_raw", [P, 2, 2 * D])
        self.low = sb("k_low", [P, 2, D])
        self.key = sb("key", [P, 2, D])
        self.value = sb("value", [P, 2, KD, P + 1])
        self.zero = sb("zeros", [P, KD * (P + 1)])
        self.map = sb("map", [P, KD, self.W])
        self.sums = c.bank[2][:, 0:KD * (P + 1)]
        (self.w_in, self.made, self.product, self.rows, self.low_ready, self.exp_ready, self.key_ready,
         self.value_ready, self.used, self.closed, self.map_ready, self.step) = c.sems(
            "kv1", "w_in", "made", "product", "rows", "low_ready", "exp_ready", "key_ready", "value_ready", "used",
            "closed", "map_ready", "step")

    def first(self, eng, which):
        c, d = self.c, self.c.dram
        if which == "sync":
            eng.dma_start(self.w[:, :, 0:D], chunked(d["L1_mix_wk"])).then_inc(self.w_in, 16)
            eng.dma_start(self.w[:, :, D:], chunked(d["L1_mix_wv"])).then_inc(self.w_in, 16)
            eng.dma_start(self.bias[:, 0:D], all_rows(d["L1_mix_bk"])).then_inc(self.w_in, 16)
            eng.dma_start(self.bias[:, D:], all_rows(d["L1_mix_bv"])).then_inc(self.w_in, 16)
        if which == "vector":
            eng.memset(self.map[:, :, :], 0.0)
            eng.memset(self.zero[:, :], 0.0).then_inc(self.made, 1)
            eng.wait_ge(self.w_in, 4 * 16)
            eng.sem_inc(self.rows, J)
        if which == "scalar":
            eng.sem_inc(self.value_ready, J)
        if which == "tensor":
            self.cols.open(eng)
            eng.wait_ge(self.w_in, 4 * 16)
            eng.wait_ge(self.made, 1)
            eng.matmul(self.sums, self.zero[:, 0:P], self.zero[:, :], start=True, stop=False,
                       skip_group_check=True)
            eng.sem_inc(self.used, J)

    def turn(self, eng, which, g):
        c = self.c
        if which == "sync":
            self.cols.load(eng, g, 0)
        if which == "tensor":
            self.cols.wait(eng, g, 0)

            def product(j):
                eng.wait_ge(self.rows, g * J + (j + 1 + J - reuse(j, 2)))
                for k in range(KD):
                    last = eng.matmul(c.bank[j % 2][:, :], self.cols.buf[:, k, j * P:j * P + P],
                                      self.w[:, k, :], start=(k == 0), stop=(k == KD - 1))
                last.then_inc(self.product, 1)

            product(0)
            for j in range(J):
                if j + 1 < J:
                    product(j + 1)
                eng.wait_ge(self.key_ready, g * J + (j + 1))
                eng.wait_ge(self.value_ready, g * J + (j + 1 + J))
                for k in range(KD):
                    last = eng.matmul(self.sums[:, k * (P + 1):(k + 1) * (P + 1)], self.key[:, j % 2, k * P:k * P + P],
                                      self.value[:, j % 2, k, :], start=False, stop=False, skip_group_check=True)
                last.then_inc(self.used, 1)
            eng.wait_ge(self.product, g * J + J)
            eng.sem_inc(self.cols.free, 1)
        if which == "scalar":
            for j in range(J):
                s = j % 2
                eng.wait_ge(self.low_ready, g * J + (j + 1))
                eng.activation(self.low[:, s, :], self.low[:, s, :], ACT.Exp).then_inc(self.exp_ready, 1)
                real = c.real[:, bass.ds(g * J + j, 1)]
                eng.activation(self.value[:, s, :, 0:P], self.raw[:, s, D:].rearrange("p (k n) -> p k n", k=KD),
                               ACT.Copy, scale=real)
                for k in range(KD):
                    last = eng.copy(self.value[:, s, k, P:P + 1], real)
                last.then_inc(self.value_ready, 1)

    def piece(self, eng, g, n):
        c = self.c
        if n % 5 == 2 and n // 5 < J:
            j = n // 5
            eng.wait_ge(self.product, g * J + (j + 1))
            eng.wait_ge(self.used, g * J + (j + 1 + J - reuse(j, 2)))
            eng.tensor_tensor(self.raw[:, j % 2, :], c.bank[j % 2][:, :], self.bias[:, :], ALU.add
                              ).then_inc(self.rows, 1)
        if n % 5 == 3 and n // 5 < J:
            j = n // 5
            eng.wait_ge(self.rows, g * J + (j + 1 + J))
            eng.tensor_scalar(self.low[:, j % 2, :], self.raw[:, j % 2, 0:D], 0.0, None, ALU.min
                              ).then_inc(self.low_ready, 1)
        if n % 5 == 0 and 1 <= n // 5 <= J:
            j = n // 5 - 1
            eng.wait_ge(self.exp_ready, g * J + (j + 1))
            eng.scalar_tensor_tensor(out=self.key[:, j % 2, :], in0=self.raw[:, j % 2, 0:D], scalar=0.0,
                                     in1=self.low[:, j % 2, :], op0=ALU.max, op1=ALU.add
                                     ).then_inc(self.key_ready, 1)

    def after(self, eng, which):
        if which == "tensor":
            eng.matmul(self.sums, self.zero[:, 0:P], self.zero[:, :], start=False, stop=True,
                       skip_group_check=True).then_inc(self.closed, 1)
        if which == "vector":
            eng.wait_ge(self.closed, 1)
            for k in range(KD):
                for h in range(PER1):
                    part = slice(h * HEAD1, (h + 1) * HEAD1)
                    at = k * (P + 1)
                    eng.tensor_copy(self.map[part, k, part], self.sums[part, at + h * HEAD1:at + (h + 1) * HEAD1])
                    last = eng.tensor_copy(self.map[part, k, P + h:P + h + 1], self.sums[part, at + P:at + P + 1])
            last.then_inc(self.map_ready, 1)


class Mixed1(Work):

    TURNS = 2

    def __init__(self, c, kv, layer):
        self.c, self.kv, self.layer = c, kv, layer

    def buffers(self, sb):
        c = self.c
        self.wx = sb("w_x", [P, KD, D])
        self.bx = sb("b_x", [1, D])
        self.own_product, self.own_ready = c.sems("mixed1", "own_product", "own_ready")
        self.wq = sb("w_q", [P, KD, D])
        self.bq = sb("b_q", [P, KD])
        self.wo = sb("w_o", [P, KD, D])
        self.bo = sb("b_o", [1, D])
        self.q = sb("q", [P, KD, GW])
        self.low = sb("q_low", [P, 2, HALF])
        self.inv = sb("inv", [P, J, 2 * PER1])
        self.heads = sb("heads", [P, J, D])
        self.heads_t = sb("heads_t", [P, 2, KD, P])
        (self.w_in, self.query, self.low_ready, self.exp_ready, self.relu_ready, self.q_ready, self.spread,
         self.inverse, self.heads_ready, self.flipped, self.heads_t_ready, self.product, self.added,
         self.step) = c.sems(
            "mixed1", "w_in", "query", "low_ready", "exp_ready", "relu_ready", "q_ready", "spread", "inverse",
            "heads_ready", "flipped", "heads_t_ready", "product", "added", "step")

    def first(self, eng, which):
        c, d = self.c, self.c.dram
        if which == "sync":
            eng.dma_start(self.wq[:, :, :], chunked(d["L1_mix_wq"])).then_inc(self.w_in, 16)
            eng.dma_start(self.wo[:, :, :], chunked(d["L1_mix_wo"])).then_inc(self.w_in, 16)
            eng.dma_start(self.bo[:, :], one_row(d["L1_mix_bo"])).then_inc(self.w_in, 16)
            eng.dma_start(self.wx[:, :, :], chunked(d["w_m1_t"])[:, 0:KD, :]).then_inc(self.w_in, 16)
            eng.dma_start(self.bx[:, :], one_row(d["L1_gnn_bm1"])).then_inc(self.w_in, 16)
            with c.nc.allow_non_contiguous_dma(reason="a bias as columns"):
                eng.dma_start(self.bq[:, :], columns(d["L1_mix_bq"])).then_inc(self.w_in, 16)

    def before(self, eng, which):
        eng.wait_ge(self.w_in, 6 * 16)
        if which == "tensor":
            eng.wait_ge(self.kv.map_ready, 1)
            eng.sem_inc(self.spread, 1)
        if which == "vector":
            eng.sem_inc(self.q_ready, 2)
            eng.sem_inc(self.heads_ready, J)
            eng.sem_inc(self.added, J)
        if which == "scalar":
            eng.sem_inc(self.heads_t_ready, J)
            eng.sem_inc(self.own_ready, 1)

    def turn(self, eng, which, g):
        c, kv = self.c, self.kv
        parts = [(m, half) for half in range(2) for m in range(KD)]
        if which == "sync":
            kv.cols.load(eng, g, G)
        if which == "tensor":
            kv.cols.wait(eng, g, G)
            for n, (m, half) in enumerate(parts):
                eng.wait_ge(self.q_ready, g * 4 + (n + 1))
                for k in range(KD):
                    last = eng.matmul(c.bank[n % 2][:, 0:HALF], self.wq[:, k, m * P:m * P + P],
                                      kv.cols.buf[:, k, half * HALF:half * HALF + HALF], start=(k == 0),
                                      stop=(k == KD - 1))
                last.then_inc(self.query, 1)
            for j in range(J):
                eng.wait_ge(self.own_ready, g * J + (j + 1))
                own_product(eng, c, c.bank[2][:, 0:D], [kv.cols.buf[:, k, j * P:j * P + P] for k in range(KD)],
                            self.wx, self.bx).then_inc(self.own_product, 1)
            eng.wait_ge(self.q_ready, g * 4 + 6)
            eng.wait_ge(self.own_product, g * J + J)
            eng.sem_inc(kv.cols.free, 1)
            for j in range(J):
                eng.wait_ge(self.heads_ready, g * J + (j + 1 + J - reuse(j, 2)))
                for k in range(KD):
                    last = eng.matmul(c.bank[3 + j % 2][:, k * kv.W:(k + 1) * kv.W], self.q[:, k, j * P:j * P + P],
                                      kv.map[:, k, :], start=True, stop=True)
                last.then_inc(self.spread, 1)
            for j in range(J):
                eng.wait_ge(self.heads_ready, g * J + (j + 1 + J))
                eng.wait_ge(self.heads_t_ready, g * J + (j + 1 + J - reuse(j, 2)))
                to_columns(eng, c.bank[5 + j % 2], self.heads[:, j, :], c.ident[:, :]).then_inc(self.flipped, 1)
                eng.wait_ge(self.heads_t_ready, g * J + (j + 1 + J))
                eng.wait_ge(self.added, g * J + (j + 1 + J - 1))
                out = c.bank[7][:, 0:D]
                for k in range(KD):
                    eng.matmul(out, self.heads_t[:, j % 2, k, :], self.wo[:, k, :], start=(k == 0), stop=False)
                eng.matmul(out, c.ones[0:1, :], self.bo[:, :], start=False, stop=True).then_inc(self.product, 1)
        if which == "scalar":
            for n, (m, half) in enumerate(parts):
                eng.wait_ge(self.low_ready, g * 4 + (n + 1))
                eng.activation(self.low[:, n % 2, :], self.low[:, n % 2, :], ACT.Exp).then_inc(self.exp_ready, 1)
                if n == 0:
                    eng.wait_ge(self.spread, g * J + 1)
                eng.activation(self.q[:, m, half * HALF:half * HALF + HALF], c.bank[n % 2][:, 0:HALF], ACT.Relu,
                               bias=self.bq[:, m:m + 1]).then_inc(self.relu_ready, 1)
            for j in range(J):
                eng.wait_ge(self.own_product, g * J + (j + 1))
                eng.copy(self.layer.own[:, g * J + j, :], c.bank[2][:, 0:D]).then_inc(self.own_ready, 1)
            for j in range(J):
                eng.wait_ge(self.flipped, g * J + (j + 1))
                eng.copy(self.heads_t[:, j % 2, :, :], split_columns(c.bank[5 + j % 2])
                         ).then_inc(self.heads_t_ready, 1)

    def piece(self, eng, g, n):
        c, kv = self.c, self.kv
        parts = [(m, half) for half in range(2) for m in range(KD)]
        if n in (2, 5, 8, 11):
            p = (n - 2) // 3
            m, half = parts[p]
            eng.wait_ge(self.query, g * 4 + (p + 1))
            eng.tensor_scalar(self.low[:, p % 2, :], c.bank[p % 2][:, 0:HALF], self.bq[:, m:m + 1], 0.0,
                              ALU.add, ALU.min).then_inc(self.low_ready, 1)
        if n in (4, 7, 10, 13):
            p = (n - 4) // 3
            m, half = parts[p]
            eng.wait_ge(self.exp_ready, g * 4 + (p + 1))
            eng.wait_ge(self.relu_ready, g * 4 + (p + 1))
            part = self.q[:, m, half * HALF:half * HALF + HALF]
            eng.tensor_tensor(part, part, self.low[:, p % 2, :], ALU.add).then_inc(self.q_ready, 1)
        if n in (26, 29, 32, 35, 38):
            j = (n - 26) // 3
            eng.wait_ge(self.spread, g * J + (j + 2))
            bank = c.bank[3 + j % 2][:, 0:KD * kv.W].rearrange("p (k w) -> p k w", k=KD)
            inv = self.inv[:, j, :].rearrange("p (k h) -> p k h", k=KD)
            eng.tensor_scalar(inv, bank[:, :, P:], 1e-6, None, ALU.add).then_inc(self.inverse, 1)
            eng.wait_ge(self.inverse, g * 2 * J + (2 * j + 1))
            eng.reciprocal(inv, inv).then_inc(self.inverse, 1)
            eng.wait_ge(self.inverse, g * 2 * J + (2 * j + 2))
            for k in range(KD):
                last = eng.tensor_tensor(
                    self.heads[:, j, k * P:k * P + P].rearrange("p (h e) -> p h e", h=PER1),
                    bank[:, k, 0:P].rearrange("p (h e) -> p h e", h=PER1),
                    inv[:, k, :].unsqueeze(2).to_broadcast([P, PER1, HEAD1]), ALU.mult)
            last.then_inc(self.heads_ready, 1)
        if n in (41, 44, 47, 50, 53):
            j = (n - 41) // 3
            eng.wait_ge(self.product, g * J + (j + 1))
            eng.tensor_tensor(c.x[:, g * J + j, :], c.x[:, g * J + j, :], c.bank[7][:, 0:D], ALU.add
                              ).then_inc(self.added, 1)


class Own(Work):

    TURNS = SLOTS

    def __init__(self, c, name, layer, w, b):
        self.c, self.name, self.layer, self.w_table, self.b_table = c, name, layer, w, b

    def buffers(self, sb):
        self.w = sb("w_x", [P, KD, D])
        self.b = sb("b_x", [1, D])
        self.cols = sb("x_cols", [P, 2, KD, P])
        self.rows = sb("x_rows", [P, 2, D])
        self.staged = self.c.sem(self.name + "_staged")
        self.w_in, self.flipped, self.cols_ready, self.product, self.ready = self.c.sems(
            self.name, "w_in", "flipped", "cols_ready", "product", "ready")

    def first(self, eng, which):
        if which == "sync":
            eng.dma_start(self.w[:, :, :], chunked(self.w_table)[:, 0:KD, :]).then_inc(self.w_in, 16)
            eng.dma_start(self.b[:, :], one_row(self.b_table)).then_inc(self.w_in, 16)
        if which == "tensor":
            eng.wait_ge(self.w_in, 2 * 16)
        if which == "scalar":
            eng.sem_inc(self.cols_ready, J)
            eng.sem_inc(self.ready, J)

    def turn(self, eng, which, g):
        c = self.c
        if which == "tensor":
            for j in range(J):
                eng.wait_ge(self.staged, g * J + (j + 1))
                eng.wait_ge(self.cols_ready, g * J + (j + 1 + J - reuse(j, 2)))
                to_columns(eng, c.bank[2 + j % 2], self.rows[:, j % 2, :], c.ident[:, :]
                           ).then_inc(self.flipped, 1)
                eng.wait_ge(self.cols_ready, g * J + (j + 1 + J))
                eng.wait_ge(self.ready, g * J + (j + 1 + J - reuse(j, 2)))
                own_product(eng, c, c.bank[4 + j % 2][:, 0:D], [self.cols[:, j % 2, k, :] for k in range(KD)],
                            self.w, self.b).then_inc(self.product, 1)
        if which == "scalar":
            for j in range(J):
                eng.copy(self.rows[:, j % 2, :], self.layer.rows[:, g * J + j, :]).then_inc(self.staged, 1)
                eng.wait_ge(self.flipped, g * J + (j + 1))
                eng.copy(self.cols[:, j % 2, :, :], split_columns(c.bank[2 + j % 2])).then_inc(self.cols_ready, 1)
                eng.wait_ge(self.product, g * J + (j + 1))
                eng.copy(self.layer.own[:, g * J + j, :], c.bank[4 + j % 2][:, 0:D]).then_inc(self.ready, 1)


def own_product(pe, c, bank, cols, w, b):
    for k in range(KD):
        pe.matmul(bank, cols[k], w[:, k, :], start=(k == 0), stop=False)
    return pe.matmul(bank, c.ones[0:1, :], b[:, :], start=False, stop=True)


class GraphLayer:

    def __init__(self, c, sb):
        self.rows = sb("rows", [P, NT, D])
        self.own = sb("own", [P, NT, D])


def update(c, name, layer, w, ln=None, out_rows=None, last=None):
    own, sb = stage(c, name)
    with own:
        d = c.dram
        pooled = sb("pooled", [P, J, D])
        pooled_t = sb("pooled_cols", [P, J, KD, P])
        weight = sb("w", [P, KD, D])
        y = sb("y", [P, NT, D])
        pooled_in = c.sems(name, *(f"pooled_in{j}" for j in range(J)))
        w_in, flipped, cols_ready, product, added, scaled_ready, done, saved, y_go, act_go = c.sems(
            name, "w_in", "flipped", "cols_ready", "product", "added", "scaled_ready", "done", "saved", "y_go",
            "act_go")
        if ln:
            gain = sb("gain", [P, D])
            offset = sb("offset", [P, D])
            norm = Norm(c, sb, name)
            scaled = sb("scaled", [P, NT, D])
            residual, gained = c.sems(name, "residual", "gained")
        if last:
            X = last.experts
            z = sb("z", [P, J, D])
            z_t = sb("z_cols", [P, J, KD, P])
            gate = sb("gate", [P, KD, X])
            norm_x = Norm(c, sb, name + "x")
            z_ready, z_flipped, z_cols, gated, logits_ready = c.sems(
                name, "z_ready", "z_flipped", "z_cols", "gated", "logits_ready")
        n_in = 1 + (2 if ln else 0) + (1 if last else 0)
        block = own.enter_context(c.nc.Block())

        def group(g):
            return bass.ds(g * J, J)

        def pipelined(engine, part_a, early_b, part_b):
            part_a(0)
            with engine.Fori(0, G - 1) as g:
                early_b(g)
                part_a(g + 1)
                part_b(g)
            early_b(G - 1)
            part_b(G - 1)

        def nothing(g):
            pass

        @block.gpsimd
        def _(pool):
            fetch_nodes(c, pool, pooled, flipped, pooled_in)

        @block.sync
        def _(sp):
            sp.dma_start(weight[:, :, :], chunked(w)[:, KD:, :]).then_inc(w_in, 16)
            if ln:
                sp.dma_start(gain[:, :], all_rows(ln[0])).then_inc(w_in, 16)
                sp.dma_start(offset[:, :], all_rows(ln[1])).then_inc(w_in, 16)
            if last:
                sp.dma_start(gate[:, :, :], chunked(d["router_w_t"])).then_inc(w_in, 16)
            with sp.Fori(0, G) as g:
                if last:
                    sp.wait_ge(z_ready, g * J + J)
                    sp.dma_start(group_rows(out_rows, g), z[:, :, :]).then_inc(saved, 16)
                else:
                    sp.wait_ge(done, g + 1 if ln else g * J + J)
                    sp.dma_start(group_rows(out_rows, g), layer.rows[:, group(g), :]).then_inc(saved, 16)
            sp.wait_ge(saved, 16 * G + (16 if last else 0))

        @block.tensor
        def _(pe):
            def flip(g, j):
                pe.wait_ge(pooled_in[j], g * 16 + 16)
                pe.wait_ge(cols_ready, g * J + (j + 1 + J - reuse(j, 2)))
                to_columns(pe, c.bank[j % 2], pooled[:, j, :], c.ident[:, :]).then_inc(flipped, 1)

            def part_a(g):
                flip(g, 0)
                for j in range(J):
                    if j + 1 < J:
                        flip(g, j + 1)
                    pe.wait_ge(cols_ready, g * J + (j + 1 + J))
                    pe.wait_ge(added, g * J + (j + 1 + J - reuse(j, 2)))
                    for k in range(KD):
                        prod = pe.matmul(c.bank[2 + j % 2][:, 0:D], pooled_t[:, j, k, :], weight[:, k, :],
                                         start=(k == 0), stop=(k == KD - 1))
                    prod.then_inc(product, 1)

            def part_b(g):
                if not last:
                    return
                pe.wait_ge(logits_ready, g + 1)
                for j in range(J):
                    pe.wait_ge(z_ready, g * J + (j + 1))
                    pe.wait_ge(z_cols, g * J + (j + 1 + J - reuse(j, 2)))
                    to_columns(pe, c.bank[4 + j % 2], z[:, j, :], c.ident[:, :]).then_inc(z_flipped, 1)
                    pe.wait_ge(z_cols, g * J + (j + 1 + J))
                    for k in range(KD):
                        prod = pe.matmul(c.bank[6][:, j * X:j * X + X], z_t[:, j, k, :], gate[:, k, :],
                                         start=(k == 0), stop=(k == KD - 1))
                    prod.then_inc(gated, 1)

            pe.wait_ge(w_in, n_in * 16)
            pipelined(pe, part_a, nothing, part_b)

        @block.scalar
        def _(act):
            def part_a(g):
                for j in range(J):
                    act.wait_ge(flipped, g * J + (j + 1))
                    act.copy(pooled_t[:, j, :, :], split_columns(c.bank[j % 2])).then_inc(cols_ready, 1)

            def early_b(g):
                if ln:
                    norm.scalar(act, g)

            def part_b(g):
                if ln:
                    act.wait_ge(norm.step, g * Norm.STEPS + Norm.STEPS)
                    act.sem_inc(act_go, 1)
                    for j in range(J):
                        norm.apply_act(act, scaled[:, g * J + j, :], y[:, g * J + j, :], g * J + j
                                       ).then_inc(scaled_ready, 1)
                else:
                    for j in range(J):
                        act.wait_ge(added, g * J + (j + 1 + J))
                        act.sem_inc(act_go, 1)
                        act.activation(layer.rows[:, g * J + j, :], y[:, g * J + j, :], ACT.Relu).then_inc(done, 1)
                if not last:
                    return
                norm_x.scalar(act, g)
                act.wait_ge(norm_x.step, g * Norm.STEPS + Norm.STEPS)
                act.wait_ge(saved, g * 16 + 16)
                act.wait_ge(z_flipped, g * J + 1)
                for j in range(J):
                    norm_x.apply_act(act, z[:, j, :], c.x[:, g * J + j, :], g * J + j).then_inc(z_ready, 1)
                for j in range(J):
                    act.wait_ge(z_flipped, g * J + (j + 2))
                    act.copy(z_t[:, j, :, :], split_columns(c.bank[4 + j % 2])).then_inc(z_cols, 1)
                act.wait_ge(gated, g * J + J)
                act.copy(last.logits[:, group(g), :], c.bank[6][:, 0:J * X].rearrange("p (j e) -> p j e", j=J)
                         ).then_inc(logits_ready, 1)

            act.sem_inc(cols_ready, J)
            if last:
                act.sem_inc(z_cols, J)
                act.sem_inc(z_flipped, 1)
                act.sem_inc(logits_ready, 1)
            pipelined(act, part_a, early_b, part_b)

        @block.vector
        def _(vec):
            def part_a(g):
                for j in range(J):
                    vec.wait_ge(product, g * J + (j + 1))
                    vec.sem_inc(y_go, 1)
                    vec.tensor_tensor(y[:, g * J + j, :], c.bank[2 + j % 2][:, 0:D], layer.own[:, g * J + j, :],
                                      ALU.add).then_inc(added, 1)

            def early_b(g):
                if ln:
                    vec.wait_ge(added, g * J + 2 * J)
                    vec.sem_inc(y_go, 1)
                    vec.scalar_tensor_tensor(out=y[:, group(g), :], in0=y[:, group(g), :], scalar=0.0,
                                             in1=layer.rows[:, group(g), :], op0=ALU.max, op1=ALU.add
                                             ).then_inc(residual, 1)
                    vec.wait_ge(residual, g + 1)
                    norm.vector(vec, g, lambda j: y[:, g * J + j, :])

            def part_b(g):
                if not ln:
                    return
                vec.wait_ge(scaled_ready, g * J + J)
                step = Chain(vec, gained, g * 2 if last else g)
                step(vec.tensor_tensor(scaled[:, group(g), :], scaled[:, group(g), :],
                                       gain[:, :].unsqueeze(1).to_broadcast([P, J, D]), ALU.mult))
                all_offset = offset[:, :].unsqueeze(1).to_broadcast([P, J, D])
                if last:
                    step(vec.tensor_tensor(scaled[:, group(g), :], scaled[:, group(g), :], all_offset, ALU.add))
                    vec.tensor_tensor(c.x[:, group(g), :], c.x[:, group(g), :], scaled[:, group(g), :], ALU.add
                                      ).then_inc(done, 1)
                    vec.wait_ge(done, g + 1)
                    norm_x.vector(vec, g, lambda j: c.x[:, g * J + j, :])
                else:
                    vec.tensor_tensor(layer.rows[:, group(g), :], scaled[:, group(g), :], all_offset, ALU.add
                                      ).then_inc(done, 1)

            vec.wait_ge(w_in, n_in * 16)
            vec.sem_inc(added, J)
            if last:
                vec.sem_inc(saved, 16)
            pipelined(vec, part_a, early_b, part_b)


def finish_layer1(c, r, out):
    own, sb = stage(c, "finish1")
    with own:
        d = c.dram
        es = ExpertSum(c, r, sb, "sum1", d["z4"], d["L1_ffn_b2"])
        saved, step = c.sems("finish1", "saved", "step")
        done = c.sem("finish1_done")
        banks = (0, 1, 2, 3)
        block = own.enter_context(c.nc.Block())

        @block.sync
        def _(sp):
            es.sync_first(sp)
            es.sync(sp, 0)
            with sp.Fori(0, G - 1) as g:
                es.sync(sp, g + 1)
                sp.wait_ge(done, g + 1)
                sp.dma_start(group_rows(out, g), es.total[:, :, :]).then_inc(saved, 16)
            sp.wait_ge(done, G)
            sp.dma_start(group_rows(out, G - 1), es.total[:, :, :]).then_inc(saved, 16)
            sp.wait_ge(saved, 16 * G + 16)

        @block.gpsimd
        def _(pool):
            with pool.Fori(0, G) as g:
                es.pool(pool, g)

        @block.tensor
        def _(pe):
            pe.wait_ge(es.bias_in, 16)
            es.open(pe)
            with pe.Fori(0, G) as g:
                es.tensor(pe, g, banks)

        @block.scalar
        def _(act):
            with act.Fori(0, G) as g:
                es.scalar(act, g, banks)

        @block.vector
        def _(vec):
            vec.sem_inc(saved, 16)
            with vec.Fori(0, G) as g:
                vec.wait_ge(saved, g * 16 + 16)
                es.vector(vec, g, step, banks)
                vec.tensor_tensor(es.total[:, :, :], es.total[:, :, :], c.x[:, bass.ds(g * J, J), :], ALU.add
                                  ).then_inc(done, 1)


def program(nc, ins, out):
    with ExitStack() as ctx:
        def scratch(name, *shape):
            return nc.dram_tensor(name, shape, F32, kind="Internal").ap()

        d = dict(ins)
        for name in ("z0", "z2", "h", "a1", "a2", "z4"):
            d[name] = scratch(name, NP, D)
        for name in ("z0_cols", "z3_cols"):
            d[name] = scratch(name, P, KD, NP)
        d["state"] = scratch("state", EP + 1 + P, D)
        d["node_ends"] = scratch("node_ends", NP + 1)
        d["expert_out"] = scratch("expert_out", 2 * NP + max(places(16), places(8)) * P, D)
        c = Core(nc, ctx, d)

        setup(c)
        kv = KeyValue0(c)
        edge_walk(c, "walk0", d["z0"], "sum", (kv, Mlp0(c, kv)))
        own, sb = stage(c, "routes0")
        with own:
            r = Routes(c, sb, 16, places(16))
            convolve0(c, r.logits)
            route(c, r, "route0", False)
            experts(c, r, "experts0", d["z2"], d["L0_ffn_w1"], d["expert_b1_0"], d["L0_ffn_w2"], ACT.Relu)
            finish_layer0(c, r)

        own, sb = stage(c, "graph1")
        with own:
            r = Routes(c, sb, 8, places(8))
            with ExitStack() as inner:
                layer = GraphLayer(c, Local(c, inner, "graph1"))
                kv = KeyValue1(c)
                edge_walk(c, "walk1", d["h"], "max0", (kv, Mixed1(c, kv, layer)))
                update(c, "update1", layer, d["w_m1_t"], out_rows=d["a1"])
                edge_walk(c, "walk2", d["a1"], "max0", (Own(c, "own2", layer, d["w_m2_t"], d["L1_gnn_bm2"]),))
                update(c, "update2", layer, d["w_m2_t"], ln=(d["L1_gnn_ln2_g"], d["L1_gnn_ln2_b"]),
                       out_rows=d["a2"])
                edge_walk(c, "walk3", d["a2"], "max", (Own(c, "own3", layer, d["w_m3_t"], d["L1_gnn_bm3"]),))
                update(c, "update3", layer, d["w_m3_t"], ln=(d["L1_gnn_ln3_g"], d["L1_gnn_ln3_b"]),
                       out_rows=d["z4"], last=r)
            route(c, r, "route1", True)
            experts(c, r, "experts1", d["z4"], d["L1_ffn_w1"], d["expert_b1_1"], d["L1_ffn_w2"], ACT.Gelu)
            finish_layer1(c, r, out)



def kernel(**inputs):
    import numpy as np
    import concourse.bacc as bacc
    from concourse.bass_utils import run_bass_kernel_spmd as run

    def padded(a, size, fill, lead=0):
        out = np.full((size,) + a.shape[1:], fill, a.dtype)
        out[lead:lead + len(a)] = a
        return out

    a = {k: np.asarray(v) for k, v in inputs.items()}
    arrays = {k: v for k, v in a.items() if k.startswith(("L0_", "L1_"))}
    arrays["x"] = padded(a["x"], NP, 0)
    arrays["src"] = padded(a["src"], EP, 0)
    arrays["dst"] = padded(a["dst"], EP + 1, NP - 1, 1)
    arrays["dst"][0] = -1
    arrays["w_q_t"] = a["L0_mix_w_qkv"][:, :D].T
    arrays["w_p1_t"] = arrays.pop("L1_gnn_Wp1").T
    for n in (1, 2, 3):
        arrays[f"w_m{n}_t"] = arrays.pop(f"L1_gnn_Wm{n}").T
    arrays["router_w_t"] = arrays.pop("L1_ffn_router_w").T
    for n in (0, 1):
        b = arrays.pop(f"L{n}_ffn_b1")
        arrays[f"expert_b1_{n}"] = b.reshape(len(b), -1, P).transpose(0, 2, 1)
    arrays = {f"in_{k}": np.ascontiguousarray(v) for k, v in arrays.items()}

    nc = bacc.Bacc("TRN2", target_bir_lowering=False, num_devices=1)
    ins = {k[3:]: nc.dram_tensor(k, v.shape, mybir.dt.from_np(v.dtype), kind="ExternalInput").ap()
           for k, v in arrays.items()}
    out = nc.dram_tensor("out", (NP, D), F32, kind="ExternalOutput").ap()
    program(nc, ins, out)
    r = run(nc, [arrays], core_ids=[0])
    return r.results[0]["out"][:N]
```

```python
from contextlib import ExitStack

import concourse.bass as bass
from concourse import mybir

F32 = mybir.dt.float32
BF16 = mybir.dt.bfloat16
I32 = mybir.dt.int32
U32 = mybir.dt.uint32
ALU = mybir.AluOpType
ACT = mybir.ActivationFunctionType
AX = mybir.AxisListType

P = 128
N = 3125
NT = -(-N // P)
NP = NT * P
G = 5
J = NT // G
GW = J * P
HALF = GW // 2
D = 256
KD = D // P
E = 53125
SLOTS = 3
RING = 14
TURN = 2 * RING
STORE = RING // 2
TURNS = SLOTS * G
LANE = TURNS * TURN
EP = P * LANE
LO = 64
HI = NP // LO
HOT = LANE // (G - 1)
EPS = 1e-5
FAR = 1.5e38
ROUND = 12582912.0
HIDDEN = 3 * D
KH = HIDDEN // P
HEAD0 = D // 4
HEAD1 = D // 8
PER1 = P // HEAD1
assert NT == G * J and NP % LO == 0 and EP >= E and LANE % (G - 1) == 0


class Chain:

    def __init__(self, engine, sem, before=0):
        self.engine, self.sem, self.n = engine, sem, before

    def __call__(self, instruction):
        self.n += 1
        instruction.then_inc(self.sem, 1)
        self.engine.wait_ge(self.sem, self.n)


class Core:

    def __init__(self, nc, ctx, dram):
        self.nc, self.ctx, self.dram = nc, ctx, dram
        self.live = []
        self.x = self.sb("x_acc", [P, NT, D])
        self.ident = self.sb("ident", [P, P])
        self.ones = self.sb("ones", [P, P])
        self.upper = self.sb("upper", [P, P])
        self.eps = self.sb("eps", [P, 1])
        self.real = self.sb("real", [P, NT])
        self.count_up = self.sb("count_up", [P, P], I32)
        self.keep = self.sb("keep", [P, LANE + TURN])
        self.cut = self.sb("cut", [P, LANE + TURN])
        self.src = self.sb("src_idx", [P, LANE + TURN], U32)
        self.lane_keep = self.sb("lane_keep", [P, P])
        self.lane_cut = self.sb("lane_cut", [P, P])
        self.end_idx = self.sb("end_idx", [P, NT], U32)
        self.run_idx = self.sb("run_idx", [P, 1], U32)
        self.fix_idx = self.sb("fix_idx", [P, 1], U32)
        self.bank = [ctx.enter_context(nc.psum_tensor(f"bank{i}", [P, 512], F32)) for i in range(8)]

    def sb(self, name, shape, dt=F32):
        return self.ctx.enter_context(self.nc.sbuf_tensor(name, shape, dt))

    def sem(self, name):
        self.live.append(self.nc.alloc_semaphore(name))
        return self.live[-1]

    def retire(self):
        if self.live:
            self.nc.clear_and_free_semaphores(self.live)
            self.nc.all_engine_barrier()
            self.live = []

    def sems(self, prefix, *names):
        return [self.sem(f"{prefix}_{n}") for n in names]


class Local:

    def __init__(self, c, own, prefix):
        self.c, self.own, self.prefix = c, own, prefix
        own.callback(c.retire)

    def __call__(self, name, shape, dt=F32):
        return self.own.enter_context(self.c.nc.sbuf_tensor(f"{self.prefix}_{name}", shape, dt))


def all_rows(ap):
    n = ap.shape[0]
    return ap.rearrange("(a n) -> a n", a=1).to_broadcast([P, n])


def one_row(ap):
    return ap.rearrange("(a n) -> a n", a=1)


def chunked(ap):
    return ap.rearrange("(k p) n -> p k n", p=P)


def group_rows(table, g):
    return table.rearrange("(g j p) d -> g p j d", g=G, p=P)[g]


class Norm:

    STEPS = 6

    def __init__(self, c, sb, prefix):
        self.c = c
        self.stats = sb(f"{prefix}_stats", [P, J, 6])
        self.m = sb(f"{prefix}_moment", [P, 4, J])
        self.var = sb(f"{prefix}_var", [P, J])
        self.std = sb(f"{prefix}_std", [P, J])
        self.rstd = sb(f"{prefix}_rstd", [P, NT])
        self.shift = sb(f"{prefix}_shift", [P, NT])
        self.var_ready, self.std_ready, self.step, self.go = c.sems(
            prefix, "var_ready", "std_ready", "norm_step", "norm_go")

    def vector(self, vec, g, rows):
        vec.sem_inc(self.go, 1)
        step = Chain(vec, self.step, g * self.STEPS)
        for j in range(J):
            last = vec.bn_stats(self.stats[:, j, :], rows(j))
        step(last)
        self.moments(vec, step, g)

    def moments(self, vec, step, g):
        st, m = self.stats, self.m
        step(vec.tensor_tensor(m[:, 0:3:2, :], st[:, :, 1:3].rearrange("p j s -> p s j"),
                               st[:, :, 4:6].rearrange("p j s -> p s j"), ALU.add))
        step(vec.tensor_tensor(m[:, 1, :], st[:, :, 1], st[:, :, 4], ALU.subtract))
        step(vec.tensor_tensor(m[:, 3, :], m[:, 1, :], m[:, 1, :], ALU.mult))
        vec.scalar_tensor_tensor(out=self.var[:, :], in0=m[:, 3, :], scalar=D / 4.0, in1=m[:, 2, :],
                                 op0=ALU.mult, op1=ALU.add).then_inc(self.var_ready, 1)
        part = bass.ds(g * J, J)
        vec.wait_ge(self.std_ready, g + 1)
        vec.sem_inc(self.go, 1)
        step(vec.reciprocal(self.rstd[:, part], self.std[:, :]))
        step(vec.scalar_tensor_tensor(out=self.shift[:, part], in0=m[:, 0, :], scalar=-0.5, in1=self.rstd[:, part],
                                      op0=ALU.mult, op1=ALU.mult))

    def scalar(self, act, g):
        act.wait_ge(self.var_ready, g + 1)
        act.activation(self.std[:, :], self.var[:, :], ACT.Sqrt, bias=self.c.eps[:, 0:1],
                       scale=1.0 / D).then_inc(self.std_ready, 1)

    def apply(self, vec, out, row, t):
        return vec.tensor_scalar(out, row, self.rstd[:, bass.ds(t, 1)], self.shift[:, bass.ds(t, 1)],
                                 ALU.mult, ALU.add)

    def apply_act(self, act, out, row, t):
        return act.activation(out, row, ACT.Identity, bias=self.shift[:, bass.ds(t, 1)],
                              scale=self.rstd[:, bass.ds(t, 1)])


class Parts:

    def ahead(self, g):
        pass

    def early(self, g):
        pass

    def middle(self, g):
        pass

    def late(self, g):
        pass

    def behind(self, g):
        pass


def one_ahead(first, second):
    first(0)
    for j in range(J):
        if j + 1 < J:
            first(j + 1)
        second(j)


def overlapped(engine, p, ahead_first=False):

    def start(g, ahead):
        if ahead_first and ahead is not None:
            p.ahead(ahead)
        p.early(g)
        if not ahead_first and ahead is not None:
            p.ahead(ahead)

    p.ahead(0)
    start(0, 1)
    p.middle(0)
    p.late(0)
    with engine.Fori(0, G - 2) as h:
        start(h + 1, h + 2)
        p.middle(h + 1)
        p.behind(h)
        p.late(h + 1)
    start(G - 1, None)
    p.middle(G - 1)
    p.behind(G - 2)
    p.late(G - 1)
    p.behind(G - 1)


def setup(c):
    nc, dram = c.nc, c.dram
    with ExitStack() as own:
        sb = Local(c, own, "setup")
        dst = sb("dst", [P, LANE], I32)
        before = sb("dst_before", [P, LANE], I32)
        run = sb("run", [P, LANE])
        step_no = sb("step_no", [P, LANE], I32)
        run_end = sb("run_end", [P, 1])
        lane_no = sb("lane_no", [P, 1], I32)
        lane_f = sb("lane_f", [P, 4])
        lane_full = sb("lane_full", [P, 1])
        diag = sb("diag", [P, P])
        zero = sb("zero", [P, D])
        z = sb("z", [P, J, D])
        zt = sb("zt", [P, KD, GW])
        norm = Norm(c, sb, "setup")
        x_in, rest_in, edges_in, pool_step, const_ready, step_sem, consts_out = c.sems(
            "setup", "x_in", "rest_in", "edges_in", "pool_step", "const_ready", "step", "consts_out")
        diag_ready, lanes_ready, z_ready, z_saved, flipped, taken, zt_saved = c.sems(
            "setup", "diag_ready", "lanes_ready", "z_ready", "z_saved", "flipped", "taken", "zt_saved")
        block = own.enter_context(nc.Block())
        lanes = c.bank[7][:, 0:P]

        @block.sync
        def _(sp):
            def lane_view(at):
                return dram["dst"][at:at + EP].rearrange("(p k) -> p k", p=P)

            sp.dma_start(dst[:, :], lane_view(1)).then_inc(edges_in, 16)
            sp.dma_start(before[:, :], lane_view(0)).then_inc(edges_in, 16)
            sp.dma_start(c.src[:, 0:LANE], dram["src"].rearrange("(p k) -> p k", p=P).bitcast(U32)
                         ).then_inc(edges_in, 16)
            x_rows = dram["x"].rearrange("(t p) d -> p t d", p=P)
            sp.dma_start(c.x[:, 0:J, :], x_rows[:, 0:J, :]).then_inc(x_in, 16)
            sp.dma_start(c.x[:, J:, :], x_rows[:, J:, :]).then_inc(rest_in, 16)
            sp.wait_ge(const_ready, 1)
            sp.dma_start(dram["state"][EP:EP + P, :], zero[:, :]).then_inc(consts_out, 16)
            sp.dma_start(dram["state"][EP + P:EP + P + 1, :], zero[0:1, :]).then_inc(consts_out, 16)
            for k in range(2):
                sp.dma_start(dram["expert_out"][k * NP + N:k * NP + NP, :], zero[0:NP - N, :]
                             ).then_inc(consts_out, 16)
            with sp.Fori(0, G) as g:
                sp.wait_ge(z_ready, g * J + J)
                sp.dma_start(group_rows(dram["z0"], g), z[:, :, :]).then_inc(z_saved, 16)
                sp.wait_ge(taken, g * J + 2 * J)
                sp.dma_start(dram["z0_cols"][:, :, bass.ds(g * GW, GW)], zt[:, :, :]).then_inc(zt_saved, 16)
            sp.wait_ge(consts_out, 4 * 16)
            sp.wait_ge(z_saved, 16 * G + 16)
            sp.wait_ge(zt_saved, 16 * G + 16)

        @block.gpsimd
        def _(pool):
            step = Chain(pool, pool_step)
            pool.memset(zero[:, :], 0.0)
            pool.memset(c.ones[:, :], 1.0)
            pool.memset(c.eps[:, :], EPS)
            pool.memset(c.src[:, LANE:], 0)
            pool.iota(c.count_up[:, :], pattern=[[1, P]], base=0, channel_multiplier=0)
            pool.iota(step_no[:, :], pattern=[[1, LANE]], base=0, channel_multiplier=0)
            pool.iota(lane_no[:, :], pattern=[[0, 1]], base=0, channel_multiplier=1)
            pool.memset(c.ident[:, :], 0.0)
            pool.memset(c.real[:, :], 1.0)
            step(pool.memset(c.upper[:, :], 1.0))
            pool.affine_select(out=c.ident[:, :], in_=c.ident[:, :], compare_op=ALU.not_equal, fill=1.0,
                               base=0, pattern=[[-1, P]], channel_multiplier=1)
            pool.affine_select(out=c.real[:, :], in_=c.real[:, :], compare_op=ALU.is_ge, fill=0.0,
                               base=N - 1, pattern=[[-P, NT]], channel_multiplier=-1)
            pool.affine_select(out=c.upper[:, :], in_=c.upper[:, :], compare_op=ALU.is_gt, fill=0.0,
                               base=0, pattern=[[1, P]], channel_multiplier=-1).then_inc(const_ready, 1)

        @block.vector
        def _(vec):
            step = Chain(vec, step_sem)
            vec.wait_ge(edges_in, 3 * 16)
            vec.wait_ge(const_ready, 1)
            vec.memset(c.keep[:, LANE:], 0.0)
            vec.memset(c.cut[:, LANE:], 0.0)
            step(vec.tensor_tensor(c.keep[:, 0:LANE], dst[:, :], before[:, :], ALU.is_equal))
            step(vec.tensor_scalar(c.cut[:, 0:LANE], c.keep[:, 0:LANE], FAR, -FAR, ALU.mult, ALU.add))
            step(vec.memset(c.cut[:, 0:1], -FAR))
            step(vec.tensor_tensor(lane_full[:, :], dst[:, LANE - 1:LANE], before[:, 0:1], ALU.is_equal))
            vec.tensor_scalar(diag[:, :], c.ident[:, :], lane_full[:, 0:1], None, ALU.mult
                              ).then_inc(diag_ready, 1)
            step(vec.tensor_scalar(run[:, :], c.keep[:, 0:LANE], float(LANE), None, ALU.mult))
            step(vec.tensor_tensor(run[:, :], run[:, :], step_no[:, :], ALU.add))
            step(vec.tensor_reduce(run_end[:, :], run[:, :], AX.X, ALU.min))
            f = lane_f
            step(vec.tensor_scalar(f[:, 0:1], lane_no[:, :], float(LANE), None, ALU.mult))
            step(vec.tensor_scalar(f[:, 1:2], run_end[:, :], -1.0, 0.0, ALU.add, ALU.max))
            step(vec.tensor_tensor(f[:, 1:2], f[:, 1:2], f[:, 0:1], ALU.add))
            step(vec.tensor_copy(c.run_idx[:, :], f[:, 1:2]))
            step(vec.tensor_scalar(f[:, 2:3], run_end[:, :], 0.0, None, ALU.is_gt))
            step(vec.tensor_scalar(f[:, 3:4], lane_no[:, :], EP + 1.0, None, ALU.add))
            step(vec.tensor_tensor(f[:, 0:1], f[:, 1:2], f[:, 3:4], ALU.subtract))
            step(vec.tensor_tensor(f[:, 0:1], f[:, 0:1], f[:, 2:3], ALU.mult))
            step(vec.tensor_tensor(f[:, 0:1], f[:, 0:1], f[:, 3:4], ALU.add))
            step(vec.tensor_copy(c.fix_idx[:, :], f[:, 0:1]))
            vec.wait_ge(lanes_ready, 1)
            step(vec.tensor_copy(c.lane_keep[:, :], lanes))
            vec.tensor_scalar(c.lane_cut[:, :], c.lane_keep[:, :], FAR, -FAR, ALU.mult, ALU.add)
            vec.wait_ge(x_in, 16)
            vec.sem_inc(z_saved, 16)

            def normalise(g):
                norm.vector(vec, g, lambda j: c.x[:, g * J + j, :])
                vec.wait_ge(z_saved, 16 * g + 16)
                vec.wait_ge(flipped, g * J + 1)
                for j in range(J):
                    norm.apply(vec, z[:, j, :], c.x[:, g * J + j, :], g * J + j).then_inc(z_ready, 1)

            normalise(0)
            vec.wait_ge(rest_in, 16)
            with vec.Fori(0, G - 1) as g:
                normalise(g + 1)

        @block.tensor
        def _(pe):
            pe.wait_ge(diag_ready, 1)
            pe.matmul(lanes, c.ones[:, :], diag[:, :], start=True, stop=True).then_inc(lanes_ready, 1)
            pe.sem_inc(flipped, 1)
            with pe.Fori(0, G) as g:
                for j in range(J):
                    pe.wait_ge(z_ready, g * J + j + 1)
                    pe.wait_ge(taken, g * J + j + 1)
                    for k in range(KD):
                        last = pe.transpose(c.bank[j][:, k * P:k * P + P], z[:, j, k * P:k * P + P], c.ident[:, :])
                    last.then_inc(flipped, 1)

        @block.scalar
        def _(act):
            act.sem_inc(taken, J)
            act.sem_inc(zt_saved, 16)
            with act.Fori(0, G) as g:
                norm.scalar(act, g)
                act.wait_ge(zt_saved, 16 * g + 16)
                for j in range(J):
                    act.wait_ge(flipped, g * J + j + 2)
                    act.copy(zt[:, :, j * P:j * P + P], c.bank[j][:, 0:D].rearrange("p (k n) -> p k n", k=KD)
                             ).then_inc(taken, 1)


def reuse(j, n):
    return n if j >= n else J + j - max(i for i in range(J) if i % n == j % n)


class Work:

    TURNS = 1
    LAST_DIFFERS = False

    def buffers(self, sb):
        pass

    def first(self, engine, which):
        pass

    def before(self, engine, which):
        pass

    def turn(self, engine, which, g):
        pass

    def piece(self, vec, g, n):
        pass

    def after(self, engine, which):
        pass


def edge_walk(c, name, table, reduce, work=None):
    nc, dram = c.nc, c.dram
    work = work or (Work(), Work(), Work())
    assert sum(w.TURNS for w in work) == SLOTS
    restart = c.cut if reduce == "max" else c.keep
    join = ALU.add if reduce == "max" else ALU.mult
    merge = ALU.add if reduce == "sum" else ALU.max
    lane_restart = c.lane_cut if reduce == "max" else c.lane_keep
    nothing = -FAR if reduce == "max" else 0.0
    CREDIT = RING + 1
    states = dram["state"][0:EP, :].rearrange("(p k) d -> p k d", p=P)

    with ExitStack() as own:
        sb = Local(c, own, name)
        ring = sb("ring", [P, RING, D])
        state = sb("state", [P, RING, D])
        idx = sb("idx", [P, 2, RING], U32)
        mark = sb("mark", [P, 2, RING])
        scanned = sb("scanned", [P, KD, P + 1])
        carry = sb("carry", [P, D])
        run = sb("run", [P, D])
        walked, idx_ready, turn_go = c.sems(name, "walked", "idx_ready", "turn_go")
        stored = c.sems(name, "stored0", "stored1")
        arrived = c.sems(name, *(f"arrived{j}" for j in range(RING)))
        flipped, summed, back, carry_rows, run_in, merged, fixed = c.sems(
            name, "flipped", "summed", "back", "carry_rows", "run_in", "merged", "fixed")
        for w in work:
            w.buffers(sb)
        block = own.enter_context(nc.Block())

        def slots(engine, which, group):
            for w in work:
                w.first(engine, which)
            turn = 0
            for w in work:
                w.before(engine, which)
                with engine.Fori(0, G - 1 if w.LAST_DIFFERS else G) as g:
                    group(turn + g * w.TURNS, g, w)
                turn += G * w.TURNS
                if w.LAST_DIFFERS:
                    group(turn - w.TURNS, G - 1, w)
                w.after(engine, which)

        @block.gpsimd
        def _(pool):
            with pool.Fori(0, TURNS) as i:
                for h in range(2):
                    pool.wait_ge(idx_ready, i * 2 + h + 1)
                    for j in range(RING):
                        if j % 2 == 0:
                            pool.wait_ge(walked, i * TURN + (h * RING + j + 2 + 1))
                            pool.sem_inc(turn_go, 1)
                        pool.indirect_dma_start(ring[:, j, :], None, table[:, :],
                                                bass.IndirectOffsetOnAxis(idx[:, h, j:j + 1], 0)
                                                ).then_inc(arrived[j], 16)
            for q in range(2):
                pool.wait_ge(stored[q], 16 + 16 * TURNS * 2)
            pool.indirect_dma_start(run[:, :], None, dram["state"][:, :],
                                    bass.IndirectOffsetOnAxis(c.run_idx[:, 0:1], 0)).then_inc(run_in, 16)
            pool.wait_ge(merged, 1)
            pool.indirect_dma_start(dram["state"][:, :], bass.IndirectOffsetOnAxis(c.fix_idx[:, 0:1], 0),
                                    run[:, :], None).then_inc(fixed, 16)
            pool.wait_ge(fixed, 16)

        @block.vector
        def _(vec):
            def stage(i, h):
                at = i * TURN + h * RING
                vec.tensor_copy(mark[:, h, :], restart[:, bass.ds(at, RING)])
                vec.tensor_copy(idx[:, h, :], c.src[:, bass.ds(at, RING)]).then_inc(idx_ready, 1)

            def walk_turn(i, g, w, before):
                for h in range(2):
                    for j in range(RING):
                        if j % STORE == 0:
                            vec.wait_ge(stored[j // STORE], i * 32 + (h + 1) * 16)
                        vec.wait_ge(arrived[j], i * 32 + (h + 1) * 16)
                        vec.wait_ge(walked, i * TURN + (h * RING + j + CREDIT))
                        vec.scalar_tensor_tensor(out=state[:, j, :], in0=state[:, (j - 1) % RING, :],
                                                 scalar=mark[:, h, j:j + 1], in1=ring[:, j, :],
                                                 op0=join, op1=merge).then_inc(walked, 1)
                        w.piece(vec, g, before + h * RING + j)
                    vec.wait_ge(walked, i * TURN + ((h + 1) * RING + CREDIT))
                    stage(i + 1, h)
                    vec.wait_ge(idx_ready, i * 2 + (h + 3))

            stage(0, 0)
            stage(0, 1)
            vec.memset(state[:, RING - 1, :], 0.0).then_inc(walked, 1)
            vec.sem_inc(walked, RING)
            for q in range(2):
                vec.sem_inc(stored[q], 16)
            vec.wait_ge(idx_ready, 2)
            def group(i, g, w):
                for r in range(w.TURNS):
                    walk_turn(i + r, g, w, r * TURN)

            slots(vec, "vector", group)
            vec.memset(scanned[:, :, 0:1], nothing)
            vec.wait_ge(flipped, 1)
            for k in range(KD):
                vec.tensor_tensor_scan(scanned[:, k, 1:P + 1], lane_restart[:, :], c.bank[0][:, k * P:k * P + P],
                                       nothing, join, merge).then_inc(summed, 1)
            vec.wait_ge(run_in, 16)
            vec.wait_ge(carry_rows, 1)
            vec.tensor_tensor(run[:, :], run[:, :], carry[:, :], merge).then_inc(merged, 1)

        @block.sync
        def _(sp):
            def group(i, g, w):
                w.turn(sp, "sync", g)
                for q in range(4 * w.TURNS):
                    first = (q % 2) * STORE
                    sp.wait_ge(walked, i * TURN + ((q + 1) * STORE + CREDIT))
                    sp.dma_start(states[:, bass.ds(i * TURN + q * STORE, STORE), :],
                                 state[:, first:first + STORE, :]).then_inc(stored[q % 2], 16)

            slots(sp, "sync", group)
            for q in range(2):
                sp.wait_ge(stored[q], 16 + 16 * TURNS * 2)

        @block.tensor
        def _(pe):
            slots(pe, "tensor", lambda i, g, w: w.turn(pe, "tensor", g))
            pe.wait_ge(walked, LANE + CREDIT)
            for k in range(KD):
                last = pe.transpose(c.bank[0][:, k * P:k * P + P], state[:, RING - 1, k * P:k * P + P],
                                    c.ident[:, :])
            last.then_inc(flipped, 1)
            pe.wait_ge(summed, KD)
            for k in range(KD):
                last = pe.transpose(c.bank[1][:, k * P:k * P + P], scanned[:, k, 0:P], c.ident[:, :])
            last.then_inc(back, 1)

        @block.scalar
        def _(act):
            slots(act, "scalar", lambda i, g, w: w.turn(act, "scalar", g))
            act.wait_ge(back, 1)
            act.copy(carry[:, :], c.bank[1][:, 0:D]).then_inc(carry_rows, 1)


def columns(ap):
    return ap.rearrange("(k p) -> p k", p=P)


class EdgeCount:

    def __init__(self, c):
        self.c = c

    def buffers(self, sb):
        c = self.c
        self.dst = sb("dst", [P, LANE], I32)
        self.low = sb("dst_low", [P, LANE], I32)
        self.is_low = sb("is_low", [P, HOT, LO], BF16)
        self.is_high = sb("is_high", [P, HOT, HI], BF16)
        self.none = sb("none", [P, LO], BF16)
        self.along = sb("along", [HI, LO])
        self.total = sb("total", [HI, LO])
        self.zero = sb("zero", [1, 1])
        self.upto = sb("upto", [P, NT])
        self.start = sb("start", [P, NT])
        self.t = [sb(f"node_t{i}", [P, NT]) for i in range(2)]
        (self.dst_in, self.hot, self.counted, self.closed, self.step, self.along_ready,
         self.before_ready, self.total_ready, self.table_out, self.table_in, self.opened) = c.sems(
            "count", "dst_in", "hot", "counted", "closed", "step", "along_ready", "before_ready",
            "total_ready", "table_out", "table_in", "opened")
        self.counts = c.bank[5][0:HI, 0:LO]
        self.before_rows = c.bank[5][0:HI, LO:LO + 1]
        self.chain = None

    def first(self, eng, which):
        c, nc = self.c, self.c.nc
        if which == "sync":
            eng.dma_start(self.dst[:, :], c.dram["dst"][1:1 + EP].rearrange("(p k) -> p k", p=P)
                          ).then_inc(self.dst_in, 16)
        if which == "vector":
            self.chain = Chain(eng, self.step)
            eng.memset(self.zero[:, :], 0.0)
            eng.memset(self.none[:, :], 0.0).then_inc(self.opened, 1)
            eng.wait_ge(self.dst_in, 16)
            self.chain(eng.tensor_scalar(self.low[:, :], self.dst[:, :], LO - 1, None, ALU.bitwise_and))
            self.chain(eng.tensor_scalar(self.dst[:, :], self.dst[:, :], LO.bit_length() - 1, None,
                                         ALU.arith_shift_right))

    def open(self, eng, which):
        if which == "tensor":
            eng.wait_ge(self.opened, 1)
            eng.matmul(self.counts, self.none[:, 0:HI], self.none[:, :], start=True, stop=False,
                       skip_group_check=True).then_inc(self.counted, 1)

    def turn(self, eng, which, g):
        c = self.c
        if which == "tensor":
            eng.wait_ge(self.hot, g + 1)
            for k in range(HOT):
                last = eng.matmul(self.counts, self.is_high[:, k, :], self.is_low[:, k, :], start=False,
                                  stop=False, skip_group_check=True)
            last.then_inc(self.counted, 1)

    def piece(self, eng, g, n):
        c = self.c
        part = bass.ds(g * HOT, HOT)
        if n == 8:
            eng.wait_ge(self.counted, g + 1)
            eng.tensor_tensor(self.is_low[:, :, :],
                              self.low[:, part].unsqueeze(2).to_broadcast([P, HOT, LO]),
                              c.count_up[:, 0:LO].unsqueeze(1).to_broadcast([P, HOT, LO]), ALU.is_equal)
        if n == 18:
            eng.tensor_tensor(self.is_high[:, :, :],
                              self.dst[:, part].unsqueeze(2).to_broadcast([P, HOT, HI]),
                              c.count_up[:, 0:HI].unsqueeze(1).to_broadcast([P, HOT, HI]),
                              ALU.is_equal).then_inc(self.hot, 1)

    def after(self, eng, which):
        c, flat, step = self.c, self.c.dram["node_ends"], self.chain
        if which == "tensor":
            eng.matmul(self.counts, self.none[:, 0:HI], self.none[:, :], start=False, stop=True,
                       skip_group_check=True).then_inc(self.closed, 1)
            eng.wait_ge(self.along_ready, 1)
            eng.matmul(self.before_rows, c.upper[0:HI, 0:HI], self.along[:, LO - 1:LO], start=True,
                       stop=True).then_inc(self.before_ready, 1)
        if which == "vector":
            eng.wait_ge(self.closed, 1)
            eng.tensor_tensor_scan(self.along[:, :], c.ones[0:HI, 0:LO], self.counts, 0.0, ALU.mult,
                                   ALU.add).then_inc(self.along_ready, 1)
            eng.wait_ge(self.along_ready, 1)
            eng.wait_ge(self.before_ready, 1)
            eng.tensor_scalar(self.total[:, :], self.along[:, :], self.before_rows, None, ALU.add
                              ).then_inc(self.total_ready, 1)
        if which == "sync":
            eng.wait_ge(self.total_ready, 1)
            eng.dma_start(one_row(flat[0:1]), self.zero[:, :]).then_inc(self.table_out, 16)
            eng.dma_start(flat[1:1 + NP].rearrange("(h l) -> h l", h=HI), self.total[:, :]
                          ).then_inc(self.table_out, 16)
            eng.wait_ge(self.table_out, 32)
            with c.nc.allow_non_contiguous_dma(reason="node numbers from rows to columns, once"):
                eng.dma_start(self.upto[:, :], flat[1:1 + NP].rearrange("(t p) -> p t", p=P)
                              ).then_inc(self.table_in, 16)
                eng.dma_start(self.start[:, :], flat[0:NP].rearrange("(t p) -> p t", p=P)
                              ).then_inc(self.table_in, 16)

    def finish(self, vec):
        step, (a, b) = self.chain, self.t
        vec.wait_ge(self.table_in, 32)
        step(vec.tensor_tensor(a[:, :], self.upto[:, :], self.start[:, :], ALU.is_gt))
        step(vec.tensor_scalar(b[:, :], self.upto[:, :], -1.0 - EP, None, ALU.add))
        step(vec.tensor_tensor(b[:, :], b[:, :], a[:, :], ALU.mult))
        step(vec.tensor_scalar(b[:, :], b[:, :], float(EP), None, ALU.add))
        step(vec.tensor_copy(self.c.end_idx[:, :], b[:, :]))


class Columns:

    def __init__(self, c, sb, name, table):
        self.table = table
        self.buf = sb(f"{name}_cols", [P, KD, GW])
        self.loaded, self.free = c.sems(name, "cols_in", "cols_free")

    def open(self, pe):
        pe.sem_inc(self.free, 1)

    def load(self, sp, g, n):
        sp.wait_ge(self.free, g + n + 1)
        sp.dma_start(self.buf[:, :, :], self.table[:, :, bass.ds(g * GW, GW)]).then_inc(self.loaded, 16)

    def wait(self, pe, g, n):
        pe.wait_ge(self.loaded, g * 16 + (n + 1) * 16)


class KeyValue0(Work):

    def __init__(self, c):
        self.c = c

    def buffers(self, sb):
        c = self.c
        self.cols = Columns(c, sb, "mix0", c.dram["z0_cols"])
        self.w = sb("w_kv", [P, KD, 2 * D])
        self.bias = sb("b_kv", [P, 2 * D])
        self.kv = sb("kv", [P, 2, 2 * D])
        self.wqt = sb("w_q_t", [P, KD, D])
        self.bq = sb("b_q", [P, KD])
        self.zero = sb("zeros", [P, D])
        self.top = sb("top", [P, KD])
        self.low = sb("minus_top", [P, KD])
        self.mass = sb("mass", [P, KD])
        self.inv = sb("inv_mass", [P, KD])
        self.attn = sb("attn", [P, KD, P])
        self.attn_t = sb("attn_t", [P, KD, P])
        self.map = sb("map", [P, KD, D])
        self.row = sb("map_row", [1, D])
        (self.w_in, self.made, self.product, self.rows, self.used, self.closed, self.low_ready,
         self.exp_ready, self.attn_ready, self.attn_flipped, self.attn_t_ready, self.map_done, self.map_ready,
         self.step) = c.sems(
            "kv0", "w_in", "made", "product", "rows", "used", "closed", "low_ready", "exp_ready",
            "attn_ready", "attn_flipped", "attn_t_ready", "map_done", "map_ready", "step")
        self.sums = c.bank[2]

    def first(self, eng, which):
        c, d = self.c, self.c.dram
        if which == "sync":
            eng.dma_start(self.w[:, :, :], chunked(d["L0_mix_w_qkv"])[:, :, D:]).then_inc(self.w_in, 16)
            eng.dma_start(self.bias[:, :], all_rows(d["L0_mix_b_qkv"][D:])).then_inc(self.w_in, 16)
            eng.dma_start(self.wqt[:, :, :], chunked(d["w_q_t"])).then_inc(self.w_in, 16)
            with c.nc.allow_non_contiguous_dma(reason="a bias as columns"):
                eng.dma_start(self.bq[:, :], columns(d["L0_mix_b_qkv"][0:D])).then_inc(self.w_in, 16)
        if which == "vector":
            eng.memset(self.attn[:, :, :], 0.0)
            eng.memset(self.zero[:, :], 0.0).then_inc(self.made, 1)
            eng.wait_ge(self.w_in, 4 * 16)
            eng.sem_inc(self.rows, J)
        if which == "tensor":
            self.cols.open(eng)
            eng.wait_ge(self.w_in, 4 * 16)
            eng.wait_ge(self.made, 1)
            eng.matmul(self.sums[:, 0:D], self.zero[:, 0:P], self.zero[:, :], start=True, stop=False,
                       skip_group_check=True)
            eng.sem_inc(self.used, J)

    def turn(self, eng, which, g):
        c = self.c
        if which == "sync":
            self.cols.load(eng, g, 0)
        if which == "tensor":
            self.cols.wait(eng, g, 0)

            def product(j):
                eng.wait_ge(self.rows, g * J + (j + 1 + J - reuse(j, 2)))
                for k in range(KD):
                    last = eng.matmul(c.bank[j % 2][:, :], self.cols.buf[:, k, j * P:j * P + P],
                                      self.w[:, k, :], start=(k == 0), stop=(k == KD - 1))
                last.then_inc(self.product, 1)

            product(0)
            for j in range(J):
                if j + 1 < J:
                    product(j + 1)
                eng.wait_ge(self.rows, g * J + (j + 1 + J))
                for k in range(KD):
                    last = eng.matmul(self.sums[:, k * P:k * P + P], self.kv[:, j % 2, k * P:k * P + P],
                                      self.kv[:, j % 2, D + k * P:D + k * P + P], start=False, stop=False,
                                      skip_group_check=True)
                last.then_inc(self.used, 1)
            eng.wait_ge(self.product, g * J + J)
            eng.sem_inc(self.cols.free, 1)

    def piece(self, eng, g, n):
        c = self.c
        if n % 5 == 2 and n // 5 < J:
            j = n // 5
            eng.wait_ge(self.product, g * J + (j + 1))
            eng.wait_ge(self.used, g * J + (j + 1 + J - reuse(j, 2)))
            eng.scalar_tensor_tensor(out=self.kv[:, j % 2, :], in0=self.bias[:, :],
                                     scalar=c.real[:, bass.ds(g * J + j, 1)], in1=c.bank[j % 2][:, :],
                                     op0=ALU.mult, op1=ALU.add).then_inc(self.rows, 1)

    def after(self, eng, which):
        c = self.c
        heads = [(k, h) for k in range(KD) for h in range(P // HEAD0)]
        scale = HEAD0 ** -0.5

        def block(buf, k, h):
            return buf[h * HEAD0:(h + 1) * HEAD0, k, h * HEAD0:(h + 1) * HEAD0]

        sums = self.sums[:, 0:D].rearrange("p (k n) -> p k n", k=KD)
        if which == "tensor":
            eng.matmul(self.sums[:, 0:D], self.zero[:, 0:P], self.zero[:, :], start=False, stop=True,
                       skip_group_check=True).then_inc(self.closed, 1)
            eng.wait_ge(self.attn_ready, 1)
            for k in range(KD):
                last = eng.transpose(c.bank[4][:, k * P:k * P + P], self.attn[:, k, :], c.ident[:, :])
            last.then_inc(self.attn_flipped, 1)
            eng.wait_ge(self.attn_t_ready, 1)
            for m in range(KD):
                for k in range(KD):
                    eng.matmul(c.bank[5][:, m * D + k * P:m * D + k * P + P], self.wqt[:, k, m * P:m * P + P],
                               self.attn_t[:, k, :], start=True, stop=True)
            for k in range(KD):
                last = eng.matmul(c.bank[7][0:1, k * P:k * P + P], self.bq[:, k:k + 1], self.attn_t[:, k, :],
                                  start=True, stop=True)
            last.then_inc(self.map_done, 1)
        if which == "vector":
            step = Chain(eng, self.step)
            eng.wait_ge(self.closed, 1)
            for k, h in heads:
                part = slice(h * HEAD0, (h + 1) * HEAD0)
                last = eng.tensor_reduce(self.top[part, k:k + 1], block(sums, k, h), AX.X, ALU.max)
            step(last)
            eng.tensor_scalar(self.low[:, :], self.top[:, :], -scale, None, ALU.mult).then_inc(self.low_ready, 1)
            eng.wait_ge(self.exp_ready, 1)
            step(eng.reciprocal(self.inv[:, :], self.mass[:, :]))
            for k in range(KD):
                last = eng.tensor_scalar(self.attn[:, k, :], self.attn[:, k, :], self.inv[:, k:k + 1], None,
                                         ALU.mult)
            last.then_inc(self.attn_ready, 1)
            eng.wait_ge(self.map_done, 1)
            for k in range(KD):
                part = slice(k * P, k * P + P)
                step(eng.tensor_copy(self.map[:, k, :], c.bank[5][:, k * D:k * D + D]))
                step(eng.tensor_tensor(self.map[:, k, part], c.bank[5][:, k * D + k * P:k * D + k * P + P],
                                       c.ident[:, :], ALU.add))
            eng.tensor_copy(self.row[:, :], c.bank[7][0:1, 0:D]).then_inc(self.map_ready, 1)
        if which == "scalar":
            eng.wait_ge(self.low_ready, 1)
            for k, h in heads:
                part = slice(h * HEAD0, (h + 1) * HEAD0)
                last = eng.activation(block(self.attn, k, h), block(sums, k, h), ACT.Exp,
                                      bias=self.low[part, k:k + 1], scale=scale,
                                      accum_out=self.mass[part, k:k + 1])
            last.then_inc(self.exp_ready, 1)
            eng.wait_ge(self.attn_flipped, 1)
            eng.copy(self.attn_t[:, :, :], c.bank[4][:, 0:D].rearrange("p (k n) -> p k n", k=KD)
                     ).then_inc(self.attn_t_ready, 1)


class Mlp0(Work):

    TURNS = 2
    LAST_DIFFERS = True

    def __init__(self, c, kv):
        self.c, self.kv = c, kv
        self.count = EdgeCount(c)

    def buffers(self, sb):
        c = self.c
        self.count.buffers(sb)
        self.w1 = sb("w_fc1", [P, KD, HIDDEN])
        self.x1 = sb("x1", [P, NT, D])
        self.norm = Norm(c, sb, "mixed0")
        self.b1 = sb("b_fc1", [P, KH])
        self.b1g = sb("b_fc1_all", [P, KH])
        self.w2 = sb("w_fc2", [P, KH, D])
        self.gain = sb("ln_gain", [P, KD])
        self.offset = sb("ln_offset", [P, KD])
        self.bias = sb("b_rows", [1, 3, D])
        self.z = sb("z1", [P, J, D])
        self.zt = sb("z1_cols", [P, KD, GW])
        self.u = sb("hidden", [P, KH, GW])
        (self.w_in, self.bias_product, self.w_ready, self.step, self.z_ready, self.flipped,
         self.zt_ready, self.up, self.up_taken, self.down, self.added) = c.sems(
            "mlp0", "w_in", "bias_product", "w_ready", "step", "z_ready", "flipped", "zt_ready",
            "up", "up_taken", "down", "added")
        self.mixed_product, self.x1_ready = c.sems("mixed0", "product", "x1_ready")

    def first(self, eng, which):
        c, d = self.c, self.c.dram
        self.count.first(eng, which)
        if which == "sync":
            eng.dma_start(self.w1[:, :, :], chunked(d["L0_mix_w_fc1"])).then_inc(self.w_in, 16)
            eng.dma_start(self.w2[:, :, :], chunked(d["L0_mix_w_fc2"])).then_inc(self.w_in, 16)
            eng.dma_start(self.bias[:, 0, :], one_row(d["L0_mix_b_fc2"])).then_inc(self.w_in, 16)
            eng.dma_start(self.bias[:, 1, :], one_row(d["L0_gnn_bias"])).then_inc(self.w_in, 16)
            with c.nc.allow_non_contiguous_dma(reason="biases as columns"):
                eng.dma_start(self.b1[:, :], columns(d["L0_mix_b_fc1"])).then_inc(self.w_in, 16)
                eng.dma_start(self.gain[:, :], columns(d["L0_mix_norm_g"])).then_inc(self.w_in, 16)
                eng.dma_start(self.offset[:, :], columns(d["L0_mix_norm_b"])).then_inc(self.w_in, 16)
        if which == "tensor":
            eng.wait_ge(self.w_in, 7 * 16)
            for f in range(KH):
                for k in range(KD):
                    last = eng.matmul(c.bank[7][:, f:f + 1], self.w1[:, k, f * P:f * P + P],
                                      self.offset[:, k:k + 1], start=(k == 0), stop=(k == KD - 1))
            last.then_inc(self.bias_product, 1)
        if which == "vector":
            eng.wait_ge(self.w_in, 7 * 16)
            eng.wait_ge(self.bias_product, 1)
            for k in range(KD):
                eng.tensor_scalar(self.w1[:, k, :], self.w1[:, k, :], self.gain[:, k:k + 1], None, ALU.mult)
            eng.tensor_tensor(self.bias[:, 2, :], self.bias[:, 0, :], self.bias[:, 1, :], ALU.add)
            eng.tensor_tensor(self.b1g[:, :], self.b1[:, :], c.bank[7][:, 0:KH], ALU.add
                              ).then_inc(self.w_ready, 1)
            eng.sem_inc(self.flipped, 1)
            eng.sem_inc(self.added, J)

    def mixed(self, eng, which, g):
        c, kv = self.c, self.kv
        if which == "tensor":
            kv.cols.wait(eng, g, G)
            for j in range(J):
                eng.wait_ge(self.x1_ready, g * J + (j + 1 + J - reuse(j, 2)))
                bank = c.bank[j % 2][:, 0:D]
                for k in range(KD):
                    eng.matmul(bank, kv.cols.buf[:, k, j * P:j * P + P], kv.map[:, k, :], start=(k == 0),
                               stop=False)
                eng.matmul(bank, c.ones[0:1, :], kv.row[:, :], start=False, stop=True
                           ).then_inc(self.mixed_product, 1)
            eng.wait_ge(self.mixed_product, g * J + J)
            eng.sem_inc(kv.cols.free, 1)
        if which == "scalar":
            for j in range(J):
                eng.wait_ge(self.mixed_product, g * J + (j + 1))
                eng.copy(self.x1[:, g * J + j, :], c.bank[j % 2][:, 0:D]).then_inc(self.x1_ready, 1)
            self.norm.scalar(eng, g)

    def stats(self, vec, g, j):
        vec.wait_ge(self.x1_ready, g * J + (j + 1 + J))
        vec.sem_inc(self.norm.go, 1)
        return vec.bn_stats(self.norm.stats[:, j, :], self.x1[:, g * J + j, :])

    def normalised(self, vec, g, j):
        self.norm.apply(vec, self.z[:, j, :], self.x1[:, g * J + j, :], g * J + j).then_inc(self.z_ready, 1)

    def before(self, eng, which):
        if which == "sync":
            self.kv.cols.load(eng, 0, G)
        if which == "tensor":
            eng.wait_ge(self.w_ready, 1)
            eng.wait_ge(self.kv.map_ready, 1)
            self.count.open(eng, which)
            eng.sem_inc(self.down, J)
        if which == "scalar":
            eng.sem_inc(self.zt_ready, J)
            eng.sem_inc(self.x1_ready, J)
            eng.sem_inc(self.up_taken, 3)
            eng.wait_ge(self.w_ready, 1)
        self.mixed(eng, which, 0)
        if which == "vector":
            for j in range(J):
                last = self.stats(eng, 0, j)
            step = Chain(eng, self.norm.step)
            step(last)
            self.norm.moments(eng, step, 0)
            for j in range(J):
                self.normalised(eng, 0, j)

    def piece(self, eng, g, n):
        c = self.c
        if 4 <= n < 4 + J:
            t = g * J + (n - 4)
            eng.tensor_tensor(c.x[:, bass.ds(t, 1), :], c.x[:, bass.ds(t, 1), :], self.x1[:, bass.ds(t, 1), :],
                              ALU.add).then_inc(self.step, 1)
        if isinstance(g, int) and n == 2:
            self.count.after(eng, "vector")
        if isinstance(g, int) and n == 24:
            self.count.finish(eng)
        if not isinstance(g, int):
            self.count.piece(eng, g, n)
            if n in (32, 34, 36, 38, 40):
                last = self.stats(eng, g + 1, (n - 32) // 2)
                if n == 40:
                    step = Chain(eng, self.norm.step, (g + 1) * Norm.STEPS)
                    step(last)
                    self.norm.moments(eng, step, g + 1)
            if n in (41, 42, 43, 44, 45):
                self.normalised(eng, g + 1, n - 41)
        if n in (42, 46, 50, 54, 55):
            j = (42, 46, 50, 54, 55).index(n)
            eng.wait_ge(self.step, g * J + J)
            eng.wait_ge(self.down, g * J + (j + 1 + J))
            eng.tensor_tensor(c.x[:, g * J + j, :], c.x[:, g * J + j, :], c.bank[6 + j % 2][:, 0:D], ALU.add
                              ).then_inc(self.added, 1)

    def turn(self, eng, which, g):
        c = self.c
        ups = 2 * KH
        ahead = not isinstance(g, int)
        if which == "sync" and ahead:
            self.kv.cols.load(eng, g + 1, G)
        if not ahead:
            self.count.after(eng, which)
        if which == "tensor":
            for j in range(J):
                eng.wait_ge(self.z_ready, g * J + (j + 1))
                eng.wait_ge(self.zt_ready, g * J + (j + 1 + J - reuse(j, 2)))
                for k in range(KD):
                    last = eng.transpose(c.bank[j % 2][:, k * P:k * P + P], self.z[:, j, k * P:k * P + P],
                                         c.ident[:, :])
                last.then_inc(self.flipped, 1)
            eng.wait_ge(self.zt_ready, g * J + 2 * J)
            for half in range(2):
                for f in range(KH):
                    n = half * KH + f
                    eng.wait_ge(self.up_taken, g * ups + (n + 1))
                    for k in range(KD):
                        last = eng.matmul(c.bank[2 + n % 3][:, 0:HALF], self.w1[:, k, f * P:f * P + P],
                                          self.zt[:, k, half * HALF:half * HALF + HALF], start=(k == 0),
                                          stop=(k == KD - 1))
                    last.then_inc(self.up, 1)
            if ahead:
                self.mixed(eng, which, g + 1)
                self.count.turn(eng, which, g)
            eng.wait_ge(self.up_taken, g * ups + (ups + 3))
            for j in range(J):
                bank = c.bank[6 + j % 2][:, 0:D]
                eng.wait_ge(self.added, g * J + (j + 1 + J - reuse(j, 2)))
                for f in range(KH):
                    eng.matmul(bank, self.u[:, f, j * P:j * P + P], self.w2[:, f, :], start=(f == 0), stop=False)
                eng.matmul(bank, c.ones[0:1, :], self.bias[:, 2, :], start=False, stop=True).then_inc(self.down, 1)
        if which == "scalar":
            for j in range(J):
                eng.wait_ge(self.flipped, g * J + (j + 2))
                eng.copy(self.zt[:, :, j * P:j * P + P],
                         c.bank[j % 2][:, 0:D].rearrange("p (k n) -> p k n", k=KD)).then_inc(self.zt_ready, 1)
            for half in range(2):
                for f in range(KH):
                    n = half * KH + f
                    eng.wait_ge(self.up, g * ups + (n + 1))
                    if n == 0:
                        eng.wait_ge(self.down, g * J + J)
                    eng.activation(self.u[:, f, half * HALF:half * HALF + HALF], c.bank[2 + n % 3][:, 0:HALF],
                                   ACT.Gelu, bias=self.b1g[:, f:f + 1]).then_inc(self.up_taken, 1)
            if ahead:
                self.mixed(eng, which, g + 1)


def stage(c, prefix):
    own = ExitStack()
    return own, Local(c, own, prefix)


def to_columns(pe, bank, rows, ident):
    for k in range(KD):
        last = pe.transpose(bank[:, k * P:k * P + P], rows[:, k * P:k * P + P], ident)
    return last


def split_columns(bank):
    return bank[:, 0:D].rearrange("p (k n) -> p k n", k=KD)


def fetch_nodes(c, pool, fetched, used, arrived):
    for t in range(NT):
        if t >= J:
            pool.wait_ge(used, t - J + 1)
        pool.indirect_dma_start(fetched[:, t % J, :], None, c.dram["state"][:, :],
                                bass.IndirectOffsetOnAxis(c.end_idx[:, t:t + 1], 0)
                                ).then_inc(arrived[t % J], 16)


PRODUCT_BANKS = (2, 3, 7)


def convolve0(c, logits):
    own, sb = stage(c, "conv0")
    with own:
        d = c.dram
        agg = sb("agg", [P, J, D])
        agg_t = sb("agg_cols", [P, J, KD, P])
        w = sb("w", [P, KD, D])
        gate = sb("gate", [P, KD, 16])
        gate_bias = sb("gate_bias", [1, 16])
        z = sb("z", [P, J, D])
        z_t = sb("z_cols", [P, J, KD, P])
        norm = Norm(c, sb, "conv0")
        agg_in = c.sems("conv0", *(f"agg_in{j}" for j in range(J)))
        w_in, flipped, agg_ready, product, added, z_ready, z_saved, z_flipped, z_cols, gated, logits_ready = c.sems(
            "conv0", "w_in", "flipped", "agg_ready", "product", "added", "z_ready", "z_saved", "z_flipped",
            "z_cols", "gated", "logits_ready")
        block = own.enter_context(c.nc.Block())

        @block.gpsimd
        def _(pool):
            fetch_nodes(c, pool, agg, flipped, agg_in)

        @block.sync
        def _(sp):
            sp.dma_start(w[:, :, :], chunked(d["L0_gnn_weight"])).then_inc(w_in, 16)
            sp.dma_start(gate[:, :, :], chunked(d["L0_ffn_gate_w"])).then_inc(w_in, 16)
            sp.dma_start(gate_bias[:, :], one_row(d["L0_ffn_gate_b"])).then_inc(w_in, 16)
            with sp.Fori(0, G) as g:
                sp.wait_ge(z_ready, g * J + J)
                sp.dma_start(group_rows(d["z2"], g), z[:, :, :]).then_inc(z_saved, 16)
            sp.wait_ge(z_saved, 16 * G + 16)

        @block.tensor
        def _(pe):
            class Part(Parts):
                def ahead(self, g):
                    def flip(j):
                        pe.wait_ge(agg_in[j], g * 16 + 16)
                        pe.wait_ge(agg_ready, g * J + (j + 1 + J - reuse(j, 2)))
                        to_columns(pe, c.bank[j % 2], agg[:, j, :], c.ident[:, :]).then_inc(flipped, 1)

                    def convolve(j):
                        pe.wait_ge(agg_ready, g * J + (j + 1 + J))
                        pe.wait_ge(added, g * J + (j + 1 + J - reuse(j, 3)))
                        for k in range(KD):
                            last = pe.matmul(c.bank[PRODUCT_BANKS[j % 3]][:, 0:D], agg_t[:, j, k, :], w[:, k, :],
                                             start=(k == 0), stop=(k == KD - 1))
                        last.then_inc(product, 1)

                    one_ahead(flip, convolve)

                def behind(self, g):
                    def flip(j):
                        pe.wait_ge(z_ready, g * J + (j + 1))
                        pe.wait_ge(z_cols, g * J + (j + 1 + J - reuse(j, 2)))
                        to_columns(pe, c.bank[4 + j % 2], z[:, j, :], c.ident[:, :]).then_inc(z_flipped, 1)

                    def score(j):
                        pe.wait_ge(z_cols, g * J + (j + 1 + J))
                        out = c.bank[6][:, j * 16:j * 16 + 16]
                        for k in range(KD):
                            pe.matmul(out, z_t[:, j, k, :], gate[:, k, :], start=(k == 0), stop=False)
                        pe.matmul(out, c.ones[0:1, :], gate_bias[:, :], start=False, stop=True).then_inc(gated, 1)

                    pe.wait_ge(logits_ready, g + 1)
                    one_ahead(flip, score)

            pe.wait_ge(w_in, 3 * 16)
            overlapped(pe, Part())

        @block.scalar
        def _(act):
            class Part(Parts):
                def ahead(self, g):
                    for j in range(J):
                        act.wait_ge(flipped, g * J + (j + 1))
                        act.copy(agg_t[:, j, :, :], split_columns(c.bank[j % 2])).then_inc(agg_ready, 1)

                def early(self, g):
                    norm.scalar(act, g)

                def behind(self, g):
                    for j in range(J):
                        act.wait_ge(z_flipped, g * J + (j + 2))
                        act.copy(z_t[:, j, :, :], split_columns(c.bank[4 + j % 2])).then_inc(z_cols, 1)
                    act.wait_ge(gated, g * J + J)
                    act.copy(logits[:, bass.ds(g * J, J), :],
                             c.bank[6][:, 0:J * 16].rearrange("p (j e) -> p j e", j=J)).then_inc(logits_ready, 1)

            act.sem_inc(agg_ready, J)
            act.sem_inc(z_cols, J)
            act.sem_inc(z_flipped, 1)
            act.sem_inc(logits_ready, 1)
            overlapped(act, Part(), ahead_first=True)

        @block.vector
        def _(vec):
            class Part(Parts):
                def ahead(self, g):
                    for j in range(J):
                        vec.wait_ge(product, g * J + (j + 1))
                        x = c.x[:, g * J + j, :]
                        vec.tensor_tensor(x, x, c.bank[PRODUCT_BANKS[j % 3]][:, 0:D], ALU.add).then_inc(added, 1)

                def early(self, g):
                    vec.wait_ge(added, g * J + 2 * J)
                    norm.vector(vec, g, lambda j: c.x[:, g * J + j, :])

                def late(self, g):
                    vec.wait_ge(z_saved, g * 16 + 16)
                    vec.wait_ge(z_flipped, g * J + 1)
                    for j in range(J):
                        norm.apply(vec, z[:, j, :], c.x[:, g * J + j, :], g * J + j).then_inc(z_ready, 1)

            vec.sem_inc(added, J)
            vec.sem_inc(z_saved, 16)
            overlapped(vec, Part())


B = 8
STREAMS = 4


def places(experts):
    n = (2 * N + experts * (P - 1)) // P
    return n + -n % B


class Routes:

    def __init__(self, c, sb, experts, places):
        self.experts, self.tiles = experts, places
        self.logits = sb("logits", [P, NT, experts])
        self.weight = sb("weight", [P, 2, NT])
        self.read_idx = sb("read_idx", [P, places + B], U32)
        self.write_idx = sb("write_idx", [P, places + B], U32)
        self.tile_expert = sb("tile_expert", [P, places + B], I32)


def route(c, r, name, all_softmax):
    X, T = r.experts, r.tiles
    own, sb = stage(c, name)
    with own:
        top = sb("top", [P, NT, 8])
        top_i = sb("top_i", [P, NT, 8], U32)
        e_no = sb("e_no", [P, X])
        pick_f = sb("pick_f", [P, 2, NT])
        second = sb("second", [P, NT])
        total = sb("total", [P, NT])
        exps = sb("exps", [P, NT, X])
        pick = [sb(f"pick{k}", [P, X, NT]) for k in range(2)]
        both = sb("both", [P, X, NT])
        keep = sb("same_expert", [P, X, NT])
        running = sb("running", [P, X, NT])
        place = sb("place", [P, X, NT])
        tiles = sb("tiles", [P, 4, X])
        slot = sb("slot", [P, 2, NT])
        high = sb("high", [P, 2, NT])
        low = sb("low", [P, 2, NT])
        rows_i = sb("rows_i", [P, 2 * NT + 1], I32)
        tile_no = sb("tile_no", [P, 2 * NT], BF16)
        row_no = sb("row_no", [P, 1])
        up = sb("up", [P, P])
        up_b = sb("up_b", [P, P + 1], BF16)
        low_b = sb("low_b", [P, 2 * NT], BF16)
        high_b = sb("high_b", [P, 2, NT], BF16)
        is_low = sb("is_low", [P, 2 * NT, P], BF16)
        is_high = sb("is_high", [P, 2 * NT, T], BF16)
        worth = sb("worth", [P, 2 * NT, 2, T], BF16)
        spare_i = sb("spare_i", [P, T], I32)
        v = [sb(f"v{i}", [P, T]) for i in range(4)]
        at_least = sb("at_least", [P, T + B, X])
        tile_f = sb("tile_f", [P, T + B])
        step_sem, made, exp_go, exp_done, picked, ranked, hot, listed, high_ready, worth_ready = c.sems(
            name, "step", "made", "exp_go", "exp_done", "picked", "ranked", "hot", "listed", "high_ready",
            "worth_ready")
        block = own.enter_context(c.nc.Block())
        ranks = c.bank[0][:, 0:X * NT]
        totals = c.bank[1][:, 0:X * NT]
        inverse = c.bank[2][:, 0:2 * T]

        def by_stream(ap):
            return ap[:, 0:T].rearrange("p (s m) -> p s m", s=STREAMS)

        def in_turn(ap):
            return ap[:, 0:T].rearrange("p (m s) -> p s m", s=STREAMS)

        def flat(ap):
            return ap[:, :, :].rearrange("p a b -> p (a b)")

        @block.gpsimd
        def _(pool):
            pool.memset(keep[:, :, :], 1.0)
            pool.iota(rows_i[:, 0:2 * NT], pattern=[[1, 2 * NT]], base=0, channel_multiplier=0)
            pool.iota(rows_i[:, 2 * NT:], pattern=[[0, 1]], base=1, channel_multiplier=1)
            pool.iota(spare_i[:, :], pattern=[[P, T]], base=2 * NP, channel_multiplier=1).then_inc(made, 1)
            pool.wait_ge(made, 1)
            pool.memset(keep[:, :, 0:1], 0.0).then_inc(made, 1)

        @block.scalar
        def _(act):
            act.wait_ge(exp_go, 1)
            act.activation(exps[:, :, :], exps[:, :, :], ACT.Exp).then_inc(exp_done, 1)
            for k in range(2):
                part = slice(k * NT, k * NT + NT)
                act.wait_ge(high_ready, k + 1)
                act.activation(worth[:, part, 0, :], is_high[:, part, :], ACT.Copy, scale=row_no[:, 0:1]
                               ).then_inc(worth_ready, 1)

        @block.vector
        def _(vec):
            step = Chain(vec, step_sem)
            vec.tensor_copy(e_no[:, :], c.count_up[:, 0:X])
            vec.tensor_copy(up[:, :], c.count_up[:, :])
            vec.wait_ge(made, 2)
            vec.tensor_copy(tile_no[:, :], rows_i[:, 0:2 * NT])
            vec.tensor_copy(row_no[:, :], rows_i[:, 2 * NT:])
            vec.tensor_copy(up_b[:, 0:P], c.count_up[:, :])
            vec.memset(up_b[:, P:], float(P))
            for t in range(NT):
                last = vec.max(top[:, t, :], r.logits[:, t, :])
            step(last)
            for t in range(NT):
                last = vec.max_index(top_i[:, t, :], top[:, t, :], r.logits[:, t, :])
            step(last)
            vec.tensor_tensor(exps[:, :, :], r.logits[:, :, :], top[:, :, 0:1].to_broadcast([P, NT, X]),
                              ALU.subtract).then_inc(exp_go, 1)
            for k in range(2):
                last = vec.tensor_copy(pick_f[:, k, :], top_i[:, :, k])
            step(last)
            for k in range(2):
                step(vec.tensor_tensor(pick[k][:, :, :], e_no[:, :].unsqueeze(2).to_broadcast([P, X, NT]),
                                       pick_f[:, k, :].unsqueeze(1).to_broadcast([P, X, NT]), ALU.is_equal))
                step(vec.tensor_tensor(pick[k][:, :, :], pick[k][:, :, :],
                                       c.real[:, :].unsqueeze(1).to_broadcast([P, X, NT]), ALU.mult))
            vec.tensor_tensor(both[:, :, :], pick[0][:, :, :], pick[1][:, :, :], ALU.add).then_inc(picked, 1)
            vec.wait_ge(exp_done, 1)
            step(vec.tensor_tensor(place[:, :, :], pick[1][:, :, :], exps[:, :, :].rearrange("p t e -> p e t"),
                                   ALU.mult))
            step(vec.tensor_reduce(second[:, :], place[:, :, :].rearrange("p e t -> p t e"), AX.X, ALU.add))
            w = r.weight
            if all_softmax:
                step(vec.tensor_reduce(total[:, :], exps[:, :, :], AX.X, ALU.add))
                step(vec.reciprocal(total[:, :], total[:, :]))
                step(vec.tensor_tensor(second[:, :], second[:, :], total[:, :], ALU.mult))
                step(vec.tensor_tensor(w[:, 1, :], second[:, :], total[:, :], ALU.add))
                step(vec.tensor_scalar(w[:, 1, :], w[:, 1, :], 1e-12, None, ALU.max))
                step(vec.reciprocal(w[:, 1, :], w[:, 1, :]))
                step(vec.tensor_tensor(w[:, 0, :], total[:, :], w[:, 1, :], ALU.mult))
                step(vec.tensor_tensor(w[:, 1, :], second[:, :], w[:, 1, :], ALU.mult))
            else:
                step(vec.tensor_scalar(total[:, :], second[:, :], 1.0, None, ALU.add))
                step(vec.reciprocal(w[:, 0, :], total[:, :]))
                step(vec.tensor_tensor(w[:, 1, :], second[:, :], w[:, 0, :], ALU.mult))
            vec.wait_ge(ranked, 1)
            step(vec.tensor_tensor_scan(flat(running), flat(keep), totals, 0.0, ALU.mult, ALU.add))
            t = tiles
            step(vec.tensor_scalar(t[:, 0, :], running[:, :, NT - 1], (P - 1) / 2.0, 1.0 / P, ALU.add, ALU.mult))
            step(vec.tensor_scalar(t[:, 1, :], t[:, 0, :], ROUND, None, ALU.add))
            step(vec.tensor_scalar(t[:, 0, :], t[:, 1, :], -ROUND, None, ALU.add))
            step(vec.tensor_tensor_scan(t[:, 1, :], c.ones[:, 0:X], t[:, 0, :], 0.0, ALU.mult, ALU.add))
            step(vec.tensor_tensor(t[:, 2, :], t[:, 1, :], t[:, 0, :], ALU.subtract))
            step(vec.tensor_scalar(t[:, 3, :], t[:, 2, :], float(P), None, ALU.mult))
            step(vec.tensor_tensor(flat(running), flat(running), totals, ALU.subtract))
            step(vec.tensor_tensor(flat(running), flat(running), ranks, ALU.add))
            step(vec.tensor_tensor(running[:, :, :], running[:, :, :],
                                   t[:, 3, :].unsqueeze(2).to_broadcast([P, X, NT]), ALU.add))
            for k in range(2):
                step(vec.tensor_tensor(place[:, :, :], pick[k][:, :, :], running[:, :, :], ALU.mult))
                step(vec.tensor_reduce(slot[:, k, :], place[:, :, :].rearrange("p e t -> p t e"), AX.X, ALU.add))
            step(vec.tensor_scalar(high[:, :, :], slot[:, :, :], -(P - 1) / 2.0, 1.0 / P, ALU.add, ALU.mult))
            step(vec.tensor_scalar(low[:, :, :], high[:, :, :], ROUND, None, ALU.add))
            step(vec.tensor_scalar(high[:, :, :], low[:, :, :], -ROUND, None, ALU.add))
            vec.scalar_tensor_tensor(out=low_b[:, :], in0=flat(high), scalar=-float(P), in1=flat(slot),
                                     op0=ALU.mult, op1=ALU.add)
            step(vec.scalar_tensor_tensor(out=high_b[:, :, :], in0=high[:, :, :], scalar=1.0,
                                          in1=c.real[:, :].unsqueeze(1).to_broadcast([P, 2, NT]),
                                          op0=ALU.add, op1=ALU.mult))
            for k in range(2):
                part = slice(k * NT, k * NT + NT)
                step(vec.tensor_tensor(is_high[:, part, :], high_b[:, k, :].unsqueeze(2).to_broadcast([P, NT, T]),
                                       up_b[:, 1:T + 1].unsqueeze(1).to_broadcast([P, NT, T]), ALU.is_equal))
                vec.sem_inc(high_ready, 1)
                vec.tensor_tensor(worth[:, part, 1, :], is_high[:, part, :],
                                  tile_no[:, part].unsqueeze(2).to_broadcast([P, NT, T]), ALU.mult)
                vec.tensor_tensor(is_low[:, part, :], low_b[:, part].unsqueeze(2).to_broadcast([P, NT, P]),
                                  up_b[:, 0:P].unsqueeze(1).to_broadcast([P, NT, P]), ALU.is_equal).then_inc(hot, 1)
            step(vec.tensor_tensor(at_least[:, 0:T, :], up[:, 0:T].unsqueeze(2).to_broadcast([P, T, X]),
                                   t[:, 1, :].unsqueeze(1).to_broadcast([P, T, X]), ALU.is_ge))
            step(vec.memset(tile_f[:, :], 0.0))
            step(vec.tensor_reduce(tile_f[:, 0:T], at_least[:, 0:T, :], AX.X, ALU.add))
            step(vec.tensor_scalar(tile_f[:, :], tile_f[:, :], float(X - 1), None, ALU.min))
            vec.tensor_copy(r.tile_expert[:, T:], tile_f[:, T:])
            step(vec.tensor_copy(in_turn(r.tile_expert), by_stream(tile_f)))
            vec.memset(r.read_idx[:, T:], 0)
            vec.memset(r.write_idx[:, T:], 2 * NP)
            vec.wait_ge(listed, 1)
            filled, place_no, is_second, spare = v
            step(vec.tensor_scalar(filled[:, :], inverse[:, 0:T], 0.0, None, ALU.is_gt))
            step(vec.tensor_scalar(place_no[:, :], inverse[:, T:], float(P), -1.0, ALU.mult, ALU.add))
            step(vec.tensor_tensor(place_no[:, :], place_no[:, :], inverse[:, 0:T], ALU.add))
            step(vec.tensor_scalar(is_second[:, :], place_no[:, :], float(NP), -float(NP), ALU.is_ge, ALU.mult))
            step(vec.tensor_tensor(is_second[:, :], is_second[:, :], place_no[:, :], ALU.add))
            step(vec.tensor_tensor(is_second[:, :], is_second[:, :], filled[:, :], ALU.mult))
            step(vec.tensor_copy(in_turn(r.read_idx), by_stream(is_second)))
            step(vec.tensor_copy(spare[:, :], spare_i[:, :]))
            step(vec.tensor_tensor(place_no[:, :], place_no[:, :], spare[:, :], ALU.subtract))
            step(vec.tensor_tensor(place_no[:, :], place_no[:, :], filled[:, :], ALU.mult))
            step(vec.tensor_tensor(place_no[:, :], place_no[:, :], spare[:, :], ALU.add))
            step(vec.tensor_copy(in_turn(r.write_idx), by_stream(place_no)))

        @block.tensor
        def _(pe):
            pe.wait_ge(picked, 1)
            pe.matmul(ranks, c.upper[:, :], flat(both), start=True, stop=True)
            pe.matmul(totals, c.ones[:, :], flat(both), start=True, stop=True).then_inc(ranked, 1)
            for n in range(2 * NT):
                if n % NT == 0:
                    pe.wait_ge(hot, n // NT + 1)
                    pe.wait_ge(worth_ready, n // NT + 1)
                last = pe.matmul(inverse, is_low[:, n, :], worth[:, n, :, :].rearrange("p a t -> p (a t)"),
                                 start=(n == 0), stop=(n == 2 * NT - 1))
            last.then_inc(listed, 1)


def experts(c, r, name, table, w1, b1, w2, b2, act_func):
    X, T = r.experts, r.tiles
    F = w1.shape[2]
    KF = F // P
    assert T % B == 0
    own, sb = stage(c, name)
    with own:
        rows = sb("rows", [P, B, D])
        cols = sb("cols", [P, 2, KD, P])
        up_w = sb("up_w", [P, STREAMS, KD, F])
        up_b = sb("up_b", [P, STREAMS, KF])
        down_w = sb("down_w", [P, STREAMS, KF, D])
        down_b = sb("down_b", [P, STREAMS, D])
        hidden = sb("hidden", [P, 2, KF, P])
        result = sb("result", [P, B, D])
        idx = sb("idx", [P, 2, B], U32)
        first_sent = sb("first_sent", [1, B])
        arrived = c.sems(name, *(f"arrived{q}" for q in range(B)))
        sent = c.sems(name, *(f"sent{q}" for q in range(B)))
        up_in = c.sems(name, *(f"up_in{s}" for s in range(STREAMS)))
        up_b_in = c.sems(name, *(f"up_b_in{s}" for s in range(STREAMS)))
        down_in = c.sems(name, *(f"down_in{s}" for s in range(STREAMS)))
        down_b_in = c.sems(name, *(f"down_b_in{s}" for s in range(STREAMS)))
        staged, go, flipped, cols_ready, up, hidden_ready, down, result_ready = c.sems(
            name, "staged", "go", "flipped", "cols_ready", "up", "hidden_ready", "down", "result_ready")
        passed = c.sem(f"{name}_passed")
        block = own.enter_context(c.nc.Block())
        out = c.dram["expert_out"]
        turns = T // B
        table_w1 = w1.rearrange("e (k p) f -> e p k f", p=P)
        table_w2 = w2.rearrange("e (k p) d -> e p k d", p=P)
        table_b2 = b2.rearrange("e (a d) -> e a d", a=1).to_broadcast([X, P, D])

        @block.gpsimd
        def _(pool):
            def gather(q):
                pool.indirect_dma_start(rows[:, q, :], None, table[:, :],
                                        bass.IndirectOffsetOnAxis(idx[:, 0, q:q + 1], 0)).then_inc(arrived[q], 16)

            for q in range(B):
                pool.dma_start(first_sent[0:1, q:q + 1], c.eps[0:1, 0:1]).then_inc(sent[q], 16)
            pool.tensor_copy(idx[:, 0, :], r.read_idx[:, 0:B]).then_inc(staged, 1)
            pool.wait_ge(staged, 1)
            for q in range(B):
                gather(q)
            with pool.Fori(0, turns) as i:
                for q in range(B):
                    pool.wait_ge(arrived[q], i * 16 + 16)
                    pool.wait_ge(sent[q], i * 16 + 16)
                pool.sem_inc(go, 1)
                pool.tensor_copy(idx[:, 0, :], r.read_idx[:, bass.ds(i * B + B, B)])
                pool.tensor_copy(idx[:, 1, :], r.write_idx[:, bass.ds(i * B, B)]).then_inc(staged, 1)
                pool.wait_ge(staged, i + 2)
                for q in range(B):
                    pool.wait_ge(flipped, i * B + (q + 1))
                    pool.sem_inc(go, 1)
                    gather(q)
                    pool.wait_ge(result_ready, i * B + (q + 3))
                    pool.sem_inc(go, 1)
                    pool.indirect_dma_start(out[:, :], bass.IndirectOffsetOnAxis(idx[:, 1, q:q + 1], 0),
                                            result[:, q, :], None).then_inc(sent[q], 16)
            for q in range(B):
                pool.wait_ge(sent[q], turns * 16 + 16)
                pool.wait_ge(arrived[q], turns * 16 + 16)

        @block.sync
        def _(sp):
            def expert(n):
                return sp.value_load(r.tile_expert[0:1, bass.ds(n, 1)], min_val=0, max_val=X - 1)

            def load(i, q, e, held):
                b = q % STREAMS
                free = ((up, i * B + (q + 1)), (hidden_ready, i * B + (q + 2)), (down, i * B + (q + 2)),
                        (result_ready, i * B + (q + 3)))
                with sp.If(e != held):
                    for (used, count), (buf, table, arrival) in zip(free, weights_of(b)):
                        sp.wait_ge(used, count)
                        sp.dma_start(buf, table[e]).then_inc(arrival, 16)
                with sp.Else():
                    for (used, count), (_, _, arrival) in zip(free, weights_of(b)):
                        sp.wait_ge(used, count)
                        sp.sem_inc(arrival, 16)

            def weights_of(b):
                return ((up_w[:, b, :, :], table_w1, up_in[b]), (up_b[:, b, :], b1, up_b_in[b]),
                        (down_w[:, b, :, :], table_w2, down_in[b]), (down_b[:, b, :], table_b2, down_b_in[b]))

            for b in range(STREAMS):
                e = expert(b)
                for buf, table, arrival in weights_of(b):
                    sp.dma_start(buf, table[e]).then_inc(arrival, 16)
            with sp.Fori(0, turns) as i:
                e = [expert(i * B + q) for q in range(B + STREAMS)]
                for q in range(B):
                    load(i, q, e[q + STREAMS], e[q])
            for b in range(STREAMS):
                for _, _, arrival in weights_of(b):
                    sp.wait_ge(arrival, 16 * (T // STREAMS + 1))

        @block.tensor
        def _(pe):
            def flip(q, arrivals, copies):
                pe.wait_ge(arrived[q % B], arrivals)
                if copies is not None:
                    pe.wait_ge(cols_ready, copies)
                to_columns(pe, c.bank[q % 2], rows[:, q % B, :], c.ident[:, :]).then_inc(flipped, 1)

            def first(q, n, weights):
                b, s = q % 2, q % STREAMS
                pe.wait_ge(up_in[s], weights)
                pe.wait_ge(cols_ready, n + 1)
                if not (isinstance(n, int) and n == 0):
                    pe.wait_ge(hidden_ready, n)
                for f in range(KF):
                    for k in range(KD):
                        last = pe.matmul(c.bank[2 + b][:, f * P:f * P + P], up_w[:, s, k, f * P:f * P + P],
                                         cols[:, b, k, :], start=(k == 0), stop=(k == KD - 1))
                last.then_inc(up, 1)

            flip(0, 16, None)
            flip(1, 16, None)
            first(0, 0, 16)
            with pe.Fori(0, turns) as i:
                for q in range(B):
                    b = q % 2
                    flip(q + 2, i * 16 + (32 if q + 2 >= B else 16), i * B + (q + 1))
                    first(q + 1, i * B + (q + 1), i * (16 * B // STREAMS) + 16 * ((q + 1) // STREAMS + 1))
                    s = q % STREAMS
                    pe.wait_ge(down_in[s], i * (16 * B // STREAMS) + 16 * (q // STREAMS + 1))
                    pe.wait_ge(hidden_ready, i * B + (q + 2))
                    pe.wait_ge(result_ready, i * B + (q + 1))
                    for f in range(KF):
                        last = pe.matmul(c.bank[4 + b][:, 0:D], hidden[:, b, f, :], down_w[:, s, f, :],
                                         start=(f == 0), stop=(f == KF - 1))
                    last.then_inc(down, 1)

        @block.scalar
        def _(act):
            def unit(q, n, biases):
                b, s = q % 2, q % STREAMS
                act.wait_ge(up_b_in[s], biases)
                act.wait_ge(up, n + 1)
                if not (isinstance(n, int) and n == 0):
                    act.wait_ge(down, n)
                    act.sem_inc(passed, 1)
                for f in range(KF):
                    last = act.activation(hidden[:, b, f, :], c.bank[2 + b][:, f * P:f * P + P], act_func,
                                          bias=up_b[:, s, f:f + 1])
                last.then_inc(hidden_ready, 1)

            act.sem_inc(hidden_ready, 1)
            unit(0, 0, 16)
            with act.Fori(0, turns) as i:
                for q in range(B):
                    unit(q + 1, i * B + (q + 1), i * (16 * B // STREAMS) + 16 * ((q + 1) // STREAMS + 1))

        @block.vector
        def _(vec):
            vec.sem_inc(down, 1)
            vec.sem_inc(result_ready, 2)
            for q in range(2):
                vec.wait_ge(flipped, q + 1)
                vec.tensor_copy(cols[:, q, :, :], split_columns(c.bank[q])).then_inc(cols_ready, 1)
            with vec.Fori(0, turns) as i:
                for q in range(B):
                    b = q % 2
                    vec.wait_ge(flipped, i * B + (q + 3))
                    vec.wait_ge(up, i * B + (q + 1))
                    vec.tensor_copy(cols[:, b, :, :], split_columns(c.bank[b])).then_inc(cols_ready, 1)
                    vec.wait_ge(sent[q], i * 16 + 16)
                    s = q % STREAMS
                    vec.wait_ge(down_b_in[s], i * (16 * B // STREAMS) + 16 * (q // STREAMS + 1))
                    vec.wait_ge(down, i * B + (q + 2))
                    vec.tensor_tensor(result[:, q, :], c.bank[4 + b][:, 0:D], down_b[:, s, :], ALU.add
                                      ).then_inc(result_ready, 1)


class ExpertSum:

    def __init__(self, c, r, sb, name, table):
        self.c, self.r, self.table = c, r, table
        self.y = sb("y_in", [P, 2, NT, D])
        self.total = sb("total", [P, NT, D])
        self.rows_in, self.first_in, self.summed, self.go = c.sems(name, "rows_in", "first_in", "summed", "go")

    def sync(self, sp, g):
        part = bass.ds(g * J, J)
        sp.dma_start(self.total[:, part, :], group_rows(self.table, g)).then_inc(self.rows_in, 16)
        for k in range(2):
            half = self.c.dram["expert_out"][k * NP:k * NP + NP, :]
            sp.dma_start(self.y[:, k, part, :], group_rows(half, g)).then_inc(self.rows_in, 16)
        sp.wait_ge(self.rows_in, g * 48 + 48)
        sp.sem_inc(self.go, 1)

    def vector(self, vec, g):
        vec.wait_ge(self.rows_in, g * 48 + 48)
        vec.sem_inc(self.go, 1)
        for k, done in enumerate((self.first_in, self.summed)):
            for j in range(J):
                total = self.total[:, g * J + j, :]
                vec.scalar_tensor_tensor(out=total, in0=self.y[:, k, g * J + j, :],
                                         scalar=self.r.weight[:, k, bass.ds(g * J + j, 1)], in1=total, op0=ALU.mult,
                                         op1=ALU.add).then_inc(done, 1)
            vec.wait_ge(done, g * J + J)
            vec.sem_inc(self.go, 1)


def finish_layer0(c, r):
    own, sb = stage(c, "finish0")
    with own:
        d = c.dram
        es = ExpertSum(c, r, sb, "sum0", d["z2"])
        norm_a, norm_b = Norm(c, sb, "finish0a"), Norm(c, sb, "finish0b")
        gamma = sb("gamma", [P, D])
        beta = sb("beta", [P, D])
        w = sb("w", [P, KD, D])
        b = sb("b", [1, D])
        y = sb("y", [P, J, D])
        xb = sb("x_beta", [P, J, D])
        z = sb("z", [P, J, D])
        zt = sb("z_cols", [P, KD, GW])
        h = sb("h", [P, J, D])
        (w_in, y_ready, xb_ready, y_used, x_ready, z_ready, flipped, zt_ready, zt_saved, product, h_ready,
         h_saved) = c.sems(
            "finish0", "w_in", "y_ready", "xb_ready", "y_used", "x_ready", "z_ready", "flipped", "zt_ready",
            "zt_saved", "product", "h_ready", "h_saved")
        act_go, pool_go = c.sems("finish0", "act_go", "pool_go")
        block = own.enter_context(c.nc.Block())

        @block.sync
        def _(sp):
            sp.dma_start(w[:, :, :], chunked(d["w_p1_t"])).then_inc(w_in, 16)
            sp.dma_start(b[:, :], one_row(d["L1_gnn_bp1"])).then_inc(w_in, 16)
            sp.dma_start(gamma[:, :], all_rows(d["L0_ffn_gamma"])).then_inc(w_in, 16)
            sp.dma_start(beta[:, :], all_rows(d["L0_ffn_beta"])).then_inc(w_in, 16)
            def save(g):
                sp.wait_ge(zt_ready, g * J + 2 * J)
                sp.dma_start(d["z3_cols"][:, :, bass.ds(g * GW, GW)], zt[:, :, :]).then_inc(zt_saved, 16)
                sp.wait_ge(h_ready, g * J + 2 * J)
                sp.dma_start(group_rows(d["h"], g), h[:, :, :]).then_inc(h_saved, 16)

            with sp.Fori(0, G) as g:
                es.sync(sp, g)
            with sp.Fori(0, G) as g:
                save(g)
            sp.wait_ge(zt_saved, 16 * G + 16)
            sp.wait_ge(h_saved, 16 * G + 16)

        @block.gpsimd
        def _(pool):
            pool.wait_ge(w_in, 4 * 16)
            with pool.Fori(0, G) as g:
                pool.wait_ge(x_ready, g + 1)
                pool.sem_inc(pool_go, 1)
                pool.tensor_tensor(xb[:, :, :], c.x[:, bass.ds(g * J, J), :],
                                   beta[:, :].unsqueeze(1).to_broadcast([P, J, D]), ALU.add).then_inc(xb_ready, 1)

        @block.tensor
        def _(pe):
            class Part(Parts):
                def behind(self, g):
                    def flip(j):
                        pe.wait_ge(z_ready, g * J + (j + 1))
                        pe.wait_ge(zt_ready, g * J + (j + 1 + J - reuse(j, 2)))
                        to_columns(pe, c.bank[4 + j % 2], z[:, j, :], c.ident[:, :]).then_inc(flipped, 1)

                    flip(0)
                    for j in range(J):
                        if j + 1 < J:
                            flip(j + 1)
                        pe.wait_ge(zt_ready, g * J + (j + 1 + J))
                        pe.wait_ge(h_ready, g * J + (j + 1 + J - reuse(j, 2)))
                        out = c.bank[6 + j % 2][:, 0:D]
                        for k in range(KD):
                            pe.matmul(out, zt[:, k, j * P:j * P + P], w[:, k, :], start=(k == 0), stop=False)
                        pe.matmul(out, c.ones[0:1, :], b[:, :], start=False, stop=True).then_inc(product, 1)

            pe.wait_ge(w_in, 4 * 16)
            overlapped(pe, Part())

        @block.scalar
        def _(act):
            class Part(Parts):
                def early(self, g):
                    norm_a.scalar(act, g)

                def middle(self, g):
                    act.wait_ge(norm_a.step, g * Norm.STEPS + Norm.STEPS)
                    act.sem_inc(act_go, 1)
                    for j in range(J):
                        norm_a.apply_act(act, y[:, j, :], es.total[:, g * J + j, :], g * J + j).then_inc(y_ready, 1)

                def late(self, g):
                    if isinstance(g, int) and g == 0:
                        norm_b.scalar(act, g)
                    act.wait_ge(norm_b.step, g * Norm.STEPS + Norm.STEPS)
                    act.sem_inc(act_go, 1)
                    for j in range(J):
                        norm_b.apply_act(act, z[:, j, :], c.x[:, g * J + j, :], g * J + j).then_inc(z_ready, 1)

                def behind(self, g):
                    def columns_of(j):
                        act.wait_ge(flipped, g * J + (j + 1))
                        act.copy(zt[:, :, j * P:j * P + P], split_columns(c.bank[4 + j % 2])).then_inc(zt_ready, 1)

                    act.wait_ge(zt_saved, g * 16 + 16)
                    act.wait_ge(h_saved, g * 16 + 16)
                    columns_of(0)
                    for j in range(J):
                        if j + 1 < J:
                            columns_of(j + 1)
                        act.wait_ge(product, g * J + (j + 1))
                        act.activation(h[:, j, :], c.bank[6 + j % 2][:, 0:D], ACT.Relu).then_inc(h_ready, 1)
                        if j == J // 2 and not (isinstance(g, int) and g == G - 1):
                            norm_b.scalar(act, g + 1)

            act.sem_inc(zt_ready, J)
            act.sem_inc(h_ready, J)
            act.sem_inc(zt_saved, 16)
            act.sem_inc(h_saved, 16)
            overlapped(act, Part())

        @block.vector
        def _(vec):
            class Part(Parts):
                def ahead(self, g):
                    es.vector(vec, g)

                def early(self, g):
                    norm_a.vector(vec, g, lambda j: es.total[:, g * J + j, :])

                def late(self, g):
                    vec.wait_ge(y_ready, g * J + J)
                    vec.tensor_tensor(y[:, :, :], y[:, :, :], gamma[:, :].unsqueeze(1).to_broadcast([P, J, D]),
                                      ALU.mult).then_inc(y_used, 1)
                    vec.wait_ge(y_used, g + 1)
                    vec.wait_ge(xb_ready, g + 1)
                    vec.tensor_tensor(c.x[:, bass.ds(g * J, J), :], y[:, :, :], xb[:, :, :], ALU.add
                                      ).then_inc(x_ready, 1)
                    vec.wait_ge(x_ready, g + 2)
                    norm_b.vector(vec, g, lambda j: c.x[:, g * J + j, :])

            vec.wait_ge(w_in, 4 * 16)
            vec.sem_inc(x_ready, 1)
            overlapped(vec, Part())


class KeyValue1(Work):

    W = P + PER1

    def __init__(self, c):
        self.c = c

    def buffers(self, sb):
        c = self.c
        self.cols = Columns(c, sb, "mix1", c.dram["z3_cols"])
        self.w = sb("w_kv", [P, KD, 2 * D])
        self.bias = sb("b_kv", [P, 2 * D])
        self.raw = sb("kv_raw", [P, 2, 2 * D])
        self.low = sb("k_low", [P, 2, D])
        self.key = sb("key", [P, 2, D])
        self.value = sb("value", [P, 2, KD, P + 1])
        self.zero = sb("zeros", [P, KD * (P + 1)])
        self.map = sb("map", [P, KD, self.W])
        self.sums = c.bank[2][:, 0:KD * (P + 1)]
        (self.w_in, self.made, self.product, self.rows, self.low_ready, self.exp_ready, self.key_ready,
         self.value_ready, self.used, self.closed, self.map_ready, self.step) = c.sems(
            "kv1", "w_in", "made", "product", "rows", "low_ready", "exp_ready", "key_ready", "value_ready", "used",
            "closed", "map_ready", "step")

    def first(self, eng, which):
        c, d = self.c, self.c.dram
        if which == "sync":
            eng.dma_start(self.w[:, :, 0:D], chunked(d["L1_mix_wk"])).then_inc(self.w_in, 16)
            eng.dma_start(self.w[:, :, D:], chunked(d["L1_mix_wv"])).then_inc(self.w_in, 16)
            eng.dma_start(self.bias[:, 0:D], all_rows(d["L1_mix_bk"])).then_inc(self.w_in, 16)
            eng.dma_start(self.bias[:, D:], all_rows(d["L1_mix_bv"])).then_inc(self.w_in, 16)
        if which == "vector":
            eng.memset(self.map[:, :, :], 0.0)
            eng.memset(self.zero[:, :], 0.0).then_inc(self.made, 1)
            eng.wait_ge(self.w_in, 4 * 16)
            eng.sem_inc(self.rows, J)
        if which == "scalar":
            eng.sem_inc(self.value_ready, J)
        if which == "tensor":
            self.cols.open(eng)
            eng.wait_ge(self.w_in, 4 * 16)
            eng.wait_ge(self.made, 1)
            eng.matmul(self.sums, self.zero[:, 0:P], self.zero[:, :], start=True, stop=False,
                       skip_group_check=True)
            eng.sem_inc(self.used, J)

    def turn(self, eng, which, g):
        c = self.c
        if which == "sync":
            self.cols.load(eng, g, 0)
        if which == "tensor":
            self.cols.wait(eng, g, 0)

            def product(j):
                eng.wait_ge(self.rows, g * J + (j + 1 + J - reuse(j, 2)))
                for k in range(KD):
                    last = eng.matmul(c.bank[j % 2][:, :], self.cols.buf[:, k, j * P:j * P + P],
                                      self.w[:, k, :], start=(k == 0), stop=(k == KD - 1))
                last.then_inc(self.product, 1)

            product(0)
            for j in range(J):
                if j + 1 < J:
                    product(j + 1)
                eng.wait_ge(self.key_ready, g * J + (j + 1))
                eng.wait_ge(self.value_ready, g * J + (j + 1 + J))
                for k in range(KD):
                    last = eng.matmul(self.sums[:, k * (P + 1):(k + 1) * (P + 1)], self.key[:, j % 2, k * P:k * P + P],
                                      self.value[:, j % 2, k, :], start=False, stop=False, skip_group_check=True)
                last.then_inc(self.used, 1)
            eng.wait_ge(self.product, g * J + J)
            eng.sem_inc(self.cols.free, 1)
        if which == "scalar":
            for j in range(J):
                s = j % 2
                eng.wait_ge(self.low_ready, g * J + (j + 1))
                eng.activation(self.low[:, s, :], self.low[:, s, :], ACT.Exp).then_inc(self.exp_ready, 1)
                real = c.real[:, bass.ds(g * J + j, 1)]
                eng.activation(self.value[:, s, :, 0:P], self.raw[:, s, D:].rearrange("p (k n) -> p k n", k=KD),
                               ACT.Copy, scale=real)
                for k in range(KD):
                    last = eng.copy(self.value[:, s, k, P:P + 1], real)
                last.then_inc(self.value_ready, 1)

    def piece(self, eng, g, n):
        c = self.c
        if n % 5 == 2 and n // 5 < J:
            j = n // 5
            eng.wait_ge(self.product, g * J + (j + 1))
            eng.wait_ge(self.used, g * J + (j + 1 + J - reuse(j, 2)))
            eng.tensor_tensor(self.raw[:, j % 2, :], c.bank[j % 2][:, :], self.bias[:, :], ALU.add
                              ).then_inc(self.rows, 1)
        if n % 5 == 3 and n // 5 < J:
            j = n // 5
            eng.wait_ge(self.rows, g * J + (j + 1 + J))
            eng.tensor_scalar(self.low[:, j % 2, :], self.raw[:, j % 2, 0:D], 0.0, None, ALU.min
                              ).then_inc(self.low_ready, 1)
        if n % 5 == 0 and 1 <= n // 5 <= J:
            j = n // 5 - 1
            eng.wait_ge(self.exp_ready, g * J + (j + 1))
            eng.scalar_tensor_tensor(out=self.key[:, j % 2, :], in0=self.raw[:, j % 2, 0:D], scalar=0.0,
                                     in1=self.low[:, j % 2, :], op0=ALU.max, op1=ALU.add
                                     ).then_inc(self.key_ready, 1)

    def after(self, eng, which):
        if which == "tensor":
            eng.matmul(self.sums, self.zero[:, 0:P], self.zero[:, :], start=False, stop=True,
                       skip_group_check=True).then_inc(self.closed, 1)
        if which == "vector":
            eng.wait_ge(self.closed, 1)
            for k in range(KD):
                for h in range(PER1):
                    part = slice(h * HEAD1, (h + 1) * HEAD1)
                    at = k * (P + 1)
                    eng.tensor_copy(self.map[part, k, part], self.sums[part, at + h * HEAD1:at + (h + 1) * HEAD1])
                    last = eng.tensor_copy(self.map[part, k, P + h:P + h + 1], self.sums[part, at + P:at + P + 1])
            last.then_inc(self.map_ready, 1)


class Mixed1(Work):

    TURNS = 2

    def __init__(self, c, kv, layer):
        self.c, self.kv, self.layer = c, kv, layer

    def buffers(self, sb):
        c = self.c
        self.wx = sb("w_x", [P, KD, D])
        self.bx = sb("b_x", [1, D])
        self.own_product, self.own_ready = c.sems("mixed1", "own_product", "own_ready")
        self.wq = sb("w_q", [P, KD, D])
        self.bq = sb("b_q", [P, KD])
        self.wo = sb("w_o", [P, KD, D])
        self.bo = sb("b_o", [1, D])
        self.q = sb("q", [P, KD, GW])
        self.low = sb("q_low", [P, 2, HALF])
        self.inv = sb("inv", [P, J, 2 * PER1])
        self.heads = sb("heads", [P, J, D])
        self.heads_t = sb("heads_t", [P, 2, KD, P])
        (self.w_in, self.query, self.low_ready, self.exp_ready, self.relu_ready, self.q_ready, self.spread,
         self.inverse, self.heads_ready, self.flipped, self.heads_t_ready, self.product, self.added,
         self.step) = c.sems(
            "mixed1", "w_in", "query", "low_ready", "exp_ready", "relu_ready", "q_ready", "spread", "inverse",
            "heads_ready", "flipped", "heads_t_ready", "product", "added", "step")

    def first(self, eng, which):
        c, d = self.c, self.c.dram
        if which == "sync":
            eng.dma_start(self.wq[:, :, :], chunked(d["L1_mix_wq"])).then_inc(self.w_in, 16)
            eng.dma_start(self.wo[:, :, :], chunked(d["L1_mix_wo"])).then_inc(self.w_in, 16)
            eng.dma_start(self.bo[:, :], one_row(d["L1_mix_bo"])).then_inc(self.w_in, 16)
            eng.dma_start(self.wx[:, :, :], chunked(d["w_m1_t"])[:, 0:KD, :]).then_inc(self.w_in, 16)
            eng.dma_start(self.bx[:, :], one_row(d["L1_gnn_bm1"])).then_inc(self.w_in, 16)
            with c.nc.allow_non_contiguous_dma(reason="a bias as columns"):
                eng.dma_start(self.bq[:, :], columns(d["L1_mix_bq"])).then_inc(self.w_in, 16)

    def before(self, eng, which):
        eng.wait_ge(self.w_in, 6 * 16)
        if which == "tensor":
            eng.wait_ge(self.kv.map_ready, 1)
            eng.sem_inc(self.spread, 1)
        if which == "vector":
            eng.sem_inc(self.q_ready, 2)
            eng.sem_inc(self.heads_ready, J)
            eng.sem_inc(self.added, J)
        if which == "scalar":
            eng.sem_inc(self.heads_t_ready, J)
            eng.sem_inc(self.own_ready, 1)

    def turn(self, eng, which, g):
        c, kv = self.c, self.kv
        parts = [(m, half) for half in range(2) for m in range(KD)]
        if which == "sync":
            kv.cols.load(eng, g, G)
        if which == "tensor":
            kv.cols.wait(eng, g, G)
            for n, (m, half) in enumerate(parts):
                eng.wait_ge(self.q_ready, g * 4 + (n + 1))
                for k in range(KD):
                    last = eng.matmul(c.bank[n % 2][:, 0:HALF], self.wq[:, k, m * P:m * P + P],
                                      kv.cols.buf[:, k, half * HALF:half * HALF + HALF], start=(k == 0),
                                      stop=(k == KD - 1))
                last.then_inc(self.query, 1)
            for j in range(J):
                eng.wait_ge(self.own_ready, g * J + (j + 1))
                own_product(eng, c, c.bank[2][:, 0:D], [kv.cols.buf[:, k, j * P:j * P + P] for k in range(KD)],
                            self.wx, self.bx).then_inc(self.own_product, 1)
            eng.wait_ge(self.q_ready, g * 4 + 6)
            eng.wait_ge(self.own_product, g * J + J)
            eng.sem_inc(kv.cols.free, 1)
            for j in range(J):
                eng.wait_ge(self.heads_ready, g * J + (j + 1 + J - reuse(j, 2)))
                for k in range(KD):
                    last = eng.matmul(c.bank[3 + j % 2][:, k * kv.W:(k + 1) * kv.W], self.q[:, k, j * P:j * P + P],
                                      kv.map[:, k, :], start=True, stop=True)
                last.then_inc(self.spread, 1)
            for j in range(J):
                eng.wait_ge(self.heads_ready, g * J + (j + 1 + J))
                eng.wait_ge(self.heads_t_ready, g * J + (j + 1 + J - reuse(j, 2)))
                to_columns(eng, c.bank[5 + j % 2], self.heads[:, j, :], c.ident[:, :]).then_inc(self.flipped, 1)
                eng.wait_ge(self.heads_t_ready, g * J + (j + 1 + J))
                eng.wait_ge(self.added, g * J + (j + 1 + J - 1))
                out = c.bank[7][:, 0:D]
                for k in range(KD):
                    eng.matmul(out, self.heads_t[:, j % 2, k, :], self.wo[:, k, :], start=(k == 0), stop=False)
                eng.matmul(out, c.ones[0:1, :], self.bo[:, :], start=False, stop=True).then_inc(self.product, 1)
        if which == "scalar":
            for n, (m, half) in enumerate(parts):
                eng.wait_ge(self.low_ready, g * 4 + (n + 1))
                eng.activation(self.low[:, n % 2, :], self.low[:, n % 2, :], ACT.Exp).then_inc(self.exp_ready, 1)
                if n == 0:
                    eng.wait_ge(self.spread, g * J + 1)
                eng.activation(self.q[:, m, half * HALF:half * HALF + HALF], c.bank[n % 2][:, 0:HALF], ACT.Relu,
                               bias=self.bq[:, m:m + 1]).then_inc(self.relu_ready, 1)
            for j in range(J):
                eng.wait_ge(self.own_product, g * J + (j + 1))
                eng.copy(self.layer.own[:, g * J + j, :], c.bank[2][:, 0:D]).then_inc(self.own_ready, 1)
            for j in range(J):
                eng.wait_ge(self.flipped, g * J + (j + 1))
                eng.copy(self.heads_t[:, j % 2, :, :], split_columns(c.bank[5 + j % 2])
                         ).then_inc(self.heads_t_ready, 1)

    def piece(self, eng, g, n):
        c, kv = self.c, self.kv
        parts = [(m, half) for half in range(2) for m in range(KD)]
        if n in (2, 5, 8, 11):
            p = (n - 2) // 3
            m, half = parts[p]
            eng.wait_ge(self.query, g * 4 + (p + 1))
            eng.tensor_scalar(self.low[:, p % 2, :], c.bank[p % 2][:, 0:HALF], self.bq[:, m:m + 1], 0.0,
                              ALU.add, ALU.min).then_inc(self.low_ready, 1)
        if n in (4, 7, 10, 13):
            p = (n - 4) // 3
            m, half = parts[p]
            eng.wait_ge(self.exp_ready, g * 4 + (p + 1))
            eng.wait_ge(self.relu_ready, g * 4 + (p + 1))
            part = self.q[:, m, half * HALF:half * HALF + HALF]
            eng.tensor_tensor(part, part, self.low[:, p % 2, :], ALU.add).then_inc(self.q_ready, 1)
        if n in (26, 29, 32, 35, 38):
            j = (n - 26) // 3
            eng.wait_ge(self.spread, g * J + (j + 2))
            bank = c.bank[3 + j % 2][:, 0:KD * kv.W].rearrange("p (k w) -> p k w", k=KD)
            inv = self.inv[:, j, :].rearrange("p (k h) -> p k h", k=KD)
            eng.tensor_scalar(inv, bank[:, :, P:], 1e-6, None, ALU.add).then_inc(self.inverse, 1)
            eng.wait_ge(self.inverse, g * 2 * J + (2 * j + 1))
            eng.reciprocal(inv, inv).then_inc(self.inverse, 1)
            eng.wait_ge(self.inverse, g * 2 * J + (2 * j + 2))
            for k in range(KD):
                last = eng.tensor_tensor(
                    self.heads[:, j, k * P:k * P + P].rearrange("p (h e) -> p h e", h=PER1),
                    bank[:, k, 0:P].rearrange("p (h e) -> p h e", h=PER1),
                    inv[:, k, :].unsqueeze(2).to_broadcast([P, PER1, HEAD1]), ALU.mult)
            last.then_inc(self.heads_ready, 1)
        if n in (41, 44, 47, 50, 53):
            j = (n - 41) // 3
            eng.wait_ge(self.product, g * J + (j + 1))
            eng.tensor_tensor(c.x[:, g * J + j, :], c.x[:, g * J + j, :], c.bank[7][:, 0:D], ALU.add
                              ).then_inc(self.added, 1)


class Own(Work):

    TURNS = SLOTS

    def __init__(self, c, name, layer, w, b, offset=None):
        self.c, self.name, self.layer, self.w_table, self.b_table = c, name, layer, w, b
        self.offset_table = offset

    def buffers(self, sb):
        self.w = sb("w_x", [P, KD, D])
        self.b = sb("b_x", [1, D])
        self.cols = sb("x_cols", [P, 2, KD, P])
        self.rows = sb("x_rows", [P, 2, D])
        self.staged = self.c.sem(self.name + "_staged")
        self.w_in, self.flipped, self.cols_ready, self.product, self.ready = self.c.sems(
            self.name, "w_in", "flipped", "cols_ready", "product", "ready")

        if self.offset_table is not None:
            self.offset = sb("offset", [P, D])
            self.offset_in = self.c.sem(self.name + "_offset_in")

    def piece(self, vec, g, n):
        if self.offset_table is not None and n in range(4, 4 + J):
            x = self.c.x[:, g * J + (n - 4), :]
            vec.tensor_tensor(x, x, self.offset[:, :], ALU.add)

    def first(self, eng, which):
        if self.offset_table is not None:
            if which == "sync":
                eng.dma_start(self.offset[:, :], all_rows(self.offset_table)).then_inc(self.offset_in, 16)
            if which == "vector":
                eng.wait_ge(self.offset_in, 16)
        if which == "sync":
            eng.dma_start(self.w[:, :, :], chunked(self.w_table)[:, 0:KD, :]).then_inc(self.w_in, 16)
            eng.dma_start(self.b[:, :], one_row(self.b_table)).then_inc(self.w_in, 16)
        if which == "tensor":
            eng.wait_ge(self.w_in, 2 * 16)
        if which == "scalar":
            eng.sem_inc(self.cols_ready, J)
            eng.sem_inc(self.ready, J)

    def turn(self, eng, which, g):
        c = self.c
        if which == "tensor":
            for j in range(J):
                eng.wait_ge(self.staged, g * J + (j + 1))
                eng.wait_ge(self.cols_ready, g * J + (j + 1 + J - reuse(j, 2)))
                to_columns(eng, c.bank[2 + j % 2], self.rows[:, j % 2, :], c.ident[:, :]
                           ).then_inc(self.flipped, 1)
                eng.wait_ge(self.cols_ready, g * J + (j + 1 + J))
                eng.wait_ge(self.ready, g * J + (j + 1 + J - reuse(j, 2)))
                own_product(eng, c, c.bank[4 + j % 2][:, 0:D], [self.cols[:, j % 2, k, :] for k in range(KD)],
                            self.w, self.b).then_inc(self.product, 1)
        if which == "scalar":
            for j in range(J):
                eng.copy(self.rows[:, j % 2, :], self.layer.rows[:, g * J + j, :]).then_inc(self.staged, 1)
                eng.wait_ge(self.flipped, g * J + (j + 1))
                eng.copy(self.cols[:, j % 2, :, :], split_columns(c.bank[2 + j % 2])).then_inc(self.cols_ready, 1)
                eng.wait_ge(self.product, g * J + (j + 1))
                eng.copy(self.layer.own[:, g * J + j, :], c.bank[4 + j % 2][:, 0:D]).then_inc(self.ready, 1)


def own_product(pe, c, bank, cols, w, b):
    for k in range(KD):
        pe.matmul(bank, cols[k], w[:, k, :], start=(k == 0), stop=False)
    return pe.matmul(bank, c.ones[0:1, :], b[:, :], start=False, stop=True)


class GraphLayer:

    def __init__(self, c, sb):
        self.rows = sb("rows", [P, NT, D])
        self.own = sb("own", [P, NT, D])


def update(c, name, layer, w, ln=None, out_rows=None, last=None):
    own, sb = stage(c, name)
    with own:
        d = c.dram
        pooled = sb("pooled", [P, J, D])
        pooled_t = sb("pooled_cols", [P, J, KD, P])
        weight = sb("w", [P, KD, D])
        y = sb("y", [P, NT, D])
        pooled_in = c.sems(name, *(f"pooled_in{j}" for j in range(J)))
        w_in, flipped, cols_ready, product, added, scaled_ready, done, saved, y_go, act_go = c.sems(
            name, "w_in", "flipped", "cols_ready", "product", "added", "scaled_ready", "done", "saved", "y_go",
            "act_go")
        if ln:
            gain = sb("gain", [P, D])
            offset = sb("offset", [P, D])
            norm = Norm(c, sb, name)
            scaled = sb("scaled", [P, NT, D])
            residual, gained = c.sems(name, "residual", "gained")
        if last:
            X = last.experts
            z = sb("z", [P, J, D])
            z_t = sb("z_cols", [P, J, KD, P])
            gate = sb("gate", [P, KD, X])
            norm_x = Norm(c, sb, name + "x")
            z_ready, z_flipped, z_cols, gated, logits_ready = c.sems(
                name, "z_ready", "z_flipped", "z_cols", "gated", "logits_ready")
        n_in = 1 + (2 if ln else 0) + (1 if last else 0)
        block = own.enter_context(c.nc.Block())

        def group(g):
            return bass.ds(g * J, J)

        @block.gpsimd
        def _(pool):
            fetch_nodes(c, pool, pooled, flipped, pooled_in)

        @block.sync
        def _(sp):
            sp.dma_start(weight[:, :, :], chunked(w)[:, KD:, :]).then_inc(w_in, 16)
            if ln:
                sp.dma_start(gain[:, :], all_rows(ln[0])).then_inc(w_in, 16)
                sp.dma_start(offset[:, :], all_rows(ln[1])).then_inc(w_in, 16)
            if last:
                sp.dma_start(gate[:, :, :], chunked(d["router_w_t"])).then_inc(w_in, 16)
            with sp.Fori(0, G) as g:
                if last:
                    sp.wait_ge(z_ready, g * J + J)
                    sp.dma_start(group_rows(out_rows, g), z[:, :, :]).then_inc(saved, 16)
                else:
                    sp.wait_ge(done, g + 1 if ln else g * J + J)
                    sp.dma_start(group_rows(out_rows, g), layer.rows[:, group(g), :]).then_inc(saved, 16)
            sp.wait_ge(saved, 16 * G + (16 if last else 0))

        @block.tensor
        def _(pe):
            class Part(Parts):
                def ahead(self, g):
                    def flip(j):
                        pe.wait_ge(pooled_in[j], g * 16 + 16)
                        pe.wait_ge(cols_ready, g * J + (j + 1 + J - reuse(j, 2)))
                        to_columns(pe, c.bank[j % 2], pooled[:, j, :], c.ident[:, :]).then_inc(flipped, 1)

                    flip(0)
                    for j in range(J):
                        if j + 1 < J:
                            flip(j + 1)
                        pe.wait_ge(cols_ready, g * J + (j + 1 + J))
                        pe.wait_ge(added, g * J + (j + 1 + J - reuse(j, 3)))
                        for k in range(KD):
                            bank = c.bank[PRODUCT_BANKS[j % 3]][:, 0:D]
                            prod = pe.matmul(bank, pooled_t[:, j, k, :], weight[:, k, :],
                                             start=(k == 0), stop=(k == KD - 1))
                        prod.then_inc(product, 1)

                def behind(self, g):
                    if not last:
                        return

                    def flip(j):
                        pe.wait_ge(z_ready, g * J + (j + 1))
                        pe.wait_ge(z_cols, g * J + (j + 1 + J - reuse(j, 2)))
                        to_columns(pe, c.bank[4 + j % 2], z[:, j, :], c.ident[:, :]).then_inc(z_flipped, 1)

                    def score(j):
                        pe.wait_ge(z_cols, g * J + (j + 1 + J))
                        for k in range(KD):
                            prod = pe.matmul(c.bank[6][:, j * X:j * X + X], z_t[:, j, k, :], gate[:, k, :],
                                             start=(k == 0), stop=(k == KD - 1))
                        prod.then_inc(gated, 1)

                    pe.wait_ge(logits_ready, g + 1)
                    one_ahead(flip, score)

            pe.wait_ge(w_in, n_in * 16)
            overlapped(pe, Part())

        @block.scalar
        def _(act):
            class Part(Parts):
                def ahead(self, g):
                    for j in range(J):
                        act.wait_ge(flipped, g * J + (j + 1))
                        act.copy(pooled_t[:, j, :, :], split_columns(c.bank[j % 2])).then_inc(cols_ready, 1)

                def early(self, g):
                    if ln:
                        norm.scalar(act, g)

                def middle(self, g):
                    if ln:
                        act.wait_ge(norm.step, g * Norm.STEPS + Norm.STEPS)
                        act.sem_inc(act_go, 1)
                        for j in range(J):
                            norm.apply_act(act, scaled[:, g * J + j, :], y[:, g * J + j, :], g * J + j
                                           ).then_inc(scaled_ready, 1)
                    else:
                        for j in range(J):
                            act.wait_ge(added, g * J + (j + 1 + J))
                            act.sem_inc(act_go, 1)
                            act.activation(layer.rows[:, g * J + j, :], y[:, g * J + j, :], ACT.Relu
                                           ).then_inc(done, 1)

                def late(self, g):
                    if not last:
                        return
                    if isinstance(g, int) and g == 0:
                        norm_x.scalar(act, g)
                    act.wait_ge(norm_x.step, g * Norm.STEPS + Norm.STEPS)
                    act.wait_ge(saved, g * 16 + 16)
                    act.wait_ge(z_flipped, g * J + 1)
                    for j in range(J):
                        norm_x.apply_act(act, z[:, j, :], c.x[:, g * J + j, :], g * J + j).then_inc(z_ready, 1)

                def behind(self, g):
                    if not last:
                        return
                    for j in range(J):
                        act.wait_ge(z_flipped, g * J + (j + 2))
                        act.copy(z_t[:, j, :, :], split_columns(c.bank[4 + j % 2])).then_inc(z_cols, 1)
                        if j == J - 2 and not (isinstance(g, int) and g == G - 1):
                            norm_x.scalar(act, g + 1)
                    act.wait_ge(gated, g * J + J)
                    act.copy(last.logits[:, group(g), :], c.bank[6][:, 0:J * X].rearrange("p (j e) -> p j e", j=J)
                             ).then_inc(logits_ready, 1)

            act.sem_inc(cols_ready, J)
            if last:
                act.sem_inc(z_cols, J)
                act.sem_inc(z_flipped, 1)
                act.sem_inc(logits_ready, 1)
            overlapped(act, Part(), ahead_first=True)

        @block.vector
        def _(vec):
            class Part(Parts):
                def ahead(self, g):
                    for j in range(J):
                        vec.wait_ge(product, g * J + (j + 1))
                        vec.sem_inc(y_go, 1)
                        vec.tensor_tensor(y[:, g * J + j, :], c.bank[PRODUCT_BANKS[j % 3]][:, 0:D],
                                          layer.own[:, g * J + j, :], ALU.add).then_inc(added, 1)

                def early(self, g):
                    if ln:
                        vec.wait_ge(added, g * J + 2 * J)
                        vec.sem_inc(y_go, 1)
                        vec.scalar_tensor_tensor(out=y[:, group(g), :], in0=y[:, group(g), :], scalar=0.0,
                                                 in1=layer.rows[:, group(g), :], op0=ALU.max, op1=ALU.add
                                                 ).then_inc(residual, 1)
                        vec.wait_ge(residual, g + 1)
                        norm.vector(vec, g, lambda j: y[:, g * J + j, :])

                def late(self, g):
                    if not ln:
                        return
                    vec.wait_ge(scaled_ready, g * J + J)
                    step = Chain(vec, gained, g)
                    step(vec.tensor_tensor(scaled[:, group(g), :], scaled[:, group(g), :],
                                           gain[:, :].unsqueeze(1).to_broadcast([P, J, D]), ALU.mult))
                    if last:
                        vec.tensor_tensor(c.x[:, group(g), :], c.x[:, group(g), :], scaled[:, group(g), :], ALU.add
                                          ).then_inc(done, 1)
                        vec.wait_ge(done, g + 1)
                        norm_x.vector(vec, g, lambda j: c.x[:, g * J + j, :])
                    else:
                        vec.tensor_tensor(layer.rows[:, group(g), :], scaled[:, group(g), :],
                                          offset[:, :].unsqueeze(1).to_broadcast([P, J, D]), ALU.add
                                          ).then_inc(done, 1)

            vec.wait_ge(w_in, n_in * 16)
            vec.sem_inc(added, J)
            if last:
                vec.sem_inc(saved, 16)
            overlapped(vec, Part())


def finish_layer1(c, r, out):
    own, sb = stage(c, "finish1")
    with own:
        d = c.dram
        es = ExpertSum(c, r, sb, "sum1", d["z4"])
        saved, done = c.sems("finish1", "saved", "done")
        block = own.enter_context(c.nc.Block())

        @block.sync
        def _(sp):
            with sp.Fori(0, G) as g:
                es.sync(sp, g)
            with sp.Fori(0, G) as g:
                sp.wait_ge(done, g + 1)
                sp.dma_start(group_rows(out, g), es.total[:, bass.ds(g * J, J), :]).then_inc(saved, 16)
            sp.wait_ge(saved, 16 * G)

        @block.vector
        def _(vec):
            with vec.Fori(0, G) as g:
                es.vector(vec, g)
                part = bass.ds(g * J, J)
                vec.tensor_tensor(es.total[:, part, :], es.total[:, part, :], c.x[:, part, :], ALU.add
                                  ).then_inc(done, 1)


def program(nc, ins, out):
    with ExitStack() as ctx:
        def scratch(name, *shape):
            return nc.dram_tensor(name, shape, F32, kind="Internal").ap()

        d = dict(ins)
        for name in ("z0", "z2", "h", "a1", "a2", "z4"):
            d[name] = scratch(name, NP, D)
        for name in ("z0_cols", "z3_cols"):
            d[name] = scratch(name, P, KD, NP)
        d["state"] = scratch("state", EP + 1 + P, D)
        d["node_ends"] = scratch("node_ends", NP + 1)
        d["expert_out"] = scratch("expert_out", 2 * NP + max(places(16), places(8)) * P, D)
        c = Core(nc, ctx, d)

        setup(c)
        kv = KeyValue0(c)
        edge_walk(c, "walk0", d["z0"], "sum", (kv, Mlp0(c, kv)))
        own, sb = stage(c, "routes0")
        with own:
            r = Routes(c, sb, 16, places(16))
            convolve0(c, r.logits)
            route(c, r, "route0", False)
            experts(c, r, "experts0", d["z2"], d["L0_ffn_w1"], d["expert_b1_0"], d["L0_ffn_w2"], d["L0_ffn_b2"],
                    ACT.Relu)
            finish_layer0(c, r)

        own, sb = stage(c, "graph1")
        with own:
            r = Routes(c, sb, 8, places(8))
            with ExitStack() as inner:
                layer = GraphLayer(c, Local(c, inner, "graph1"))
                kv = KeyValue1(c)
                edge_walk(c, "walk1", d["h"], "max0", (kv, Mixed1(c, kv, layer)))
                update(c, "update1", layer, d["w_m1_t"], out_rows=d["a1"])
                edge_walk(c, "walk2", d["a1"], "max0", (Own(c, "own2", layer, d["w_m2_t"], d["L1_gnn_bm2"]),))
                update(c, "update2", layer, d["w_m2_t"], ln=(d["L1_gnn_ln2_g"], d["L1_gnn_ln2_b"]),
                       out_rows=d["a2"])
                edge_walk(c, "walk3", d["a2"], "max", (
                    Own(c, "own3", layer, d["w_m3_t"], d["L1_gnn_bm3"], offset=d["L1_gnn_ln3_b"]),))
                update(c, "update3", layer, d["w_m3_t"], ln=(d["L1_gnn_ln3_g"], d["L1_gnn_ln3_b"]),
                       out_rows=d["z4"], last=r)
            route(c, r, "route1", True)
            experts(c, r, "experts1", d["z4"], d["L1_ffn_w1"], d["expert_b1_1"], d["L1_ffn_w2"], d["L1_ffn_b2"],
                    ACT.Gelu)
            finish_layer1(c, r, out)



def kernel(**inputs):
    import numpy as np
    import concourse.bacc as bacc
    from concourse.bass_utils import run_bass_kernel_spmd as run

    def padded(a, size, fill, lead=0):
        out = np.full((size,) + a.shape[1:], fill, a.dtype)
        out[lead:lead + len(a)] = a
        return out

    a = {k: np.asarray(v) for k, v in inputs.items()}
    arrays = {k: v for k, v in a.items() if k.startswith(("L0_", "L1_"))}
    arrays["x"] = padded(a["x"], NP, 0)
    arrays["src"] = padded(a["src"], EP, 0)
    arrays["dst"] = padded(a["dst"], EP + 1, NP - 1, 1)
    arrays["dst"][0] = -1
    arrays["w_q_t"] = a["L0_mix_w_qkv"][:, :D].T
    arrays["w_p1_t"] = arrays.pop("L1_gnn_Wp1").T
    for n in (1, 2, 3):
        arrays[f"w_m{n}_t"] = arrays.pop(f"L1_gnn_Wm{n}").T
    arrays["router_w_t"] = arrays.pop("L1_ffn_router_w").T
    for n in (0, 1):
        b = arrays.pop(f"L{n}_ffn_b1")
        arrays[f"expert_b1_{n}"] = b.reshape(len(b), -1, P).transpose(0, 2, 1)
    arrays = {f"in_{k}": np.ascontiguousarray(v) for k, v in arrays.items()}

    nc = bacc.Bacc("TRN2", target_bir_lowering=False, num_devices=1)
    ins = {k[3:]: nc.dram_tensor(k, v.shape, mybir.dt.from_np(v.dtype), kind="ExternalInput").ap()
           for k, v in arrays.items()}
    out = nc.dram_tensor("out", (NP, D), F32, kind="ExternalOutput").ap()
    program(nc, ins, out)
    r = run(nc, [arrays], core_ids=[0])
    return r.results[0]["out"][:N]
```
